# Optimizing a Trainium2 kernel written in Bass

```python
import numpy as np
import jax
import jax.numpy as jnp

def _softmax(x, axis=-1):
    return jax.nn.softmax(x, axis=axis)

def _gelu(x):
    return jax.nn.gelu(x, approximate=True)

def _silu(x):
    return jax.nn.silu(x)

def _sigmoid(x):
    return jax.nn.sigmoid(x)

def _layernorm(x, axis=-1, eps=1e-05):
    m = jnp.mean(x, axis=axis, keepdims=True)
    v = jnp.var(x, axis=axis, keepdims=True)
    return (x - m) / jnp.sqrt(v + eps)

def _scatter_add(tgt, idx, src, axis=0):
    return tgt.at[idx].add(src)

def _segment_sum(src, seg, n):
    return jax.ops.segment_sum(src, seg, n)
kernel_name = 'mk_vit_tower_d2_tok_img768_r4_ce2e4a'

def setup_inputs(seed: int=0):
    np.random.seed(seed)
    _w = jnp.asarray

    def _rec_inputs():
        import jax
        import jax.numpy as jnp
        _rk = jax.random.key(seed)
        x = -0.000356955 + 1 * jax.random.normal(jax.random.fold_in(_rk, 1), (64, 3, 128, 128), jnp.float32)
        return x
    x = _rec_inputs()

    def _L0_tok_setup():
        import jax, jax.numpy as jnp
        import numpy as np
        NBITS = 8
        QN = -2 ** (NBITS - 1)
        QP = 2 ** (NBITS - 1) - 1
        PATCH = 16

        def _ste_round(v):
            return v + jax.lax.stop_gradient(jnp.round(v) - v)

        def lsq_quant(x, alpha, qn, qp):
            return _ste_round(jnp.clip(x / alpha, qn, qp)) * alpha
        key = jax.random.key(seed)
        k1, k2 = jax.random.split(key)
        x = jax.random.normal(k1, (128, 3, 224, 224), jnp.float32)
        W = jax.random.normal(k2, (192, 3, 16, 16), jnp.float32) * 0.02
        b = jnp.zeros((192,), jnp.float32)
        alpha_w = (2.0 * jnp.mean(jnp.abs(W)) / jnp.sqrt(jnp.float32(QP))).astype(jnp.float32)
        alpha_a = (2.0 * jnp.mean(jnp.abs(x)) / jnp.sqrt(jnp.float32(QP))).astype(jnp.float32)
        return {'x': x, 'W': W, 'b': b, 'alpha_w': alpha_w, 'alpha_a': alpha_a}
    _L0_tok_all = _L0_tok_setup()
    _L0_tok_in = {k: v for k, v in _L0_tok_all.items() if k in ('W', 'b', 'alpha_w', 'alpha_a')}
    del _L0_tok_all

    def _L0_attn_setup():
        import jax, jax.numpy as jnp
        import numpy as np
        EMBED_DIM = 192
        NUM_HEADS = 12
        PROJ_DIM = EMBED_DIM // NUM_HEADS
        M_FEATURES = 128
        EPS = 1e-06

        def _orthogonal_projection(key, m, d):
            nb_full_blocks = m // d
            keys = jax.random.split(key, nb_full_blocks + 2)
            blocks = []
            for i in range(nb_full_blocks):
                q, _ = jnp.linalg.qr(jax.random.normal(keys[i], (d, d)))
                blocks.append(q.T)
            rem = m - nb_full_blocks * d
            if rem > 0:
                q, _ = jnp.linalg.qr(jax.random.normal(keys[nb_full_blocks], (d, d)))
                blocks.append(q.T[:rem])
            final = jnp.vstack(blocks)
            multiplier = jnp.linalg.norm(jax.random.normal(keys[-1], (m, d)), axis=1)
            return multiplier[:, None] * final

        def _softmax_kernel(data, projection_matrix):
            data_normalizer = 1.0 / jnp.sqrt(jnp.sqrt(jnp.float32(PROJ_DIM)))
            data = data_normalizer * data
            ratio = 1.0 / jnp.sqrt(jnp.float32(projection_matrix.shape[0]))
            data_dash = jnp.einsum('blhd,md->blhm', data, projection_matrix)
            diag_data = jnp.sum(jnp.square(data), axis=-1, keepdims=True) / 2.0
            stab = jnp.max(data_dash, axis=-1, keepdims=True)
            return ratio * (jnp.exp(data_dash - diag_data - stab) + EPS)
        key = jax.random.key(seed)
        ks = jax.random.split(key, 8)
        B, L, E = (4, 1024, EMBED_DIM)
        s = 1.0 / np.sqrt(E)
        inp = {'x': jax.random.normal(ks[0], (B, L, E), jnp.float32), 'Wq': jax.random.normal(ks[1], (E, E), jnp.float32) * s, 'bq': jnp.zeros((E,), jnp.float32), 'Wk': jax.random.normal(ks[2], (E, E), jnp.float32) * s, 'bk': jnp.zeros((E,), jnp.float32), 'Wv': jax.random.normal(ks[3], (E, E), jnp.float32) * s, 'bv': jnp.zeros((E,), jnp.float32), 'Wo': jax.random.normal(ks[4], (E, E), jnp.float32) * s, 'bo': jnp.zeros((E,), jnp.float32), 'proj': _orthogonal_projection(ks[5], M_FEATURES, PROJ_DIM)}
        return inp
    _L0_attn_all = _L0_attn_setup()
    _L0_attn_in = {k: v for k, v in _L0_attn_all.items() if k in ('Wq', 'bq', 'Wk', 'bk', 'Wv', 'bv', 'Wo', 'bo', 'proj')}
    del _L0_attn_all

    def _L0_ffn_setup():
        import jax, jax.numpy as jnp
        import numpy as np
        EPS = 1e-05

        def _ln(x, g, b):
            m = jnp.mean(x, axis=-1, keepdims=True)
            v = jnp.mean((x - m) ** 2, axis=-1, keepdims=True)
            return (x - m) / jnp.sqrt(v + EPS) * g + b
        key = jax.random.key(seed)
        ks = jax.random.split(key, 16)
        B, S, D, H, E, K = (32, 128, 192, 12, 8, 2)
        Dff = 4 * D
        s = 0.02
        return {'x': jax.random.normal(ks[0], (B, S, D), dtype=jnp.float32), 'ln1_g': jnp.ones((D,), jnp.float32), 'ln1_b': jnp.zeros((D,), jnp.float32), 'in_proj_w': jax.random.normal(ks[1], (3 * D, D), jnp.float32) * s, 'in_proj_b': jnp.zeros((3 * D,), jnp.float32), 'out_proj_w': jax.random.normal(ks[2], (D, D), jnp.float32) * s, 'out_proj_b': jnp.zeros((D,), jnp.float32), 'ln2_g': jnp.ones((D,), jnp.float32), 'ln2_b': jnp.zeros((D,), jnp.float32), 'router_w': jax.random.normal(ks[3], (E, D), jnp.float32) * s, 'router_b': jnp.zeros((E,), jnp.float32), 'w1': jax.random.normal(ks[4], (E, D, Dff), jnp.float32) * s, 'b1': jnp.zeros((E, Dff), jnp.float32), 'w2': jax.random.normal(ks[5], (E, Dff, D), jnp.float32) * s, 'b2': jnp.zeros((E, D), jnp.float32)}
    _L0_ffn_all = _L0_ffn_setup()
    _L0_ffn_in = {k: v for k, v in _L0_ffn_all.items() if k in ('ln1_g', 'ln1_b', 'in_proj_w', 'in_proj_b', 'out_proj_w', 'out_proj_b', 'ln2_g', 'ln2_b', 'router_w', 'router_b', 'w1', 'b1', 'w2', 'b2')}
    del _L0_ffn_all

    def _L1_attn_setup():
        import jax, jax.numpy as jnp
        import numpy as np
        D_MODEL, D_INNER, D_STATE, D_CONV = (192, 384, 16, 4)
        BATCH, SEQ = (2, 512)

        def rmsnorm(x, w, eps=1e-05):
            norm = jax.lax.rsqrt(jnp.mean(x * x, axis=-1, keepdims=True) + eps)
            return x * norm * w

        def bitlinear(x, w):
            scale = jnp.maximum(jnp.mean(jnp.abs(w)), 1e-05)
            wn = w / scale
            wq = wn + jax.lax.stop_gradient(jnp.round(jnp.clip(wn, -1.0, 1.0)) - wn)
            return x @ wq.T * scale

        def mamba_forward(x, norm_weight, in_proj_weight, conv_weight, conv_bias, x_proj_weight, dt_proj_weight, dt_proj_bias, A_log, D, out_norm_weight, out_proj_weight):
            b, l, _ = x.shape
            residual = x
            xn = rmsnorm(x, norm_weight)
            xz = bitlinear(xn, in_proj_weight)
            x_path, z = jnp.split(xz, 2, axis=-1)
            xc = jnp.transpose(x_path, (0, 2, 1))
            xc = jax.lax.conv_general_dilated(xc, conv_weight, window_strides=(1,), padding=[(D_CONV - 1, 0)], feature_group_count=D_INNER, dimension_numbers=('NCH', 'OIH', 'NCH'))
            xc = xc + conv_bias[None, :, None]
            xc = jax.nn.silu(xc)
            x_path = jnp.transpose(xc, (0, 2, 1))
            x_dbc = x_path @ x_proj_weight.T
            dt = x_dbc[..., :1]
            B_mat = x_dbc[..., 1:1 + D_STATE]
            C_mat = x_dbc[..., 1 + D_STATE:]
            A = -jnp.exp(jnp.clip(A_log, -20.0, 2.0))
            delta = jax.nn.softplus(dt @ dt_proj_weight.T + dt_proj_bias)
            dA = jnp.exp(delta[..., None] * A)
            dBu = (delta * x_path)[..., None] * B_mat[:, :, None, :]

            def step(h, inp):
                dA_t, dBu_t, C_t = inp
                h = dA_t * h + dBu_t
                y_t = jnp.einsum('bdn,bn->bd', h, C_t)
                return (h, y_t)
            h0 = jnp.zeros((b, D_INNER, D_STATE), x.dtype)
            xs = (jnp.transpose(dA, (1, 0, 2, 3)), jnp.transpose(dBu, (1, 0, 2, 3)), jnp.transpose(C_mat, (1, 0, 2)))
            _, ys = jax.lax.scan(step, h0, xs)
            y = jnp.transpose(ys, (1, 0, 2)) + x_path * D
            y = y * jax.nn.silu(z)
            out = bitlinear(rmsnorm(y, out_norm_weight), out_proj_weight)
            return out + residual
        key = jax.random.key(seed)
        ks = jax.random.split(key, 8)
        x = jax.random.normal(ks[0], (BATCH, SEQ, D_MODEL), dtype=jnp.float32)
        norm_weight = jnp.ones((D_MODEL,), jnp.float32)
        in_proj_weight = jax.random.normal(ks[1], (2 * D_INNER, D_MODEL), jnp.float32) * 0.02
        conv_weight = jax.random.normal(ks[2], (D_INNER, 1, D_CONV), jnp.float32) * 0.3
        conv_bias = jnp.zeros((D_INNER,), jnp.float32)
        x_proj_weight = jax.random.normal(ks[3], (2 * D_STATE + 1, D_INNER), jnp.float32) * 0.02
        dt_proj_weight = jax.random.uniform(ks[4], (D_INNER, 1), jnp.float32, -0.1, 0.1)
        dt_proj_bias = jnp.full((D_INNER,), 0.5, jnp.float32)
        A_log = jnp.log(jnp.broadcast_to(jnp.arange(1, D_STATE + 1, dtype=jnp.float32), (D_INNER, D_STATE)))
        D = jnp.ones((D_INNER,), jnp.float32)
        out_norm_weight = jnp.ones((D_INNER,), jnp.float32)
        out_proj_weight = jax.random.normal(ks[5], (D_MODEL, D_INNER), jnp.float32) * 0.02
        return {'x': x, 'norm_weight': norm_weight, 'in_proj_weight': in_proj_weight, 'conv_weight': conv_weight, 'conv_bias': conv_bias, 'x_proj_weight': x_proj_weight, 'dt_proj_weight': dt_proj_weight, 'dt_proj_bias': dt_proj_bias, 'A_log': A_log, 'D': D, 'out_norm_weight': out_norm_weight, 'out_proj_weight': out_proj_weight}
    _L1_attn_all = _L1_attn_setup()
    _L1_attn_in = {k: v for k, v in _L1_attn_all.items() if k in ('norm_weight', 'in_proj_weight', 'conv_weight', 'conv_bias', 'x_proj_weight', 'dt_proj_weight', 'dt_proj_bias', 'A_log', 'D', 'out_norm_weight', 'out_proj_weight')}
    del _L1_attn_all

    def _L1_ffn_setup():
        import jax, jax.numpy as jnp
        import numpy as np
        B, L, D, H, F = (4, 512, 192, 12, 768)
        ROUTE_FRAC = 0.15
        LN_EPS = 1e-05

        def _ln(x, g, b):
            m = jnp.mean(x, axis=-1, keepdims=True)
            v = jnp.mean((x - m) ** 2, axis=-1, keepdims=True)
            return (x - m) * jax.lax.rsqrt(v + LN_EPS) * g + b
        key = jax.random.key(seed)
        ks = jax.random.split(key, 20)
        s = 0.02
        return {'hidden_states': jax.random.normal(ks[0], (B, L, D), dtype=jnp.float32), 'g1': jnp.ones((D,), jnp.float32), 'b1': jnp.zeros((D,), jnp.float32), 'g2': jnp.ones((D,), jnp.float32), 'b2': jnp.zeros((D,), jnp.float32), 'Wr': jax.random.normal(ks[1], (D,), jnp.float32) * s, 'br': jnp.zeros((), jnp.float32), 'Wq': jax.random.normal(ks[2], (D, D), jnp.float32) * s, 'bq': jnp.zeros((D,), jnp.float32), 'Wk': jax.random.normal(ks[3], (D, D), jnp.float32) * s, 'bk': jnp.zeros((D,), jnp.float32), 'Wv': jax.random.normal(ks[4], (D, D), jnp.float32) * s, 'bv': jnp.zeros((D,), jnp.float32), 'Wo': jax.random.normal(ks[5], (D, D), jnp.float32) * s, 'bo': jnp.zeros((D,), jnp.float32), 'Wm': jax.random.normal(ks[6], (D, D), jnp.float32) * s, 'bm': jnp.zeros((D,), jnp.float32), 'W1': jax.random.normal(ks[7], (D, F), jnp.float32) * s, 'bf1': jnp.zeros((F,), jnp.float32), 'W2': jax.random.normal(ks[8], (F, D), jnp.float32) * s, 'bf2': jnp.zeros((D,), jnp.float32)}
    _L1_ffn_all = _L1_ffn_setup()
    _L1_ffn_in = {k: v for k, v in _L1_ffn_all.items() if k in ('g1', 'b1', 'g2', 'b2', 'Wr', 'br', 'Wq', 'bq', 'Wk', 'bk', 'Wv', 'bv', 'Wo', 'bo', 'Wm', 'bm', 'W1', 'bf1', 'W2', 'bf2')}
    del _L1_ffn_all
    return {'x': x, 'L0_tok_W': _L0_tok_in['W'], 'L0_tok_b': _L0_tok_in['b'], 'L0_tok_alpha_w': _L0_tok_in['alpha_w'], 'L0_tok_alpha_a': _L0_tok_in['alpha_a'], 'L0_attn_Wq': _L0_attn_in['Wq'], 'L0_attn_bq': _L0_attn_in['bq'], 'L0_attn_Wk': _L0_attn_in['Wk'], 'L0_attn_bk': _L0_attn_in['bk'], 'L0_attn_Wv': _L0_attn_in['Wv'], 'L0_attn_bv': _L0_attn_in['bv'], 'L0_attn_Wo': _L0_attn_in['Wo'], 'L0_attn_bo': _L0_attn_in['bo'], 'L0_attn_proj': _L0_attn_in['proj'], 'L0_ffn_ln1_g': _L0_ffn_in['ln1_g'], 'L0_ffn_ln1_b': _L0_ffn_in['ln1_b'], 'L0_ffn_in_proj_w': _L0_ffn_in['in_proj_w'], 'L0_ffn_in_proj_b': _L0_ffn_in['in_proj_b'], 'L0_ffn_out_proj_w': _L0_ffn_in['out_proj_w'], 'L0_ffn_out_proj_b': _L0_ffn_in['out_proj_b'], 'L0_ffn_ln2_g': _L0_ffn_in['ln2_g'], 'L0_ffn_ln2_b': _L0_ffn_in['ln2_b'], 'L0_ffn_router_w': _L0_ffn_in['router_w'], 'L0_ffn_router_b': _L0_ffn_in['router_b'], 'L0_ffn_w1': _L0_ffn_in['w1'], 'L0_ffn_b1': _L0_ffn_in['b1'], 'L0_ffn_w2': _L0_ffn_in['w2'], 'L0_ffn_b2': _L0_ffn_in['b2'], 'L1_attn_norm_weight': _L1_attn_in['norm_weight'], 'L1_attn_in_proj_weight': _L1_attn_in['in_proj_weight'], 'L1_attn_conv_weight': _L1_attn_in['conv_weight'], 'L1_attn_conv_bias': _L1_attn_in['conv_bias'], 'L1_attn_x_proj_weight': _L1_attn_in['x_proj_weight'], 'L1_attn_dt_proj_weight': _L1_attn_in['dt_proj_weight'], 'L1_attn_dt_proj_bias': _L1_attn_in['dt_proj_bias'], 'L1_attn_A_log': _L1_attn_in['A_log'], 'L1_attn_D': _L1_attn_in['D'], 'L1_attn_out_norm_weight': _L1_attn_in['out_norm_weight'], 'L1_attn_out_proj_weight': _L1_attn_in['out_proj_weight'], 'L1_ffn_g1': _L1_ffn_in['g1'], 'L1_ffn_b1': _L1_ffn_in['b1'], 'L1_ffn_g2': _L1_ffn_in['g2'], 'L1_ffn_b2': _L1_ffn_in['b2'], 'L1_ffn_Wr': _L1_ffn_in['Wr'], 'L1_ffn_br': _L1_ffn_in['br'], 'L1_ffn_Wq': _L1_ffn_in['Wq'], 'L1_ffn_bq': _L1_ffn_in['bq'], 'L1_ffn_Wk': _L1_ffn_in['Wk'], 'L1_ffn_bk': _L1_ffn_in['bk'], 'L1_ffn_Wv': _L1_ffn_in['Wv'], 'L1_ffn_bv': _L1_ffn_in['bv'], 'L1_ffn_Wo': _L1_ffn_in['Wo'], 'L1_ffn_bo': _L1_ffn_in['bo'], 'L1_ffn_Wm': _L1_ffn_in['Wm'], 'L1_ffn_bm': _L1_ffn_in['bm'], 'L1_ffn_W1': _L1_ffn_in['W1'], 'L1_ffn_bf1': _L1_ffn_in['bf1'], 'L1_ffn_W2': _L1_ffn_in['W2'], 'L1_ffn_bf2': _L1_ffn_in['bf2']}

def reference(x, L0_tok_W, L0_tok_b, L0_tok_alpha_w, L0_tok_alpha_a, L0_attn_Wq, L0_attn_bq, L0_attn_Wk, L0_attn_bk, L0_attn_Wv, L0_attn_bv, L0_attn_Wo, L0_attn_bo, L0_attn_proj, L0_ffn_ln1_g, L0_ffn_ln1_b, L0_ffn_in_proj_w, L0_ffn_in_proj_b, L0_ffn_out_proj_w, L0_ffn_out_proj_b, L0_ffn_ln2_g, L0_ffn_ln2_b, L0_ffn_router_w, L0_ffn_router_b, L0_ffn_w1, L0_ffn_b1, L0_ffn_w2, L0_ffn_b2, L1_attn_norm_weight, L1_attn_in_proj_weight, L1_attn_conv_weight, L1_attn_conv_bias, L1_attn_x_proj_weight, L1_attn_dt_proj_weight, L1_attn_dt_proj_bias, L1_attn_A_log, L1_attn_D, L1_attn_out_norm_weight, L1_attn_out_proj_weight, L1_ffn_g1, L1_ffn_b1, L1_ffn_g2, L1_ffn_b2, L1_ffn_Wr, L1_ffn_br, L1_ffn_Wq, L1_ffn_bq, L1_ffn_Wk, L1_ffn_bk, L1_ffn_Wv, L1_ffn_bv, L1_ffn_Wo, L1_ffn_bo, L1_ffn_Wm, L1_ffn_bm, L1_ffn_W1, L1_ffn_bf1, L1_ffn_W2, L1_ffn_bf2):
    import jax
    import jax.numpy as jnp

    def _L0_tok_ref(x, W, b, alpha_w, alpha_a):
        import jax, jax.numpy as jnp
        import numpy as np
        NBITS = 8
        QN = -2 ** (NBITS - 1)
        QP = 2 ** (NBITS - 1) - 1
        PATCH = 16

        def _ste_round(v):
            return v + jax.lax.stop_gradient(jnp.round(v) - v)

        def lsq_quant(x, alpha, qn, qp):
            return _ste_round(jnp.clip(x / alpha, qn, qp)) * alpha
        xq = lsq_quant(x, alpha_a, QN, QP)
        wq = lsq_quant(W, alpha_w, QN, QP)
        y = jax.lax.conv_general_dilated(xq, wq, window_strides=(PATCH, PATCH), padding='VALID', dimension_numbers=('NCHW', 'OIHW', 'NCHW'))
        y = y + b[None, :, None, None]
        B, E, Hp, Wp = y.shape
        return jnp.transpose(y.reshape(B, E, Hp * Wp), (0, 2, 1))

    def _L0_attn_ref(x, Wq, bq, Wk, bk, Wv, bv, Wo, bo, proj):
        import jax, jax.numpy as jnp
        import numpy as np
        EMBED_DIM = 192
        NUM_HEADS = 12
        PROJ_DIM = EMBED_DIM // NUM_HEADS
        M_FEATURES = 128
        EPS = 1e-06

        def _orthogonal_projection(key, m, d):
            nb_full_blocks = m // d
            keys = jax.random.split(key, nb_full_blocks + 2)
            blocks = []
            for i in range(nb_full_blocks):
                q, _ = jnp.linalg.qr(jax.random.normal(keys[i], (d, d)))
                blocks.append(q.T)
            rem = m - nb_full_blocks * d
            if rem > 0:
                q, _ = jnp.linalg.qr(jax.random.normal(keys[nb_full_blocks], (d, d)))
                blocks.append(q.T[:rem])
            final = jnp.vstack(blocks)
            multiplier = jnp.linalg.norm(jax.random.normal(keys[-1], (m, d)), axis=1)
            return multiplier[:, None] * final

        def _softmax_kernel(data, projection_matrix):
            data_normalizer = 1.0 / jnp.sqrt(jnp.sqrt(jnp.float32(PROJ_DIM)))
            data = data_normalizer * data
            ratio = 1.0 / jnp.sqrt(jnp.float32(projection_matrix.shape[0]))
            data_dash = jnp.einsum('blhd,md->blhm', data, projection_matrix)
            diag_data = jnp.sum(jnp.square(data), axis=-1, keepdims=True) / 2.0
            stab = jnp.max(data_dash, axis=-1, keepdims=True)
            return ratio * (jnp.exp(data_dash - diag_data - stab) + EPS)
        B, L, E = x.shape
        H, D = (NUM_HEADS, PROJ_DIM)

        def split_heads(t):
            return t.reshape(B, L, H, D)
        q = split_heads(x @ Wq + bq)
        k = split_heads(x @ Wk + bk)
        v = split_heads(x @ Wv + bv)
        q_prime = _softmax_kernel(q, proj)
        k_prime = _softmax_kernel(k, proj)
        kvs = jnp.einsum('blhm,blhd->bhmd', k_prime, v)
        num = jnp.einsum('blhm,bhmd->blhd', q_prime, kvs)
        ks_sum = jnp.sum(k_prime, axis=1)
        den = jnp.einsum('blhm,bhm->blh', q_prime, ks_sum)
        attention = num / den[..., None]
        concat = jnp.transpose(attention, (0, 2, 1, 3)).reshape(B, -1, E)
        return concat @ Wo + bo

    def _L0_ffn_ref(x, ln1_g, ln1_b, in_proj_w, in_proj_b, out_proj_w, out_proj_b, ln2_g, ln2_b, router_w, router_b, w1, b1, w2, b2):
        import jax, jax.numpy as jnp
        import numpy as np
        EPS = 1e-05

        def _ln(x, g, b):
            m = jnp.mean(x, axis=-1, keepdims=True)
            v = jnp.mean((x - m) ** 2, axis=-1, keepdims=True)
            return (x - m) / jnp.sqrt(v + EPS) * g + b
        B, S, D = x.shape
        H = 12
        Dh = D // H
        E = router_w.shape[0]
        K = 2
        x2 = _ln(x, ln1_g, ln1_b)
        qkv = x2 @ in_proj_w.T + in_proj_b
        q, k, v = jnp.split(qkv, 3, axis=-1)
        q = q.reshape(B, S, H, Dh)
        k = k.reshape(B, S, H, Dh)
        v = v.reshape(B, S, H, Dh)
        scores = jnp.einsum('bqhd,bkhd->bhqk', q, k) / jnp.sqrt(jnp.float32(Dh))
        attn = jax.nn.softmax(scores, axis=-1)
        ao = jnp.einsum('bhqk,bkhd->bqhd', attn, v).reshape(B, S, D)
        ao = ao @ out_proj_w.T + out_proj_b
        x = x + ao
        xm = _ln(x, ln2_g, ln2_b).reshape(B * S, D)
        T = B * S
        logits = xm @ router_w.T + router_b
        probs = jax.nn.softmax(logits, axis=-1)
        topw, topi = jax.lax.top_k(probs, K)
        topw = topw / jnp.sum(topw, axis=-1, keepdims=True)
        combine = jnp.zeros((T, E), xm.dtype).at[jnp.arange(T)[:, None], topi].add(topw)
        out = jnp.zeros_like(xm)
        for e in range(E):
            h = jax.nn.gelu(xm @ w1[e] + b1[e], approximate=False)
            y = h @ w2[e] + b2[e]
            out = out + combine[:, e:e + 1] * y
        x = x + out.reshape(B, S, D)
        return x

    def _L1_attn_ref(x, norm_weight, in_proj_weight, conv_weight, conv_bias, x_proj_weight, dt_proj_weight, dt_proj_bias, A_log, D, out_norm_weight, out_proj_weight):
        import jax, jax.numpy as jnp
        import numpy as np
        D_MODEL, D_INNER, D_STATE, D_CONV = (192, 384, 16, 4)
        BATCH, SEQ = (2, 512)

        def rmsnorm(x, w, eps=1e-05):
            norm = jax.lax.rsqrt(jnp.mean(x * x, axis=-1, keepdims=True) + eps)
            return x * norm * w

        def bitlinear(x, w):
            scale = jnp.maximum(jnp.mean(jnp.abs(w)), 1e-05)
            wn = w / scale
            wq = wn + jax.lax.stop_gradient(jnp.round(jnp.clip(wn, -1.0, 1.0)) - wn)
            return x @ wq.T * scale

        def mamba_forward(x, norm_weight, in_proj_weight, conv_weight, conv_bias, x_proj_weight, dt_proj_weight, dt_proj_bias, A_log, D, out_norm_weight, out_proj_weight):
            b, l, _ = x.shape
            residual = x
            xn = rmsnorm(x, norm_weight)
            xz = bitlinear(xn, in_proj_weight)
            x_path, z = jnp.split(xz, 2, axis=-1)
            xc = jnp.transpose(x_path, (0, 2, 1))
            xc = jax.lax.conv_general_dilated(xc, conv_weight, window_strides=(1,), padding=[(D_CONV - 1, 0)], feature_group_count=D_INNER, dimension_numbers=('NCH', 'OIH', 'NCH'))
            xc = xc + conv_bias[None, :, None]
            xc = jax.nn.silu(xc)
            x_path = jnp.transpose(xc, (0, 2, 1))
            x_dbc = x_path @ x_proj_weight.T
            dt = x_dbc[..., :1]
            B_mat = x_dbc[..., 1:1 + D_STATE]
            C_mat = x_dbc[..., 1 + D_STATE:]
            A = -jnp.exp(jnp.clip(A_log, -20.0, 2.0))
            delta = jax.nn.softplus(dt @ dt_proj_weight.T + dt_proj_bias)
            dA = jnp.exp(delta[..., None] * A)
            dBu = (delta * x_path)[..., None] * B_mat[:, :, None, :]

            def step(h, inp):
                dA_t, dBu_t, C_t = inp
                h = dA_t * h + dBu_t
                y_t = jnp.einsum('bdn,bn->bd', h, C_t)
                return (h, y_t)
            h0 = jnp.zeros((b, D_INNER, D_STATE), x.dtype)
            xs = (jnp.transpose(dA, (1, 0, 2, 3)), jnp.transpose(dBu, (1, 0, 2, 3)), jnp.transpose(C_mat, (1, 0, 2)))
            _, ys = jax.lax.scan(step, h0, xs)
            y = jnp.transpose(ys, (1, 0, 2)) + x_path * D
            y = y * jax.nn.silu(z)
            out = bitlinear(rmsnorm(y, out_norm_weight), out_proj_weight)
            return out + residual
        return mamba_forward(x, norm_weight, in_proj_weight, conv_weight, conv_bias, x_proj_weight, dt_proj_weight, dt_proj_bias, A_log, D, out_norm_weight, out_proj_weight)

    def _L1_ffn_ref(hidden_states, g1, b1, g2, b2, Wr, br, Wq, bq, Wk, bk, Wv, bv, Wo, bo, Wm, bm, W1, bf1, W2, bf2):
        import jax, jax.numpy as jnp
        import numpy as np
        B, L, D, H, F = (4, 512, 192, 12, 768)
        ROUTE_FRAC = 0.15
        LN_EPS = 1e-05

        def _ln(x, g, b):
            m = jnp.mean(x, axis=-1, keepdims=True)
            v = jnp.mean((x - m) ** 2, axis=-1, keepdims=True)
            return (x - m) * jax.lax.rsqrt(v + LN_EPS) * g + b
        b, l, d = hidden_states.shape
        dh = d // H
        normed = _ln(hidden_states, g1, b1)
        scores = jax.nn.sigmoid(jnp.einsum('bld,d->bl', normed, Wr) + br)
        k = max(1, int(round(ROUTE_FRAC * l)))
        _, idx = jax.lax.top_k(-scores, k)
        attn_mask = jnp.zeros((b, l), bool).at[jnp.arange(b)[:, None], idx].set(True)
        q = (normed @ Wq + bq).reshape(b, l, H, dh)
        kk = (normed @ Wk + bk).reshape(b, l, H, dh)
        v = (normed @ Wv + bv).reshape(b, l, H, dh)
        logits = jnp.einsum('blhd,bmhd->bhlm', q, kk) / jnp.sqrt(jnp.float32(dh))
        probs = jax.nn.softmax(logits, axis=-1)
        ctx = jnp.einsum('bhlm,bmhd->blhd', probs, v).reshape(b, l, d)
        attn_out = ctx @ Wo + bo
        w = scores / (jnp.sum(scores, axis=1, keepdims=True) + 1e-06)
        pooled = jnp.einsum('bl,bld->bd', w, normed)
        mix_out = (normed + scores[..., None] * pooled[:, None, :]) @ Wm + bm
        merged = jnp.where(attn_mask[..., None], attn_out, mix_out)
        h = hidden_states + merged
        n2 = _ln(h, g2, b2)
        ffn = jax.nn.gelu(n2 @ W1 + bf1, approximate=False) @ W2 + bf2
        return h + ffn
    h = _L0_tok_ref(x, L0_tok_W, L0_tok_b, L0_tok_alpha_w, L0_tok_alpha_a)
    h = h + _L0_attn_ref(_layernorm(h, axis=-1), L0_attn_Wq, L0_attn_bq, L0_attn_Wk, L0_attn_bk, L0_attn_Wv, L0_attn_bv, L0_attn_Wo, L0_attn_bo, L0_attn_proj)
    h = h + _L0_ffn_ref(_layernorm(h, axis=-1), L0_ffn_ln1_g, L0_ffn_ln1_b, L0_ffn_in_proj_w, L0_ffn_in_proj_b, L0_ffn_out_proj_w, L0_ffn_out_proj_b, L0_ffn_ln2_g, L0_ffn_ln2_b, L0_ffn_router_w, L0_ffn_router_b, L0_ffn_w1, L0_ffn_b1, L0_ffn_w2, L0_ffn_b2)
    h = h + _L1_attn_ref(_layernorm(h, axis=-1), L1_attn_norm_weight, L1_attn_in_proj_weight, L1_attn_conv_weight, L1_attn_conv_bias, L1_attn_x_proj_weight, L1_attn_dt_proj_weight, L1_attn_dt_proj_bias, L1_attn_A_log, L1_attn_D, L1_attn_out_norm_weight, L1_attn_out_proj_weight)
    h = h + _L1_ffn_ref(_layernorm(h, axis=-1), L1_ffn_g1, L1_ffn_b1, L1_ffn_g2, L1_ffn_b2, L1_ffn_Wr, L1_ffn_br, L1_ffn_Wq, L1_ffn_bq, L1_ffn_Wk, L1_ffn_bk, L1_ffn_Wv, L1_ffn_bv, L1_ffn_Wo, L1_ffn_bo, L1_ffn_Wm, L1_ffn_bm, L1_ffn_W1, L1_ffn_bf1, L1_ffn_W2, L1_ffn_bf2)
    return h

_drawn_inputs = setup_inputs


def setup_inputs(seed=0):
    import zlib

    import numpy as np

    out = dict(_drawn_inputs(seed))
    spreads = {'L0_tok_b': (0.0, 0.1),
     'L0_attn_bq': (0.0, 0.1),
     'L0_attn_bk': (0.0, 0.1),
     'L0_attn_bv': (0.0, 0.1),
     'L0_attn_bo': (0.0, 0.1),
     'L0_ffn_ln1_g': (1.0, 0.6),
     'L0_ffn_ln1_b': (0.0, 0.8),
     'L0_ffn_in_proj_b': (0.0, 0.4),
     'L0_ffn_out_proj_b': (0.0, 0.1),
     'L0_ffn_ln2_g': (1.0, 0.6),
     'L0_ffn_ln2_b': (0.0, 0.548),
     'L0_ffn_router_b': (0.0, 0.1),
     'L0_ffn_b1': (0.0, 0.572),
     'L0_ffn_b2': (0.0, 0.1),
     'L1_attn_norm_weight': (1.0, 0.6),
     'L1_attn_conv_bias': (0.0, 0.1),
     'L1_attn_dt_proj_bias': (0.5, 0.6),
     'L1_attn_D': (1.0, 0.6),
     'L1_attn_out_norm_weight': (1.0, 0.6),
     'L1_ffn_g1': (1.0, 0.6),
     'L1_ffn_b1': (0.0, 0.728),
     'L1_ffn_g2': (1.0, 0.6),
     'L1_ffn_b2': (0.0, 2.0),
     'L1_ffn_bq': (0.0, 0.8),
     'L1_ffn_bk': (0.0, 2.0),
     'L1_ffn_bv': (0.0, 0.8),
     'L1_ffn_bo': (0.0, 0.8),
     'L1_ffn_bm': (0.0, 0.33),
     'L1_ffn_bf1': (0.0, 0.8),
     'L1_ffn_bf2': (0.0, 0.291)}
    factors = {'L0_ffn_in_proj_w': 3.435,
     'L1_attn_x_proj_weight': 8.0,
     'L1_attn_dt_proj_weight': 8.0,
     'L1_attn_A_log': 8.0,
     'L1_ffn_Wq': 8.0,
     'L1_ffn_Wk': 8.0,
     'L1_ffn_Wv': 8.0,
     'L1_ffn_Wo': 8.0}
    for name, (base, spread) in spreads.items():
        noise = np.random.default_rng([zlib.crc32(name.encode()), seed]).standard_normal(out[name].shape)
        drawn = base * np.exp(spread * noise) if base else spread * noise
        out[name] = jnp.asarray(drawn.astype(out[name].dtype))
    for name, factor in factors.items():
        out[name] = (out[name] * factor).astype(out[name].dtype)
    return out
```

```python
from contextlib import ExitStack

import concourse.bass as bass
from concourse import mybir

F32 = mybir.dt.float32
BF16 = mybir.dt.bfloat16
ALU = mybir.AluOpType
ACT = mybir.ActivationFunctionType
AX = mybir.AxisListType

P = 128
IMAGES = 64
SEQ = 64
TOKENS = IMAGES * SEQ
D = 192
DC = D // 2
HEADS = 12
DH = D // HEADS
TILES = TOKENS // P
TPG = 4
GROUPS = TILES // TPG
GT = TPG * P
PATCH_K = 3 * 16 * 16
PKC = PATCH_K // P
FEATURES = 128
EXPERTS = 8
FF = 768
FC = FF // P
INNER = 384
IC = INNER // P
STATES = 16
TAPS = 4
ROUND = 12582912.0
LN_EPS = 1e-5
FEATURE_EPS = 1e-6
POOL_EPS = 1e-6
ROUTED = max(1, int(round(0.15 * SEQ)))
LOG_EXP = "natural_log_exp_and_others"

W97 = [("pq", D), ("pk", D), ("pv", D), ("po", D), ("aq", D), ("ak", D), ("av", D), ("ao", D), ("router", EXPERTS),
       ("mq", D), ("mk", D), ("mv", D + 1), ("mo", D), ("mm", D), ("f1", FF), ("inproj", 2 * INNER)]
ROWS = [("tok_b", D), ("alpha_w", 1), ("alpha_a", 1)]
COLS = [("f2", FC * D), ("outproj", IC * D), ("xproj", IC * 33), ("headsum", 6), ("half", 2), ("tri", EXPERTS * EXPERTS), ("f1b", FC), ("conv", IC * TAPS), ("convb", IC),
        ("dtb", IC), ("alog", IC * STATES), ("dskip", IC), ("onorm", IC), 
        ("ln1g", 2), ("ln1b", 2), ("ln2g", 2), ("ln2b", 2), ("rmsw", 2), ("g1", 2), ("b1", 2), ("g2", 2), ("b2", 2)]


def offsets(parts):
    at, out = 0, {}
    for name, n in parts:
        out[name] = (at, n)
        at += n
    return out, at


W97_AT, W97_N = offsets(W97)
ROWS_AT, ROWS_N = offsets(ROWS)
COLS_AT, COLS_N = offsets(COLS)


ROWP_DT, ROWP_BF2, ROWP_BM, ROWP_N = 0, INNER, INNER + D, INNER + 2 * D


class Count:

    def __init__(self, sem, base=0):
        self.sem, self.base, self.n = sem, base, 0

    def inc(self, ins):
        self.n += 1
        return ins.then_inc(self.sem, 1)

    def link(self, eng, ins):
        self.inc(ins)
        eng.wait_ge(self.sem, self.base + self.n)


class Semaphores:

    def __init__(self, nc):
        self.nc, self.all = nc, []

    def __enter__(self):
        return self

    def new(self, name):
        self.all.append(self.nc.alloc_semaphore(name))
        return self.all[-1]

    def __exit__(self, *_):
        self.nc.clear_and_free_semaphores(self.all)
        self.nc.all_engine_barrier()


class Core:
    pass


def make_core(nc, ctx):
    c = Core()

    def sb(name, shape, dt=F32):
        return ctx.enter_context(nc.sbuf_tensor(name, shape, dt))

    c.h = sb("h", [P, TILES, D])
    c.x1 = sb("x1", [P, TILES, D])
    c.w = sb("w97", [DC + 1, 2, W97_N])
    c.cols = sb("cols", [P, COLS_N])
    c.rows = sb("rows", [P, ROWS_N])
    c.rowp = sb("rowp", [1, ROWP_N])
    c.ident = sb("ident", [P, P])
    c.same = sb("same", [P, P])
    c.lower = sb("lower", [P, P])
    c.ones = sb("ones", [P, P])
    c.st = sb("st", [P, TILES, 6])
    c.mv = sb("mv", [P, 2, TILES])
    c.rstd = sb("rstd", [P, 6, TILES])
    return c


def weight(c, name):
    at, n = W97_AT[name]
    return c.w[:, :, at:at + n]


def col(c, name):
    at, n = COLS_AT[name]
    return c.cols[:, at:at + n]


def tile_view(x, g, j):
    return x[:, bass.ds(g * TPG + j, 1), :].rearrange("p a d -> p (a d)")


def token_stats(nc, dve, c, link, x):
    with dve.Fori(0, TILES) as t:
        nc.vector.bn_stats(c.st[:, bass.ds(t, 1), :].rearrange("p a s -> p (a s)"),
                           x[:, bass.ds(t, 1), :].rearrange("p a d -> p (a d)"))
    link(dve, nc.vector.memset(c.rstd[:, 0, :], 0.0))
    mean, var, t = c.mv[:, 0, :], c.mv[:, 1, :], c.rstd[:, 0, :]
    even, odd, even2, odd2 = (c.st[:, :, i] for i in (1, 4, 2, 5))
    link(dve, nc.vector.tensor_tensor(mean, even, odd, ALU.add))
    link(dve, nc.vector.tensor_scalar(mean, mean, 0.5, None, ALU.mult))
    link(dve, nc.vector.tensor_tensor(var, even2, odd2, ALU.add))
    link(dve, nc.vector.tensor_scalar(var, var, 1.0 / D, None, ALU.mult))
    link(dve, nc.vector.tensor_tensor(t, even, odd, ALU.subtract))
    link(dve, nc.vector.scalar_tensor_tensor(out=t, in0=t, scalar=0.25, in1=t, op0=ALU.mult, op1=ALU.mult))
    link(dve, nc.vector.tensor_tensor(var, var, t, ALU.add))


def norm_factors_dve(nc, dve, c, link, s_var, s_guess, twice):
    mean, var = c.mv[:, 0, :], c.mv[:, 1, :]
    r, nm, r2, nm2, v, t = (c.rstd[:, i, :] for i in range(6))
    for turn in range(2 if twice else 1):
        if turn == 1:
            link(dve, nc.vector.tensor_tensor(t, r, r, ALU.mult))
            link(dve, nc.vector.tensor_tensor(t, t, var, ALU.mult))
        dve_in = var if turn == 0 else t
        out = r if turn == 0 else r2
        link(dve, nc.vector.tensor_scalar(v, dve_in, LN_EPS, None, ALU.add))
        nc.vector.tensor_copy(out, v).then_inc(s_var, 1)
        dve.wait_ge(s_guess, turn + 1)
        link(dve, nc.vector.tensor_tensor(t, out, out, ALU.mult))
        link(dve, nc.vector.tensor_tensor(t, t, v, ALU.mult))
        link(dve, nc.vector.tensor_scalar(t, t, -0.5, 1.5, ALU.mult, ALU.add))
        link(dve, nc.vector.tensor_tensor(out, out, t, ALU.mult))
    link(dve, nc.vector.scalar_tensor_tensor(out=nm, in0=mean, scalar=-1.0, in1=r, op0=ALU.mult, op1=ALU.mult))
    if twice:
        link(dve, nc.vector.tensor_tensor(r2, r2, r, ALU.mult))
        link(dve, nc.vector.scalar_tensor_tensor(out=nm2, in0=mean, scalar=-1.0, in1=r2, op0=ALU.mult, op1=ALU.mult))


def norm_factors_act(nc, act, c, s_var, s_log, s_guess, twice):
    for turn in range(2 if twice else 1):
        out = c.rstd[:, 2 * turn, :]
        act.wait_ge(s_var, turn + 1)
        nc.scalar.activation(out, out, ACT.Ln).then_inc(s_log, 1)
        act.wait_ge(s_log, turn + 1)
        nc.scalar.activation(out, out, ACT.Exp, scale=-0.5).then_inc(s_guess, 1)


def factor(c, i, g, j):
    return c.rstd[:, i, bass.ds(g * TPG + j, 1)]



def tokenize(nc, c, patches, w_tok, w97, rows, cols, rowp):
    with Semaphores(nc) as pool, ExitStack() as ctx:
        def sb(name, shape, dt=F32):
            return ctx.enter_context(nc.sbuf_tensor(name, shape, dt))

        def sem(name):
            return pool.new(name)

        NB = 2
        xin = sb("xin", [P, NB, PKC * GT])
        xr = sb("xr", [P, NB, PKC * GT])
        xq = sb("xq", [P, NB, PKC * GT], BF16)
        wt = sb("wt", [P, PKC * D])
        wq = sb("wq", [P, PKC * D], BF16)
        sc = sb("sc", [P, 4])
        acc = ctx.enter_context(nc.psum_tensor("acc", [P, TPG, 512], F32))
        s_small, s_wt, s_rest, s_bigcols = sem("s_small"), sem("s_wt"), sem("s_rest"), sem("s_bigcols")
        s_x = [sem(f"s_x{b}") for b in range(NB)]
        s_dve, s_scale, s_wq = sem("s_dve0"), sem("s_scale"), sem("s_wq")
        s_rounded, s_quant, s_acc, s_tok = sem("s_rounded"), sem("s_quant"), sem("s_acc"), sem("s_tok")
        s_const, s_masks = sem("s_const"), sem("s_masks")
        block = ctx.enter_context(nc.Block())

        @block.sync
        def _(sp):
            sp.dma_start(c.rows[:, :], rows[0:1, :].broadcast_to([P, ROWS_N])).then_inc(s_small, 16)
            sp.dma_start(wt[:, :], w_tok).then_inc(s_wt, 16)
            for b in range(NB):
                sp.dma_start(xin[:, b, :], patches[b]).then_inc(s_x[b], 16)
            with sp.Fori(0, GROUPS // NB - 1) as i:
                for b in range(NB):
                    sp.wait_ge(s_rounded, i * NB + b + 1)
                    sp.dma_start(xin[:, b, :], patches[i * NB + (b + NB)]).then_inc(s_x[b], 16)
            sp.dma_start(c.w[:, :, :], w97).then_inc(s_rest, 16)
            sp.dma_start(c.cols[:, :], cols).then_inc(s_rest, 16)
            sp.dma_start(c.rowp[:, :], rowp).then_inc(s_rest, 16)
            sp.wait_ge(s_rest, 48)

        @block.gpsimd
        def _(gp):
            nc.gpsimd.memset(c.ones[:, :], 1.0).then_inc(s_const, 1)
            for i in range(2):
                for k in range(2):
                    gp.wait_ge(s_const, i * 2 + k + 1)
                    nc.gpsimd.memset(c.same[i * SEQ:(i + 1) * SEQ, k * SEQ:(k + 1) * SEQ],
                                     float(i == k)).then_inc(s_const, 1)
            gp.wait_ge(s_const, 5)
            nc.gpsimd.affine_select(out=c.ident[:, :], in_=c.ones[:, :], compare_op=ALU.is_equal, fill=0.0,
                                    base=0, pattern=[[-1, P]], channel_multiplier=1).then_inc(s_masks, 1)
            nc.gpsimd.affine_select(out=c.lower[:, :], in_=c.same[:, :], compare_op=ALU.is_gt, fill=0.0,
                                    base=0, pattern=[[-1, P]], channel_multiplier=1).then_inc(s_masks, 1)
            gp.wait_ge(s_masks, 2)

        @block.scalar
        def _(act):
            nc.scalar.preload_act_table_set(LOG_EXP)
            act.wait_ge(s_scale, 1)
            with act.Fori(0, GROUPS // NB) as i:
                for b in range(NB):
                    act.wait_ge(s_x[b], i * 16 + 16)
                    act.wait_ge(s_quant, i * NB + b + 1)
                    nc.scalar.activation(xr[:, b, :], xin[:, b, :], ACT.Copy, bias=ROUND,
                                         scale=sc[:, 1:2]).then_inc(s_rounded, 1)

        @block.vector
        def _(dve):
            cnt = Count(s_dve)
            dve.wait_ge(s_small, 16)
            a = ROWS_AT["alpha_w"][0]
            nc.vector.reciprocal(sc[:, 0:2], c.rows[:, a:a + 2]).then_inc(s_scale, 1)
            cnt.link(dve, nc.vector.tensor_tensor(sc[:, 2:3], c.rows[:, a:a + 1], c.rows[:, a + 1:a + 2], ALU.mult))
            dve.wait_ge(s_scale, 1)
            dve.wait_ge(s_wt, 16)
            cnt.link(dve, nc.vector.tensor_scalar(wt[:, :], wt[:, :], sc[:, 0:1], ROUND, ALU.mult, ALU.add))
            cnt.link(dve, nc.vector.tensor_scalar(wt[:, :], wt[:, :], ROUND - 128, ROUND + 127, ALU.max, ALU.min))
            nc.vector.tensor_scalar(wq[:, :], wt[:, :], ROUND, None, ALU.subtract).then_inc(s_wq, 1)
            dve.sem_inc(s_quant, NB)
            with dve.Fori(0, GROUPS // NB) as i:
                for b in range(NB):
                    dve.wait_ge(s_rounded, i * NB + b + 1)
                    own = Count(s_dve, i * NB + b + 3)
                    own.link(dve, nc.vector.tensor_scalar(xr[:, b, :], xr[:, b, :], ROUND - 128, ROUND + 127,
                                                          ALU.max, ALU.min))
                    nc.vector.tensor_scalar(xq[:, b, :], xr[:, b, :], ROUND, None, ALU.subtract).then_inc(s_quant, 1)
                    for j in range(TPG):
                        dve.wait_ge(s_acc, (i * NB + b) * TPG + j + 1)
                        tile = c.h[:, bass.ds((i * NB + b) * TPG + j, 1), :].rearrange("p a d -> p (a d)")
                        nc.vector.scalar_tensor_tensor(out=tile, in0=acc[:, j, 0:D], scalar=sc[:, 2:3],
                                                       in1=c.rows[:, 0:D], op0=ALU.mult, op1=ALU.add).then_inc(s_tok, 1)

        @block.tensor
        def _(pe):
            pe.wait_ge(s_wq, 1)
            with pe.Fori(0, GROUPS // NB) as i:
                for b in range(NB):
                    pe.wait_ge(s_quant, (i * NB + b) + NB + 1)
                    for j in range(TPG):
                        if b == 1:
                            pe.wait_ge(s_tok, (i * NB) * TPG + j + 1)
                        for k in range(PKC):
                            mm = nc.tensor.matmul(acc[:, j, 0:D], xq[:, b, k * GT + j * P:k * GT + (j + 1) * P],
                                                  wq[:, k * D:(k + 1) * D], start=(k == 0), stop=(k == PKC - 1))
                        mm.then_inc(s_acc, 1)
                pe.wait_ge(s_tok, (i + 1) * (NB * TPG))



def performer(nc, c, proj, scratch):
    with Semaphores(nc) as pool, ExitStack() as ctx:
        def sb(name, shape, dt=F32):
            return ctx.enter_context(nc.sbuf_tensor(name, shape, dt))

        def sem(name):
            return pool.new(name)

        def ps(name, shape):
            return ctx.enter_context(nc.psum_tensor(name, shape, F32))

        N17 = DH + 1
        wproj = sb("wproj", [DC, 2 * FEATURES])
        projn = sb("projn", [DC, 2 * FEATURES])
        epsv = sb("epsv", [P, FEATURES])
        n = sb("n", [P, TPG, D])
        xT = sb("xT", [DC + 1, 2, GT])
        qkT = sb("qkT", [DC, 4, GT])
        sq = sb("sq", [DC, 4, GT])
        va = sb("va", [P, TPG, HEADS, N17])
        diag = sb("diag", [P, TPG, 2, HEADS])
        mx = sb("mx", [P, 2, HEADS])
        feat = sb("feat", [P, 2, 2, HEADS, FEATURES])
        qT = sb("qT", [P, HEADS, P])
        kvs = sb("kvs", [P, 2, HEADS, N17])
        den = sb("den", [P, HEADS])
        att = sb("att", [P, 2, HEADS, DH])
        ddk, ddq, fr = ps("ddk", [P, 3, 512]), ps("ddq", [P, 3, 512]), ps("fr", [P, 2, 512])
        dd = [ddq, ddk]
        num_ps = fr[:, 0, 208:208 + HEADS * N17].rearrange("p (h e) -> p h e", e=N17)
        diag_ps = fr[:, 0, 0:TPG * 2 * HEADS]
        s_ld, s_dve, s_var, s_log, s_guess = sem("s_ld"), sem("s_dve1"), sem("s_var"), sem("s_log"), sem("s_guess")
        s_n, s_T, s_xT, s_qk, s_qkT, s_sq = [sem(f"p_{x}") for x in ("n", "T", "xT", "qk", "qkT", "sq")]
        s_v, s_va, s_diag, s_diags = [sem(f"p_{x}") for x in ("v", "va", "diag", "diags")]
        s_dd = [sem("p_ddq"), sem("p_ddk")]
        s_sub = [sem("p_subq"), sem("p_subk")]
        s_exp = [sem("p_expq"), sem("p_expk")]
        s_kv, s_kvs, s_tr, s_qTa, s_qTd, s_num, s_att = [sem(f"p_{x}") for x in ("kv", "kvs", "tr", "qTa", "qTd", "num", "att")]
        s_out = [sem("p_out0"), sem("p_out1")]
        block = ctx.enter_context(nc.Block())

        @block.sync
        def _(sp):
            sp.dma_start(wproj[:, :], proj).then_inc(s_ld, 16)
            for b in range(2):
                sp.sem_inc(s_out[b], 32)
            with sp.Fori(0, GROUPS) as g:
                for j in range(TPG):
                    sp.wait_ge(s_att, g * TPG + j + 1)
                    for i in range(2):
                        img = (g * TPG + j) * 2 + i
                        sp.dma_start(scratch[bass.ds(img, 1)].rearrange("a h l d -> l (a h) d"),
                                     att[i * SEQ:(i + 1) * SEQ, j % 2]).then_inc(s_out[j % 2], 16)
            for b in range(2):
                sp.wait_ge(s_out[b], TILES // 2 * 32 + 32)

        @block.gpsimd
        def _(gp):
            pass

        @block.vector
        def _(dve):
            own = Count(s_dve)
            token_stats(nc, dve, c, own.link, c.h)
            norm_factors_dve(nc, dve, c, own.link, s_var, s_guess, twice=False)
            own.link(dve, nc.vector.memset(epsv[:, :], FEATURE_EPS))
            own.link(dve, nc.vector.memset(va[:, :, :, DH:N17], 1.0))
            own.link(dve, nc.vector.memset(xT[DC:DC + 1, 0, :], 1.0))
            dve.wait_ge(s_ld, 16)
            own.link(dve, nc.vector.tensor_scalar(projn[:, :], wproj[:, :], float(DH) ** -0.25, None, ALU.mult))
            done = own.n

            def features(g, own, j, kind):
                dve.wait_ge(s_dd[kind], g * TPG + j + 1)
                own.link(dve, nc.vector.tensor_reduce(mx[:, kind, :].rearrange("p (b s) -> p b s", b=3),
                                                      dd[kind][:, :, :].rearrange("p b (s m) -> p b s m", s=4), AX.X, ALU.max))
                own.link(dve, nc.vector.tensor_tensor(mx[:, kind, :], mx[:, kind, :], diag[:, j, kind, :], ALU.add))
                nc.vector.tensor_tensor(feat[:, j % 2, kind].rearrange("p (b s) m -> p b s m", b=3),
                                        dd[kind][:, :, :].rearrange("p b (s m) -> p b s m", s=4),
                                        mx[:, kind, :].rearrange("p (b s o) -> p b s o", b=3, o=1).broadcast_to([P, 3, 4, FEATURES]),
                                        ALU.subtract).then_inc(s_sub[kind], 1)

            def reads(g, own, j):
                dve.wait_ge(s_kv, g * TPG + j + 1)
                nc.vector.tensor_scalar(kvs[:, :, :, :].rearrange("p i h e -> p i (h e)"), fr[:, :, 0:HEADS * N17],
                                        1.0, None, ALU.mult).then_inc(s_kvs, 1)
                dve.wait_ge(s_tr, g * TPG + j + 1)
                nc.vector.tensor_scalar(qT[:, 8:12, :].rearrange("p h m -> p (h m)"), ddq[:, 2, :], FEATURE_EPS, None,
                                        ALU.add).then_inc(s_qTd, 1)

            def divide(g, own, j):
                dve.wait_ge(s_num, g * TPG + j + 1)
                own.link(dve, nc.vector.reciprocal(den[:, :], num_ps[:, :, DH]))
                if j >= 0:
                    dve.wait_ge(s_out[j % 2], 32 * (g * 2 + j // 2) + 32)
                nc.vector.tensor_tensor(att[:, j % 2], num_ps[:, :, 0:DH],
                                        den[:, :].rearrange("p (h o) -> p h o", o=1).broadcast_to([P, HEADS, DH]),
                                        ALU.mult).then_inc(s_att, 1)

            per_group = TPG * 5
            with dve.Fori(0, GROUPS) as g:
                own = Count(s_dve, g * per_group + done)
                for j in range(TPG):
                    nc.vector.tensor_scalar(n[:, j, :], tile_view(c.h, g, j), factor(c, 0, g, j), factor(c, 1, g, j),
                                            ALU.mult, ALU.add).then_inc(s_n, 1)
                dve.wait_ge(s_T, g * 2 + 2)
                nc.vector.tensor_scalar(xT[0:DC, 1, :], fr[0:DC, 1, :], 1.0, None, ALU.mult).then_inc(s_xT, 1)
                for i in range(4):
                    dve.wait_ge(s_qk, g * 4 + i + 1)
                    nc.vector.tensor_scalar(qkT[:, i, :], (ddk[0:DC, i, :] if i < 3 else ddq[0:DC, 0, :]), 1.0, None,
                                            ALU.mult).then_inc(s_qkT, 1)
                dve.wait_ge(s_diag, g + 1)
                nc.vector.tensor_scalar(diag[:, :, :, :].rearrange("p a b h -> p (a b h)"), diag_ps, 1.0, None,
                                        ALU.mult).then_inc(s_diags, 1)
                dve.wait_ge(s_diags, g + 1)
                for step in range(TPG + 1):
                    if step < TPG:
                        features(g, own, step, 1)
                    if step >= 1:
                        reads(g, own, step - 1)
                    if step < TPG:
                        features(g, own, step, 0)
                    if step >= 1:
                        divide(g, own, step - 1)
                assert own.n == per_group

        @block.scalar
        def _(act):
            nc.scalar.preload_act_table_set(LOG_EXP)
            norm_factors_act(nc, act, c, s_var, s_log, s_guess, twice=False)
            with act.Fori(0, GROUPS) as g:
                act.wait_ge(s_T, g * 2 + 1)
                nc.scalar.activation(xT[0:DC, 0, :], fr[0:DC, 0, :], ACT.Copy).then_inc(s_xT, 1)
                for i in range(4):
                    act.wait_ge(s_qkT, g * 4 + i + 1)
                    nc.scalar.activation(sq[:, i, :], qkT[:, i, :], ACT.Square).then_inc(s_sq, 1)
                for b in range(2):
                    act.wait_ge(s_v, g * 2 + b + 1)
                    nc.scalar.activation(va[:, 2 * b:2 * b + 2, :, 0:DH],
                                         ddq[:, 1 + b, 0:2 * D].rearrange("p (a h d) -> p a h d", a=2, d=DH),
                                         ACT.Copy).then_inc(s_va, 1)

                def turned(j):
                    act.wait_ge(s_tr, g * TPG + j + 1)
                    nc.scalar.activation(qT[:, 0:8, :].rearrange("p (b s) m -> p b (s m)", b=2), ddq[:, 0:2, :], ACT.Copy,
                                         bias=FEATURE_EPS).then_inc(s_qTa, 1)

                for step in range(TPG + 1):
                    if step < TPG:
                        for kind in (1, 0):
                            act.wait_ge(s_sub[kind], g * TPG + step + 1)
                            e = feat[:, step % 2, kind].rearrange("p h m -> p (h m)")
                            nc.scalar.activation(e, e, ACT.Exp).then_inc(s_exp[kind], 1)
                            if kind == 1 and step >= 1:
                                turned(step - 1)
                    else:
                        turned(step - 1)

        @block.tensor
        def _(pe):
            wq, wk, wv = weight(c, "pq"), weight(c, "pk"), weight(c, "pv")
            blk = col(c, "headsum")[0:DC, :]

            def products(g, j, kind):
                for b in range(3):
                    for cc in range(2):
                        mm = nc.tensor.matmul(dd[kind][:, b, cc * 256:cc * 256 + 256],
                                              qkT[32 * b:32 * b + 32, 2 * kind + cc, j * P:(j + 1) * P],
                                              projn[32 * b:32 * b + 32, :], start=True, stop=True)
                mm.then_inc(s_dd[kind], 1)

            with pe.Fori(0, GROUPS) as g:
                pe.wait_ge(s_n, g * TPG + TPG)
                for cc in range(2):
                    for j in range(TPG):
                        mm = nc.tensor.transpose(fr[0:DC, cc, j * P:(j + 1) * P], n[:, j, cc * DC:(cc + 1) * DC], c.ident[:, :])
                    mm.then_inc(s_T, 1)
                pe.wait_ge(s_xT, g * 2 + 2)
                for i in range(4):
                    w = (wq if i < 2 else wk)[:, :, (i % 2) * DC:(i % 2 + 1) * DC]
                    o = ddk[0:DC, i, :] if i < 3 else ddq[0:DC, 0, :]
                    nc.tensor.matmul(o, w[:, 0, :], xT[:, 0, :], start=True, stop=False)
                    nc.tensor.matmul(o, w[0:DC, 1, :], xT[0:DC, 1, :], start=False, stop=True).then_inc(s_qk, 1)
                for b in range(2):
                    for a in range(2):
                        j = 2 * b + a
                        o = ddq[:, 1 + b, a * D:(a + 1) * D]
                        nc.tensor.matmul(o, xT[:, 0, j * P:(j + 1) * P], wv[:, 0, :], start=True, stop=False)
                        mm = nc.tensor.matmul(o, xT[0:DC, 1, j * P:(j + 1) * P], wv[0:DC, 1, :], start=False, stop=True)
                    mm.then_inc(s_v, 1)
                pe.wait_ge(s_sq, g * 4 + 4)
                for j in range(TPG):
                    for kind in range(2):
                        for cc in range(2):
                            at = (j * 2 + kind) * HEADS
                            o = diag_ps[:, at:at + HEADS].rearrange("p (b c r) -> p b c r", b=3, c=2)[:, :, cc, :]
                            mm = nc.tensor.matmul(o, sq[:, 2 * kind + cc, j * P:(j + 1) * P], blk, start=True, stop=True)
                mm.then_inc(s_diag, 1)
                pe.wait_ge(s_qkT, g * 4 + 4)
                products(g, 0, 1)
                pe.wait_ge(s_va, g * 2 + 2)
                products(g, 0, 0)
                pe.wait_ge(s_diags, g + 1)
                for j in range(TPG):
                    if j + 1 < TPG:
                        pe.wait_ge(s_sub[1], g * TPG + j + 1)
                        products(g, j + 1, 1)
                    pe.wait_ge(s_exp[1], g * TPG + j + 1)
                    if j >= 1:
                        pe.wait_ge(s_att, g * TPG + j)
                    for i in range(2):
                        rows = slice(i * SEQ, (i + 1) * SEQ)
                        nc.tensor.matmul(fr[:, i, 0:HEADS * N17], epsv[rows, :],
                                         va[rows, j].rearrange("p h e -> p (h e)"), start=True, stop=False,
                                         skip_group_check=True)
                        for h in range(HEADS):
                            mm = nc.tensor.matmul(fr[:, i, h * N17:(h + 1) * N17], feat[rows, j % 2, 1, h, :],
                                                  va[rows, j, h, :], start=False, stop=(h == HEADS - 1),
                                                  skip_group_check=True)
                    mm.then_inc(s_kv, 1)
                    pe.wait_ge(s_exp[0], g * TPG + j + 1)
                    for h in range(HEADS):
                        mm = nc.tensor.transpose(ddq[:, h // 4, (h % 4) * P:(h % 4 + 1) * P], feat[:, j % 2, 0, h, :],
                                                 c.ident[:, :])
                    mm.then_inc(s_tr, 1)
                    pe.wait_ge(s_qTa, g * TPG + j + 1)
                    pe.wait_ge(s_qTd, g * TPG + j + 1)
                    if j + 1 < TPG:
                        products(g, j + 1, 0)
                    pe.wait_ge(s_kvs, g * TPG + j + 1)
                    for i in range(2):
                        for h in range(HEADS):
                            mm = nc.tensor.matmul(num_ps[i * SEQ:(i + 1) * SEQ, h, :], qT[:, h, i * SEQ:(i + 1) * SEQ],
                                                  kvs[:, i, h, :], start=True, stop=True)
                    mm.then_inc(s_num, 1)
                pe.wait_ge(s_att, g * TPG + TPG)


def performer_out(nc, c, scratch):
    with Semaphores(nc) as pool, ExitStack() as ctx:
        def sb(name, shape, dt=F32):
            return ctx.enter_context(nc.sbuf_tensor(name, shape, dt))

        def sem(name):
            return pool.new(name)

        NB = 2
        cat = sb("cat", [P, NB, TPG, D])
        xT = sb("cT", [DC + 1, 2, 2, GT])
        tp = ctx.enter_context(nc.psum_tensor("tp", [P, NB, 2, 512], F32))
        op = ctx.enter_context(nc.psum_tensor("op", [P, NB, 2, 512], F32))
        s_in = [sem("o_in0"), sem("o_in1")]
        s_dve, s_T, s_xT0, s_xT1, s_o, s_h, s_one = [sem(f"o_{x}") for x in ("dve", "T", "xT0", "xT1", "o", "h", "one")]
        block = ctx.enter_context(nc.Block())
        rows = scratch.rearrange("(t i) h l d -> t (i h l d)", i=2).rearrange("t (p e) -> p t e", e=D)

        @block.sync
        def _(sp):
            sp.sem_inc(s_T, NB * 2)
            with sp.Fori(0, GROUPS // NB) as i:
                for b in range(NB):
                    sp.wait_ge(s_T, (i * NB + b) * 2 + 2)
                    sp.dma_start(cat[:, b], rows[:, bass.ds((i * NB + b) * TPG, TPG), :]).then_inc(s_in[b], 16)

        @block.tensor
        def _(pe):
            wo = weight(c, "po")
            pe.wait_ge(s_one, 1)
            with pe.Fori(0, GROUPS // NB) as i:
                for b in range(NB):
                    g = i * NB + b
                    pe.wait_ge(s_in[b], i * 16 + 16)
                    for cc in range(2):
                        for j in range(TPG):
                            mm = nc.tensor.transpose(tp[0:DC, b, cc, j * P:(j + 1) * P], cat[:, b, j, cc * DC:(cc + 1) * DC],
                                                     c.ident[:, :])
                        mm.then_inc(s_T, 1)
                    pe.wait_ge(s_xT0, g + 1)
                    pe.wait_ge(s_xT1, g + 1)
                    pe.wait_ge(s_h, g * 2 + 2)
                    for j in range(TPG):
                        o = op[:, b, j // 2, (j % 2) * D:(j % 2 + 1) * D]
                        nc.tensor.matmul(o, xT[:, b, 0, j * P:(j + 1) * P], wo[:, 0, :], start=True, stop=False)
                        mm = nc.tensor.matmul(o, xT[0:DC, b, 1, j * P:(j + 1) * P], wo[0:DC, 1, :], start=False, stop=True)
                        if j % 2:
                            mm.then_inc(s_o, 1)

        @block.scalar
        def _(act):
            act.wait_ge(s_one, 1)
            with act.Fori(0, GROUPS // NB) as i:
                for b in range(NB):
                    act.wait_ge(s_T, (i * NB + b) * 2 + NB * 2 + 1)
                    nc.scalar.activation(xT[0:DC, b, 0, :], tp[0:DC, b, 0, :], ACT.Copy).then_inc(s_xT0, 1)

        @block.vector
        def _(dve):
            nc.vector.memset(xT[DC:DC + 1, :, 0, :], 1.0).then_inc(s_one, 1)
            dve.sem_inc(s_h, 2 * NB)
            with dve.Fori(0, GROUPS // NB) as i:
                for b in range(NB):
                    g = i * NB + b
                    dve.wait_ge(s_T, g * 2 + NB * 2 + 2)
                    nc.vector.tensor_scalar(xT[0:DC, b, 1, :], tp[0:DC, b, 1, :], 1.0, None, ALU.mult).then_inc(s_xT1, 1)
                    for j in range(TPG):
                        if j % 2 == 0:
                            dve.wait_ge(s_o, g * 2 + j // 2 + 1)
                        ins = nc.vector.tensor_tensor(tile_view(c.h, g, j), op[:, b, j // 2, (j % 2) * D:(j % 2 + 1) * D],
                                                      tile_view(c.h, g, j), ALU.add)
                        if j % 2:
                            ins.then_inc(s_h, 1)



def attention(nc, c, names, gain, shift, mixing):
    wq, wk, wv, wo = (weight(c, x) for x in names)
    wm = weight(c, "mm")
    VW = D + 1 if mixing else D
    tag = "m" if mixing else "a"
    with Semaphores(nc) as pool, ExitStack() as ctx:
        def sb(name, shape, dt=F32):
            return ctx.enter_context(nc.sbuf_tensor(tag + "_" + name, shape, dt))

        def sem(name):
            return pool.new(tag + "_" + name)

        def ps(name, shape):
            return ctx.enter_context(nc.psum_tensor(tag + "_" + name, shape, F32))

        N17 = DH + 1
        n = sb("n", [P, TPG, D])
        n1 = sb("n1", [P, TPG, D])
        xT = sb("xT", [DC + 1, 2, GT])
        qT = sb("qT", [DC, 2, GT])
        kT = sb("kT", [DC, 2, 2, GT])
        va = sb("va", [P, TPG, HEADS, N17])
        mx = sb("mx", [P, HEADS])
        sc = sb("sc", [P, 2, HEADS, SEQ])
        prob = sb("prob", [P, 2, HEADS, P])
        pT = sb("pT", [P, HEADS, P])
        den = sb("den", [P, HEADS])
        ao = sb("ao", [P, TPG, HEADS, DH])
        aT = sb("aT", [DC + 1, 2, GT])
        S, T, F = ps("S", [P, 3, 512]), ps("T", [P, 3, 512]), ps("F", [P, 2, 512])
        if mixing:
            es, score, share, ssum = (sb(x, [P, TPG]) for x in ("es", "score", "share", "ssum"))
            sel, nsel, rank = (sb(x, [P, TPG]) for x in ("sel", "nsel", "rank"))
            pm = sb("pm", [P, TPG, D])
            spread, sT, mixer, before = (sb(x, [P, TPG, P]) for x in ("spread", "sT", "mixer", "before"))
            mixed = sb("mixed", [P, TPG, D])
        s_dve, s_var, s_log, s_guess = [sem(x) for x in ("dve", "var", "log", "guess")]
        s_n, s_T, s_xT, s_q, s_qT, s_kTa, s_kTd, s_v, s_va = [sem(x) for x in ("n", "T", "xT", "q", "qT", "kTa", "kTd", "v", "va")]
        s_S, s_sub, s_exp, s_tr, s_pTa, s_pTd, s_o, s_ao = [sem(x) for x in ("S", "sub", "exp", "tr", "pTa", "pTd", "o", "ao")]
        s_at, s_aTa, s_aTd, s_out, s_h = [sem(x) for x in ("at", "aTa", "aTd", "out", "h")]
        s_pm, s_pms, s_es, s_score, s_tot, s_share, s_sT, s_mixer, s_mix = [
            sem(x) for x in ("pm", "pms", "es", "score", "tot", "share", "sT", "mixer", "mix")]
        block = ctx.enter_context(nc.Block())
        bank = [S[0:DC, 0, :], S[0:DC, 1, :], S[0:DC, 2, :], T[0:DC, 0, :]]

        def o_ps(j):
            return F[:, j % 2, 0:HEADS * N17].rearrange("p (h e) -> p h e", e=N17)

        @block.vector
        def _(dve):
            own = Count(s_dve)
            token_stats(nc, dve, c, own.link, c.h)
            norm_factors_dve(nc, dve, c, own.link, s_var, s_guess, twice=True)
            own.link(dve, nc.vector.memset(va[:, :, :, DH:N17], 1.0))
            own.link(dve, nc.vector.memset(xT[DC:DC + 1, 0, :], 1.0))
            own.link(dve, nc.vector.memset(aT[DC:DC + 1, 0, :], 1.0))
            own.link(dve, nc.vector.memset(prob[:, :, :, :], 0.0))
            done = own.n

            def scores(g, own, j):
                view = S[:, :, 0:4 * SEQ].rearrange("p b (s k) -> p b s k", s=4)
                dve.wait_ge(s_S, g * TPG + j + 1)
                own.link(dve, nc.vector.tensor_reduce(mx[:, :].rearrange("p (b s) -> p b s", b=3), view, AX.X, ALU.max))
                nc.vector.tensor_tensor(sc[:, j % 2].rearrange("p (b s) k -> p b s k", b=3), view,
                                        mx[:, :].rearrange("p (b s o) -> p b s o", b=3, o=1).broadcast_to([P, 3, 4, SEQ]),
                                        ALU.subtract).then_inc(s_sub, 1)

            def divide(g, own, j):
                dve.wait_ge(s_o, g * TPG + j + 1)
                own.link(dve, nc.vector.reciprocal(den[:, :], o_ps(j)[:, :, DH]))
                nc.vector.tensor_tensor(ao[:, j], o_ps(j)[:, :, 0:DH],
                                        den[:, :].rearrange("p (h o) -> p h o", o=1).broadcast_to([P, HEADS, DH]),
                                        ALU.mult).then_inc(s_ao, 1)

            def turned(g, own, j):
                dve.wait_ge(s_tr, g * TPG + j + 1)
                nc.vector.tensor_scalar(pT[:, 8:12, :].rearrange("p h m -> p (h m)"), T[:, 2, :], 1.0, None,
                                        ALU.mult).then_inc(s_pTd, 1)

            def routing(g, own):
                for b in range(2):
                    dve.wait_ge(s_pm, g * 2 + b + 1)
                    nc.vector.tensor_scalar(pm[:, 2 * b:2 * b + 2, :].rearrange("p a d -> p (a d)"), F[:, b, 0:2 * D], 1.0,
                                            None, ALU.mult).then_inc(s_pms, 1)
                dve.wait_ge(s_es, g * 2 + 2)
                own.link(dve, nc.vector.tensor_scalar(score[:, :], es[:, :], 1.0, None, ALU.add))
                own.link(dve, nc.vector.reciprocal(score[:, :], score[:, :]))
                for j in range(TPG):
                    own.link(dve, nc.vector.tensor_scalar(spread[:, j, :], c.ones[:, :], score[:, j:j + 1], None, ALU.mult))
                dve.sem_inc(s_score, 1)
                dve.wait_ge(s_tot, g + 1)
                own.link(dve, nc.vector.tensor_scalar(ssum[:, :], F[:, 0, 0:TPG], POOL_EPS, None, ALU.add))
                own.link(dve, nc.vector.reciprocal(ssum[:, :], ssum[:, :]))
                own.link(dve, nc.vector.tensor_tensor(share[:, :], score[:, :], ssum[:, :], ALU.mult))
                own.link(dve, nc.vector.tensor_scalar(sT[:, :, :].rearrange("p j k -> p (j k)"), F[:, 1, :], 1.0, None,
                                                      ALU.mult))
                dve.sem_inc(s_share, 1)
                for j in range(TPG):
                    one = score[:, j:j + 1]
                    own.link(dve, nc.vector.scalar_tensor_tensor(out=before[:, j, :], in0=sT[:, j, :], scalar=one,
                                                                 in1=c.same[:, :], op0=ALU.is_lt, op1=ALU.mult))
                    own.link(dve, nc.vector.scalar_tensor_tensor(out=spread[:, j, :], in0=sT[:, j, :], scalar=one,
                                                                 in1=c.lower[:, :], op0=ALU.is_equal, op1=ALU.mult))
                    own.link(dve, nc.vector.scalar_tensor_tensor(out=mixer[:, j, :], in0=sT[:, j, :], scalar=share[:, j:j + 1],
                                                                 in1=c.same[:, :], op0=ALU.mult, op1=ALU.mult))
                    own.link(dve, nc.vector.tensor_tensor(mixer[:, j, :], mixer[:, j, :], c.ident[:, :], ALU.add))
                own.link(dve, nc.vector.tensor_tensor(before[:, :, :], before[:, :, :], spread[:, :, :], ALU.add))
                own.link(dve, nc.vector.tensor_reduce(rank[:, :], before[:, :, :], AX.X, ALU.add))
                own.link(dve, nc.vector.tensor_scalar(sel[:, :], rank[:, :], ROUTED - 0.5, None, ALU.is_lt))
                own.link(dve, nc.vector.tensor_scalar(nsel[:, :], rank[:, :], ROUTED - 0.5, None, ALU.is_gt))
                dve.sem_inc(s_mixer, 1)

            per_group = TPG * 2 + TPG + (30 + 2 * TPG if mixing else 0)
            with dve.Fori(0, GROUPS) as g:
                own = Count(s_dve, g * per_group + done)
                for j in range(TPG):
                    nc.vector.tensor_scalar(n[:, j, :], tile_view(c.h, g, j), factor(c, 2, g, j), factor(c, 3, g, j),
                                            ALU.mult, ALU.add).then_inc(s_n, 1)
                for j in range(TPG):
                    own.link(dve, nc.vector.tensor_scalar(n1[:, j, :], tile_view(c.h, g, j), factor(c, 0, g, j),
                                                          factor(c, 1, g, j), ALU.mult, ALU.add))
                for j in range(TPG):
                    nc.vector.tensor_tensor(tile_view(c.h, g, j), n1[:, j, :], tile_view(c.h, g, j), ALU.add).then_inc(s_h, 1)
                dve.wait_ge(s_T, g * 2 + 2)
                nc.vector.tensor_scalar(xT[0:DC, 1, :], F[0:DC, 1, :], col(c, gain)[0:DC, 1:2], col(c, shift)[0:DC, 1:2],
                                        ALU.mult, ALU.add).then_inc(s_xT, 1)
                for i in range(2):
                    dve.wait_ge(s_q, g * 4 + i + 1)
                    nc.vector.tensor_scalar(qT[:, i, :], bank[i], 1.0, None, ALU.mult).then_inc(s_qT, 1)
                dve.wait_ge(s_q, g * 4 + 4)
                for r in range(2):
                    nc.vector.tensor_scalar(kT[:, 1, r, :], bank[3], col(c, "half")[0:DC, r:r + 1], None,
                                            ALU.mult).then_inc(s_kTd, 1)
                if mixing:
                    routing(g, own)
                for step in range(TPG + 2):
                    if step < TPG:
                        scores(g, own, step)
                    if step >= 2:
                        divide(g, own, step - 2)
                    if 1 <= step <= TPG:
                        turned(g, own, step - 1)
                dve.wait_ge(s_at, g * 2 + 2)
                nc.vector.tensor_scalar(aT[0:DC, 1, :], T[0:DC, 1, :], 1.0, None, ALU.mult).then_inc(s_aTd, 1)
                if mixing:
                    for j in range(TPG):
                        if j % 2 == 0:
                            dve.wait_ge(s_mix, g * 2 + j // 2 + 1)
                        own.link(dve, nc.vector.tensor_scalar(mixed[:, j, :], F[:, j // 2, (j % 2) * D:(j % 2 + 1) * D],
                                                              nsel[:, j:j + 1], None, ALU.mult))
                dve.wait_ge(s_h, g * (TPG * 3) + TPG)
                for j in range(TPG):
                    if j % 2 == 0:
                        dve.wait_ge(s_out, g * 2 + j // 2 + 1)
                    block_out = S[:, j // 2, (j % 2) * D:(j % 2 + 1) * D]
                    if mixing:
                        own.link(dve, nc.vector.scalar_tensor_tensor(out=mixed[:, j, :], in0=block_out, scalar=sel[:, j:j + 1],
                                                                     in1=mixed[:, j, :], op0=ALU.mult, op1=ALU.add))
                        block_out = mixed[:, j, :]
                    nc.vector.tensor_tensor(tile_view(c.x1, g, j), block_out, n1[:, j, :], ALU.add).then_inc(s_h, 1)
                    nc.vector.tensor_tensor(tile_view(c.h, g, j), block_out, tile_view(c.h, g, j), ALU.add).then_inc(s_h, 1)
                dve.wait_ge(s_h, (g + 1) * (TPG * 3))
                assert own.n == per_group, (own.n, per_group)

        @block.scalar
        def _(act):
            nc.scalar.preload_act_table_set(LOG_EXP)
            norm_factors_act(nc, act, c, s_var, s_log, s_guess, twice=True)
            with act.Fori(0, GROUPS) as g:
                act.wait_ge(s_T, g * 2 + 1)
                nc.scalar.activation(xT[0:DC, 0, :], F[0:DC, 0, :], ACT.Identity, scale=col(c, gain)[0:DC, 0:1],
                                     bias=col(c, shift)[0:DC, 0:1]).then_inc(s_xT, 1)
                act.wait_ge(s_q, g * 4 + 3)
                for r in range(2):
                    nc.scalar.activation(kT[:, 0, r, :], bank[2], ACT.Copy,
                                         scale=col(c, "half")[0:DC, r:r + 1]).then_inc(s_kTa, 1)
                for b in range(2):
                    act.wait_ge(s_v, g * 2 + b + 1)
                    src = T[:, 1 + b, 0:2 * VW].rearrange("p (a w) -> p a w", a=2)
                    if mixing:
                        nc.scalar.activation(es[:, 2 * b:2 * b + 2], src[:, :, D], ACT.Exp, scale=-1.0).then_inc(s_es, 1)
                    nc.scalar.activation(va[:, 2 * b:2 * b + 2, :, 0:DH],
                                         src[:, :, 0:D].rearrange("p a (h d) -> p a h d", d=DH), ACT.Copy).then_inc(s_va, 1)
                for step in range(TPG + 1):
                    if step < TPG:
                        act.wait_ge(s_sub, g * TPG + step + 1)
                        for i in range(2):
                            rows = slice(i * SEQ, (i + 1) * SEQ)
                            nc.scalar.activation(prob[rows, step % 2, :, rows], sc[rows, step % 2], ACT.Exp,
                                                 scale=float(DH) ** -0.5).then_inc(s_exp, 1)
                    if step >= 1:
                        act.wait_ge(s_tr, g * TPG + step)
                        nc.scalar.activation(pT[:, 0:8, :].rearrange("p (b s) m -> p b (s m)", b=2), T[:, 0:2, :],
                                             ACT.Copy).then_inc(s_pTa, 1)
                act.wait_ge(s_at, g * 2 + 1)
                nc.scalar.activation(aT[0:DC, 0, :], T[0:DC, 0, :], ACT.Copy).then_inc(s_aTa, 1)

        @block.tensor
        def _(pe):
            with pe.Fori(0, GROUPS) as g:
                pe.wait_ge(s_n, g * TPG + TPG)
                for cc in range(2):
                    for j in range(TPG):
                        mm = nc.tensor.transpose(F[0:DC, cc, j * P:(j + 1) * P], n[:, j, cc * DC:(cc + 1) * DC], c.ident[:, :])
                    mm.then_inc(s_T, 1)
                pe.wait_ge(s_xT, g * 2 + 2)
                for i in range(4):
                    w = (wq if i < 2 else wk)[:, :, (i % 2) * DC:(i % 2 + 1) * DC]
                    nc.tensor.matmul(bank[i], w[:, 0, :], xT[:, 0, :], start=True, stop=False)
                    nc.tensor.matmul(bank[i], w[0:DC, 1, :], xT[0:DC, 1, :], start=False, stop=True).then_inc(s_q, 1)
                for b in range(2):
                    for a in range(2):
                        j = 2 * b + a
                        o = T[:, 1 + b, a * VW:(a + 1) * VW]
                        nc.tensor.matmul(o, xT[:, 0, j * P:(j + 1) * P], wv[:, 0, :], start=True, stop=False)
                        mm = nc.tensor.matmul(o, xT[0:DC, 1, j * P:(j + 1) * P], wv[0:DC, 1, :], start=False, stop=True)
                    mm.then_inc(s_v, 1)
                if mixing:
                    for b in range(2):
                        for a in range(2):
                            j = 2 * b + a
                            o = F[:, b, a * D:(a + 1) * D]
                            nc.tensor.matmul(o, xT[0:DC, 0, j * P:(j + 1) * P], wm[0:DC, 0, :], start=True, stop=False)
                            mm = nc.tensor.matmul(o, xT[0:DC, 1, j * P:(j + 1) * P], wm[0:DC, 1, :], start=False, stop=True)
                        mm.then_inc(s_pm, 1)
                    pe.wait_ge(s_pms, g * 2 + 2)
                    pe.wait_ge(s_score, g + 1)
                    nc.tensor.matmul(F[:, 0, 0:TPG], c.same[:, :], score[:, :], start=True, stop=True)
                    for j in range(TPG):
                        mm = nc.tensor.transpose(F[:, 1, j * P:(j + 1) * P], spread[:, j, :], c.ident[:, :])
                    mm.then_inc(s_tot, 1)
                pe.wait_ge(s_qT, g * 2 + 2)
                pe.wait_ge(s_kTa, g * 2 + 2)
                pe.wait_ge(s_kTd, g * 2 + 2)
                for step in range(TPG + 2):
                    if step < TPG:
                        if step >= 1:
                            pe.wait_ge(s_sub, g * TPG + step)
                        for b in range(3):
                            rows = slice(32 * b, 32 * b + 32)
                            for cc in range(2):
                                for i in range(2):
                                    at = step * P + i * SEQ
                                    mm = nc.tensor.matmul(
                                        S[i * SEQ:(i + 1) * SEQ, b, cc * 2 * SEQ:(cc + 1) * 2 * SEQ].rearrange(
                                            "p (r k) -> p r k", r=2),
                                        qT[rows, cc, at:at + SEQ], kT[rows, cc, :, at:at + SEQ], start=True, stop=True)
                        mm.then_inc(s_S, 1)
                    if step >= 2:
                        j = step - 2
                        pe.wait_ge(s_pTa, g * TPG + j + 1)
                        pe.wait_ge(s_pTd, g * TPG + j + 1)
                        if j >= 2:
                            pe.wait_ge(s_ao, g * TPG + j - 1)
                        elif mixing:
                            pe.wait_ge(s_share, g + 1)
                        for h in range(HEADS):
                            mm = nc.tensor.matmul(o_ps(j)[:, h, :], pT[:, h, :], va[:, j, h, :], start=True, stop=True)
                        mm.then_inc(s_o, 1)
                    if 1 <= step <= TPG:
                        j = step - 1
                        if j == 0:
                            pe.wait_ge(s_va, g * 2 + 2)
                        pe.wait_ge(s_exp, (g * TPG + j) * 2 + 2)
                        for h in range(HEADS):
                            mm = nc.tensor.transpose(T[:, h // 4, (h % 4) * P:(h % 4 + 1) * P], prob[:, j % 2, h, :],
                                                     c.ident[:, :])
                        mm.then_inc(s_tr, 1)
                pe.wait_ge(s_ao, g * TPG + TPG)
                for cc in range(2):
                    for j in range(TPG):
                        mm = nc.tensor.transpose(T[0:DC, cc, j * P:(j + 1) * P],
                                                 ao[:, j].rearrange("p h d -> p (h d)")[:, cc * DC:(cc + 1) * DC], c.ident[:, :])
                    mm.then_inc(s_at, 1)
                if mixing:
                    pe.wait_ge(s_mixer, g + 1)
                    for j in range(TPG):
                        o = F[:, j // 2, (j % 2) * D:(j % 2 + 1) * D]
                        nc.tensor.matmul(o, mixer[:, j, :], pm[:, j, :], start=True, stop=False)
                        mm = nc.tensor.matmul(o, c.ones[0:1, :], c.rowp[0:1, ROWP_BM:ROWP_BM + D], start=False, stop=True)
                        if j % 2:
                            mm.then_inc(s_mix, 1)
                pe.wait_ge(s_aTa, g + 1)
                pe.wait_ge(s_aTd, g + 1)
                for j in range(TPG):
                    o = S[:, j // 2, (j % 2) * D:(j % 2 + 1) * D]
                    nc.tensor.matmul(o, aT[:, 0, j * P:(j + 1) * P], wo[:, 0, :], start=True, stop=False)
                    mm = nc.tensor.matmul(o, aT[0:DC, 1, j * P:(j + 1) * P], wo[0:DC, 1, :], start=False, stop=True)
                    if j % 2:
                        mm.then_inc(s_out, 1)
                pe.wait_ge(s_h, (g + 1) * (TPG * 3))



def experts(nc, c, e1, e2, eb1, eb2):
    with Semaphores(nc) as pool, ExitStack() as ctx:
        def sb(name, shape, dt=F32):
            return ctx.enter_context(nc.sbuf_tensor("e_" + name, shape, dt))

        def sem(name):
            return pool.new("e_" + name)

        def ps(name, shape):
            return ctx.enter_context(nc.psum_tensor("e_" + name, shape, F32))

        n = sb("n", [P, TPG, D])
        xT = sb("xT", [DC + 1, 2, GT])
        xall = sb("xall", [DC, 2, TOKENS])
        logit = sb("logit", [P, TILES, EXPERTS])
        ex = sb("ex", [P, TILES, EXPERTS])
        top = sb("top", [P, TILES])
        cmp1 = sb("cmp1", [P, TILES, EXPERTS * EXPERTS])
        cmp2 = sb("cmp2", [P, TILES, EXPERTS * EXPERTS])
        comb = sb("comb", [P, TILES, EXPERTS])
        cg = sb("cg", [P, TPG * EXPERTS])
        cT = sb("cT", [EXPERTS, GT])
        b2 = sb("b2", [EXPERTS, D])
        w1 = sb("w1", [DC, 2, 2, FF])
        w2 = sb("w2", [P, 2, FC, D])
        b1 = sb("b1", [P, 2, FC])
        hT = sb("hT", [P, FC, GT])
        H, O = ps("H", [P, FC, 512]), ps("O", [P, 2, 512])
        s_w = [sem("w0"), sem("w1")]
        s_dve, s_var, s_log, s_guess, s_b2 = [sem(x) for x in ("dve", "var", "log", "guess", "b2")]
        s_n, s_T, s_xT, s_lg, s_x, s_z, s_ex, s_comb = [sem(x) for x in ("n", "T", "xT", "lg", "x", "z", "ex", "comb")]
        s_cg, s_ct, s_cTs, s_bo, s_bh = [sem(x) for x in ("cg", "ct", "cTs", "bo", "bh")]
        s_up, s_gelu, s_down, s_o, s_y = [sem(x) for x in ("up", "gelu", "down", "o", "y")]
        block = ctx.enter_context(nc.Block())

        @block.sync
        def _(sp):
            sp.dma_start(b2[:, :], eb2).then_inc(s_b2, 16)
            sp.sem_inc(s_down, GROUPS * FC * 2)
            with sp.Fori(0, EXPERTS // 2) as ep:
                for b in range(2):
                    e = ep * 2 + b
                    sp.wait_ge(s_down, e * (GROUPS * FC) + GROUPS * FC)
                    sp.dma_start(w1[:, b], e1[bass.ds(e, 1)].rearrange("a p c f -> p (a c) f")).then_inc(s_w[b], 16)
                    sp.dma_start(w2[:, b], e2[bass.ds(e, 1)].rearrange("a p c f -> p (a c) f")).then_inc(s_w[b], 16)
                    sp.dma_start(b1[:, b], eb1[bass.ds(e, 1)].rearrange("a p f -> p (a f)")).then_inc(s_w[b], 16)
            for b in range(2):
                sp.wait_ge(s_w[b], EXPERTS // 2 * 48)

        @block.vector
        def _(dve):
            own = Count(s_dve)
            token_stats(nc, dve, c, own.link, c.x1)
            norm_factors_dve(nc, dve, c, own.link, s_var, s_guess, twice=False)
            own.link(dve, nc.vector.memset(xT[DC:DC + 1, 0, :], 1.0))
            with dve.Fori(0, GROUPS) as g:
                for j in range(TPG):
                    nc.vector.tensor_scalar(n[:, j, :], tile_view(c.x1, g, j), factor(c, 0, g, j), factor(c, 1, g, j),
                                            ALU.mult, ALU.add).then_inc(s_n, 1)
                for cc in range(2):
                    dve.wait_ge(s_T, g * 2 + cc + 1)
                    nc.vector.tensor_scalar(xT[0:DC, cc, :], O[0:DC, cc, :], col(c, "ln2g")[0:DC, cc:cc + 1],
                                            col(c, "ln2b")[0:DC, cc:cc + 1], ALU.mult, ALU.add).then_inc(s_xT, 1)
                dve.wait_ge(s_xT, g * 2 + 2)
                nc.vector.tensor_scalar(xall[:, :, bass.ds(g * GT, GT)], xT[0:DC, :, :], 1.0, None, ALU.mult).then_inc(s_x, 1)
                dve.wait_ge(s_lg, g + 1)
                nc.vector.tensor_scalar(logit[:, bass.ds(g * TPG, TPG), :].rearrange("p a e -> p (a e)"),
                                        H[:, 0, 0:TPG * EXPERTS], 1.0, None, ALU.mult).then_inc(s_x, 1)
                dve.wait_ge(s_x, g * 2 + 2)

            own.link(dve, nc.vector.tensor_reduce(top[:, :], logit[:, :, :], AX.X, ALU.max))
            nc.vector.tensor_tensor(ex[:, :, :], logit[:, :, :],
                                    top[:, :].rearrange("p (t o) -> p t o", o=1).broadcast_to([P, TILES, EXPERTS]),
                                    ALU.subtract).then_inc(s_z, 1)
            shape = [P, TILES, EXPERTS, EXPERTS]
            other = logit[:, :, :].rearrange("p t (o f) -> p t o f", o=1).broadcast_to(shape)
            this = logit[:, :, :].rearrange("p t (e o) -> p t e o", o=1).broadcast_to(shape)
            c1, c2 = (x[:, :, :].rearrange("p t (e f) -> p t e f", e=EXPERTS) for x in (cmp1, cmp2))
            own.link(dve, nc.vector.tensor_tensor(c1, other, this, ALU.is_gt))
            own.link(dve, nc.vector.tensor_tensor(c2, other, this, ALU.is_equal))
            tri = col(c, "tri").rearrange("p (o k) -> p o k", o=1).broadcast_to([P, TILES, EXPERTS * EXPERTS])
            own.link(dve, nc.vector.tensor_tensor(cmp2[:, :, :], cmp2[:, :, :], tri, ALU.mult))
            own.link(dve, nc.vector.tensor_tensor(cmp1[:, :, :], cmp1[:, :, :], cmp2[:, :, :], ALU.add))
            own.link(dve, nc.vector.tensor_reduce(comb[:, :, :], c1, AX.X, ALU.add))
            dve.wait_ge(s_ex, 1)
            own.link(dve, nc.vector.scalar_tensor_tensor(out=comb[:, :, :], in0=comb[:, :, :], scalar=1.5, in1=ex[:, :, :],
                                                         op0=ALU.is_lt, op1=ALU.mult))
            own.link(dve, nc.vector.tensor_reduce(top[:, :], comb[:, :, :], AX.X, ALU.add))
            own.link(dve, nc.vector.reciprocal(top[:, :], top[:, :]))
            own.link(dve, nc.vector.tensor_tensor(comb[:, :, :], comb[:, :, :],
                                                  top[:, :].rearrange("p (t o) -> p t o", o=1).broadcast_to([P, TILES, EXPERTS]),
                                                  ALU.mult))
            with dve.Fori(0, GROUPS) as g:
                nc.vector.tensor_scalar(cg[:, :], comb[:, bass.ds(g * TPG, TPG), :].rearrange("p a e -> p (a e)"), 1.0, None,
                                        ALU.mult).then_inc(s_cg, 1)
                dve.wait_ge(s_ct, g + 1)
                nc.vector.tensor_scalar(cT[:, :], H[0:EXPERTS, 0, :], 1.0, None, ALU.mult).then_inc(s_cTs, 1)
                for j in range(TPG):
                    if j % 2 == 0:
                        dve.wait_ge(s_bo, g * 2 + j // 2 + 1)
                    nc.vector.tensor_tensor(tile_view(c.h, g, j), O[:, j // 2, (j % 2) * D:(j % 2 + 1) * D],
                                            tile_view(c.h, g, j), ALU.add).then_inc(s_bh, 1)
            dve.wait_ge(s_bh, TILES)
            dve.sem_inc(s_y, TPG)
            with dve.Fori(0, EXPERTS) as e:
                with dve.Fori(0, GROUPS) as g:
                    it = e * GROUPS + g
                    for j in range(TPG):
                        if j == 0:
                            dve.wait_ge(s_o, it + 1)
                        if j == 2:
                            dve.wait_ge(s_down, (it + 1) * FC + GROUPS * FC * 2)
                        nc.vector.scalar_tensor_tensor(
                            out=tile_view(c.h, g, j), in0=O[:, j // 2, (j % 2) * D:(j % 2 + 1) * D],
                            scalar=comb[:, bass.ds(g * TPG + j, 1), bass.ds(e, 1)].rearrange("p a o -> p (a o)"),
                            in1=tile_view(c.h, g, j), op0=ALU.mult, op1=ALU.add).then_inc(s_y, 1)
                    dve.wait_ge(s_y, it * TPG + TPG * 2)

        @block.scalar
        def _(act):
            nc.scalar.preload_act_table_set(LOG_EXP)
            norm_factors_act(nc, act, c, s_var, s_log, s_guess, twice=False)
            act.wait_ge(s_z, 1)
            nc.scalar.activation(ex[:, :, :], ex[:, :, :], ACT.Exp).then_inc(s_ex, 1)
            nc.scalar.preload_act_table(ACT.Gelu)
            with act.Fori(0, EXPERTS // 2) as ep:
                for b in range(2):
                    act.wait_ge(s_w[b], ep * 48 + 48)
                    with act.Fori(0, GROUPS) as g:
                        it = (ep * 2 + b) * GROUPS + g
                        for f in range(FC):
                            act.wait_ge(s_up, it * FC + f + 1)
                            act.wait_ge(s_down, it * FC + f + 1 + (GROUPS * 2 - 1) * FC)
                            nc.scalar.activation(hT[:, f, :], H[:, f, :], ACT.Gelu, bias=b1[:, b, f:f + 1]).then_inc(s_gelu, 1)

        @block.tensor
        def _(pe):
            router = weight(c, "router")
            with pe.Fori(0, GROUPS) as g:
                pe.wait_ge(s_n, g * TPG + TPG)
                for cc in range(2):
                    for j in range(TPG):
                        mm = nc.tensor.transpose(O[0:DC, cc, j * P:(j + 1) * P], n[:, j, cc * DC:(cc + 1) * DC], c.ident[:, :])
                    mm.then_inc(s_T, 1)
                pe.wait_ge(s_xT, g * 2 + 2)
                for j in range(TPG):
                    o = H[:, 0, j * EXPERTS:(j + 1) * EXPERTS]
                    nc.tensor.matmul(o, xT[:, 0, j * P:(j + 1) * P], router[:, 0, :], start=True, stop=False)
                    mm = nc.tensor.matmul(o, xT[0:DC, 1, j * P:(j + 1) * P], router[0:DC, 1, :], start=False, stop=True)
                mm.then_inc(s_lg, 1)
                pe.wait_ge(s_x, g * 2 + 2)
            pe.wait_ge(s_b2, 16)
            with pe.Fori(0, GROUPS) as g:
                pe.wait_ge(s_cg, g + 1)
                for j in range(TPG):
                    mm = nc.tensor.transpose(H[0:EXPERTS, 0, j * P:(j + 1) * P], cg[:, j * EXPERTS:(j + 1) * EXPERTS],
                                             c.ident[:, :])
                mm.then_inc(s_ct, 1)
                pe.wait_ge(s_cTs, g + 1)
                for j in range(TPG):
                    mm = nc.tensor.matmul(O[:, j // 2, (j % 2) * D:(j % 2 + 1) * D], cT[:, j * P:(j + 1) * P], b2[:, :],
                                          start=True, stop=True)
                    if j % 2:
                        mm.then_inc(s_bo, 1)
                pe.wait_ge(s_bh, g * TPG + TPG)
            with pe.Fori(0, EXPERTS // 2) as ep:
                for b in range(2):
                    with pe.Fori(0, GROUPS) as g:
                        it = (ep * 2 + b) * GROUPS + g
                        pe.wait_ge(s_w[b], ep * 48 + 48)

                        def down(f):
                            pe.wait_ge(s_gelu, it * FC + f + 1)
                            if f == 0:
                                pe.wait_ge(s_y, it * TPG + TPG)
                            for j in range(TPG):
                                mm = nc.tensor.matmul(O[:, j // 2, (j % 2) * D:(j % 2 + 1) * D],
                                                      hT[:, f, j * P:(j + 1) * P], w2[:, b, f, :],
                                                      start=(f == 0 and j % 2 == 0), stop=(f == FC - 1),
                                                      skip_group_check=True)
                                if f == FC - 1 and j == 1:
                                    mm.then_inc(s_o, 1)
                            mm.then_inc(s_down, 1)

                        for f in range(FC):
                            for cc in range(2):
                                mm = nc.tensor.matmul(H[:, f, :], w1[:, b, cc, f * P:(f + 1) * P],
                                                      xall[:, cc, bass.ds(g * GT, GT)], start=(cc == 0), stop=(cc == 1))
                            mm.then_inc(s_up, 1)
                            if f >= 1:
                                down(f - 1)
                        down(FC - 1)



def scan_block(nc, c):
    with Semaphores(nc) as pool, ExitStack() as ctx:
        def sb(name, shape, dt=F32):
            return ctx.enter_context(nc.sbuf_tensor("s_" + name, shape, dt))

        def sem(name):
            return pool.new("scan_" + name)

        def ps(name, shape):
            return ctx.enter_context(nc.psum_tensor("s_" + name, shape, F32))

        W = IC * GT
        IMG = GT // SEQ
        FIRST = 1e30
        n = sb("n", [P, TPG, D])
        n1 = sb("n1", [P, TPG, D])
        xT = sb("xT", [DC, 2, GT])
        xpad = sb("xpad", [P, IC, IMG, SEQ + TAPS - 1])
        pool4 = c.x1[:, :, :].rearrange("p t d -> p (t d)")
        xc, sz, delta, u = (pool4[:, i * W:(i + 1) * W] for i in range(4))
        pre = sb("pre", [P, W])
        soft = sb("soft", [P, W])
        dbc = sb("dbc", [2 * STATES + 1, GT])
        dA = sb("dA", [P, 2, W])
        hs = sb("hs", [P, 2, W])
        hc = sb("hc", [P, 2, W])
        A = sb("A", [P, IC * STATES])
        wo = sb("wo", [P, IC * D])
        part = sb("part", [P, 2])
        scale = sb("scale", [P, 4])
        ss, rs, rt = sb("ss", [P, TPG]), sb("rs", [P, TPG]), sb("rt", [P, TPG])
        BC, Y, X = ps("BC", [P, 4, 512]), ps("Y", [P, IC, 512]), ps("X", [P, 512])
        s_dve, s_var, s_log, s_guess = [sem(x) for x in ("dve", "var", "log", "guess")]
        s_part, s_tot, s_alog, s_A = [sem(x) for x in ("part", "tot", "alog", "A")]
        s_n, s_h, s_T, s_xTa, s_xTd, s_in, s_sz, s_conv, s_xc = [sem(x) for x in ("n", "h", "T", "xTa", "xTd", "in", "sz", "conv", "xc")]
        s_dbc, s_dbcs, s_dt, s_pre, s_abs, s_soft, s_u = [sem(x) for x in ("dbc", "dbcs", "dt", "pre", "abs", "soft", "u")]
        s_bc, s_dA, s_scan, s_hc, s_hcu, s_y, s_yg, s_sq, s_out, s_v, s_r0, s_rg = [
            sem(x) for x in ("bc", "dA", "scan", "hc", "hcu", "y", "yg", "sq", "out", "v", "r0", "rg")]
        block = ctx.enter_context(nc.Block())
        win = weight(c, "inproj")
        bank = [BC[:, 0, :], BC[:, 1, :], BC[:, 2, :], BC[:, 3, :], Y[:, 0, :], Y[:, 1, :]]

        def chunk(x, i):
            return x[:, i * GT:(i + 1) * GT]

        @block.vector
        def _(dve):
            own = Count(s_dve)
            token_stats(nc, dve, c, own.link, c.h)
            norm_factors_dve(nc, dve, c, own.link, s_var, s_guess, twice=True)
            woraw = col(c, "outproj")
            own.link(dve, nc.vector.memset(part[:, :], 0.0))
            own.link(dve, nc.vector.tensor_reduce(part[0:DC, 0:1], win[0:DC], AX.XY, ALU.add, apply_absolute_value=True))
            own.link(dve, nc.vector.tensor_reduce(part[:, 1:2], woraw, AX.X, ALU.add, apply_absolute_value=True))
            dve.sem_inc(s_part, 1)
            dve.wait_ge(s_tot, 1)
            own.link(dve, nc.vector.tensor_scalar(scale[:, 0:1], X[:, 0:1], 1.0 / (2 * INNER * D), 1e-5, ALU.mult, ALU.max))
            own.link(dve, nc.vector.tensor_scalar(scale[:, 1:2], X[:, 1:2], 1.0 / (INNER * D), 1e-5, ALU.mult, ALU.max))
            own.link(dve, nc.vector.reciprocal(scale[:, 2:4], scale[:, 0:2]))
            for w, k, m in ((win[0:DC], 2, DC), (woraw, 3, P)):
                own.link(dve, nc.vector.tensor_scalar(w, w, scale[0:m, k:k + 1], 1.0, ALU.mult, ALU.min))
                own.link(dve, nc.vector.tensor_scalar(w, w, -1.0, ROUND, ALU.max, ALU.add))
                own.link(dve, nc.vector.tensor_scalar(w, w, ROUND, None, ALU.subtract))
            for i in range(IC):
                own.link(dve, nc.vector.tensor_scalar(wo[:, i * D:(i + 1) * D], woraw[:, i * D:(i + 1) * D],
                                                      col(c, "onorm")[:, i:i + 1], None, ALU.mult))
            nc.vector.tensor_scalar(A[:, :], col(c, "alog"), -20.0, 2.0, ALU.max, ALU.min).then_inc(s_alog, 1)
            dve.wait_ge(s_A, 1)
            own.link(dve, nc.vector.tensor_scalar(A[:, :], A[:, :], -1.0, None, ALU.mult))
            own.link(dve, nc.vector.memset(xpad[:, :, :, 0:TAPS - 1], 0.0))
            dve.sem_inc(s_part, 1)
            dve.sem_inc(s_scan, 4)
            done = own.n
            per_group = TPG + IC * TAPS + 1 + 2 + IC + 1 + 4
            with dve.Fori(0, GROUPS) as g:
                own = Count(s_dve, g * per_group + done)
                for j in range(TPG):
                    nc.vector.tensor_scalar(n[:, j, :], tile_view(c.h, g, j), factor(c, 2, g, j), factor(c, 3, g, j),
                                            ALU.mult, ALU.add).then_inc(s_n, 1)
                for j in range(TPG):
                    own.link(dve, nc.vector.tensor_scalar(n1[:, j, :], tile_view(c.h, g, j), factor(c, 0, g, j),
                                                          factor(c, 1, g, j), ALU.mult, ALU.add))
                for j in range(TPG):
                    nc.vector.tensor_tensor(tile_view(c.h, g, j), n1[:, j, :], tile_view(c.h, g, j), ALU.add).then_inc(s_h, 1)
                dve.wait_ge(s_T, g * 2 + 2)
                nc.vector.tensor_scalar(xT[:, 1, :], Y[0:DC, 1, :], col(c, "rmsw")[0:DC, 1:2], None, ALU.mult).then_inc(s_xTd, 1)
                for i in range(IC):
                    dve.wait_ge(s_in, g * 6 + i + 1)
                    own.link(dve, nc.vector.tensor_scalar(xpad[:, i, :, TAPS - 1:], bank[i].rearrange("p (m t) -> p m t", t=SEQ),
                                                          scale[:, 0:1], None, ALU.mult))
                    out = chunk(pre, i).rearrange("p (m t) -> p m t", t=SEQ)
                    for k in range(TAPS):
                        w = col(c, "conv")[:, i * TAPS + k:i * TAPS + k + 1]
                        src = xpad[:, i, :, k:k + SEQ]
                        if k == 0:
                            own.link(dve, nc.vector.tensor_scalar(out, src, w, col(c, "convb")[:, i:i + 1], ALU.mult, ALU.add))
                        else:
                            ins = nc.vector.scalar_tensor_tensor(out=out, in0=src, scalar=w, in1=out, op0=ALU.mult, op1=ALU.add)
                            if k < TAPS - 1:
                                own.link(dve, ins)
                            else:
                                ins.then_inc(s_conv, 1)
                dve.wait_ge(s_dbc, g + 1)
                own.link(dve, nc.vector.tensor_scalar(dbc[:, :], X[0:2 * STATES + 1, :], 1.0, None, ALU.mult))
                dve.sem_inc(s_dbcs, 1)
                for i in range(IC):
                    dve.wait_ge(s_dt, g * IC + i + 1)
                    nc.vector.tensor_scalar(chunk(pre, i), BC[:, i, :], col(c, "dtb")[:, i:i + 1], None, ALU.add).then_inc(s_pre, 1)
                dve.wait_ge(s_soft, g + 1)
                own.link(dve, nc.vector.scalar_tensor_tensor(out=delta, in0=pre[:, :], scalar=0.0, in1=soft[:, :],
                                                             op0=ALU.max, op1=ALU.add))
                own.link(dve, nc.vector.tensor_tensor(u, delta, xc, ALU.mult))
                nc.vector.memset(delta.rearrange("p (m t) -> p m t", t=SEQ)[:, :, 0:1], FIRST).then_inc(s_u, 1)
                for s in range(STATES):
                    b = s % 2
                    dve.wait_ge(s_bc, (g * STATES + s) * 2 + 1)
                    nc.vector.tensor_tensor(hs[:, b].rearrange("p (i t) -> p i t", i=IC), u.rearrange("p (i t) -> p i t", i=IC),
                                            BC[:, b:b + 1, :].broadcast_to([P, IC, GT]), ALU.mult).then_inc(s_scan, 1)
                    dve.wait_ge(s_scan, (g * STATES + s) * 2 + 5)
                    dve.wait_ge(s_dA, (g * STATES + s) * IC + IC)
                    nc.vector.tensor_tensor_scan(hs[:, b], dA[:, b], hs[:, b], 0.0, ALU.mult, ALU.add).then_inc(s_scan, 1)
                    dve.wait_ge(s_scan, (g * STATES + s) * 2 + 6)
                    dve.wait_ge(s_bc, (g * STATES + s) * 2 + 2)
                    dve.wait_ge(s_hcu, (g * STATES + s) + 1)
                    nc.vector.tensor_tensor(hc[:, b].rearrange("p (i t) -> p i t", i=IC), hs[:, b].rearrange("p (i t) -> p i t", i=IC),
                                            BC[:, 2 + b:3 + b, :].broadcast_to([P, IC, GT]), ALU.mult).then_inc(s_hc, 1)
                dve.wait_ge(s_hc, (g + 1) * STATES)
                dve.wait_ge(s_hcu, (g + 1) * STATES + 2)
                for i in range(IC):
                    own.link(dve, nc.vector.scalar_tensor_tensor(out=chunk(pre, i), in0=chunk(xc, i),
                                                                 scalar=col(c, "dskip")[:, i:i + 1], in1=Y[:, i, :],
                                                                 op0=ALU.mult, op1=ALU.add))
                nc.vector.tensor_tensor(pre[:, :], pre[:, :], sz, ALU.mult).then_inc(s_yg, 1)
                dve.wait_ge(s_out, g * 3 + 1)
                own.link(dve, nc.vector.tensor_scalar(ss[:, :], X[:, 0:TPG], 1.0 / INNER, LN_EPS, ALU.mult, ALU.add))
                dve.sem_inc(s_v, 1)
                dve.wait_ge(s_rg, g + 1)
                own.link(dve, nc.vector.tensor_tensor(rt[:, :], rs[:, :], rs[:, :], ALU.mult))
                own.link(dve, nc.vector.tensor_tensor(rt[:, :], rt[:, :], ss[:, :], ALU.mult))
                own.link(dve, nc.vector.tensor_scalar(rt[:, :], rt[:, :], -0.5, 1.5, ALU.mult, ALU.add))
                own.link(dve, nc.vector.scalar_tensor_tensor(out=rt[:, :], in0=rs[:, :], scalar=scale[:, 1:2], in1=rt[:, :],
                                                             op0=ALU.mult, op1=ALU.mult))
                dve.wait_ge(s_h, g * (TPG * 2) + TPG)
                for j in range(TPG):
                    if j % 2 == 0:
                        dve.wait_ge(s_out, g * 3 + 2 + j // 2)
                    nc.vector.scalar_tensor_tensor(out=tile_view(c.h, g, j), in0=BC[:, j // 2, (j % 2) * D:(j % 2 + 1) * D],
                                                   scalar=rt[:, j:j + 1], in1=tile_view(c.h, g, j), op0=ALU.mult,
                                                   op1=ALU.add).then_inc(s_h, 1)
                dve.wait_ge(s_h, (g + 1) * (TPG * 2))
                assert own.n == per_group, (own.n, per_group)

        @block.scalar
        def _(act):
            nc.scalar.preload_act_table_set(LOG_EXP)
            norm_factors_act(nc, act, c, s_var, s_log, s_guess, twice=True)
            act.wait_ge(s_alog, 1)
            nc.scalar.activation(A[:, :], A[:, :], ACT.Exp).then_inc(s_A, 1)
            act.wait_ge(s_part, 2)
            with act.Fori(0, GROUPS) as g:
                act.wait_ge(s_T, g * 2 + 1)
                nc.scalar.activation(xT[:, 0, :], Y[0:DC, 0, :], ACT.Copy, scale=col(c, "rmsw")[0:DC, 0:1]).then_inc(s_xTa, 1)
                for i in range(IC):
                    act.wait_ge(s_in, g * 6 + 4 + i)
                    nc.scalar.activation(chunk(sz, i), bank[3 + i], ACT.Silu, scale=scale[:, 0:1]).then_inc(s_sz, 1)
                for i in range(IC):
                    act.wait_ge(s_conv, g * IC + i + 1)
                    nc.scalar.activation(chunk(xc, i), chunk(pre, i), ACT.Silu).then_inc(s_xc, 1)
                act.wait_ge(s_pre, g * IC + IC)
                nc.scalar.activation(soft[:, :], pre[:, :], ACT.Abs).then_inc(s_abs, 1)
                act.wait_ge(s_abs, g * 2 + 1)
                nc.scalar.activation(soft[:, :], soft[:, :], ACT.Exp, scale=-1.0).then_inc(s_abs, 1)
                act.wait_ge(s_abs, g * 2 + 2)
                nc.scalar.activation(soft[:, :], soft[:, :], ACT.Ln, bias=1.0).then_inc(s_soft, 1)
                act.wait_ge(s_u, g + 1)
                for s in range(STATES):
                    act.wait_ge(s_scan, (g * STATES + s) * 2 + 2)
                    for i in range(IC):
                        nc.scalar.activation(dA[:, s % 2, i * GT:(i + 1) * GT], chunk(delta, i), ACT.Exp,
                                             scale=A[:, i * STATES + s:i * STATES + s + 1]).then_inc(s_dA, 1)
                act.wait_ge(s_yg, g + 1)
                nc.scalar.activation(soft[:, :], pre[:, :], ACT.Square).then_inc(s_sq, 1)
                act.wait_ge(s_v, g + 1)
                nc.scalar.activation(rs[:, :], ss[:, :], ACT.Ln).then_inc(s_r0, 1)
                act.wait_ge(s_r0, g + 1)
                nc.scalar.activation(rs[:, :], rs[:, :], ACT.Exp, scale=-0.5).then_inc(s_rg, 1)

        @block.tensor
        def _(pe):
            pe.wait_ge(s_part, 1)
            mm = nc.tensor.matmul(X[:, 0:2], c.ones[:, :], part[:, :], start=True, stop=True).then_inc(s_tot, 1)
            pe.wait_ge(s_part, 2)
            pe.sem_inc(s_hcu, 2)
            with pe.Fori(0, GROUPS) as g:
                pe.wait_ge(s_n, g * TPG + TPG)
                for cc in range(2):
                    for j in range(TPG):
                        mm = nc.tensor.transpose(Y[0:DC, cc, j * P:(j + 1) * P], n[:, j, cc * DC:(cc + 1) * DC], c.ident[:, :])
                    mm.then_inc(s_T, 1)
                pe.wait_ge(s_xTa, g + 1)
                pe.wait_ge(s_xTd, g + 1)
                for i in range(2 * IC):
                    for cc in range(2):
                        mm = nc.tensor.matmul(bank[i], win[0:DC, cc, i * P:(i + 1) * P], xT[:, cc, :], start=(cc == 0), stop=(cc == 1))
                    mm.then_inc(s_in, 1)
                for i in range(IC):
                    pe.wait_ge(s_xc, g * IC + i + 1)
                    mm = nc.tensor.matmul(X[0:2 * STATES + 1, :], col(c, "xproj")[:, i * 33:(i + 1) * 33], chunk(xc, i),
                                          start=(i == 0), stop=(i == IC - 1))
                mm.then_inc(s_dbc, 1)
                pe.wait_ge(s_dbcs, g + 1)
                for i in range(IC):
                    nc.tensor.matmul(BC[:, i, :], c.rowp[0:1, ROWP_DT + i * P:ROWP_DT + (i + 1) * P], dbc[0:1, :],
                                     start=True, stop=True).then_inc(s_dt, 1)
                pe.wait_ge(s_pre, g * IC + IC)
                pe.wait_ge(s_sz, g * IC + IC)

                def spread(s):
                    b = s % 2
                    for k in range(2):
                        row = 1 + k * STATES + s
                        nc.tensor.matmul(BC[:, 2 * k + b, :],
                                         c.ident[0:2 * STATES + 1, row:row + 1].broadcast_to([2 * STATES + 1, P]),
                                         dbc[:, :], start=True, stop=True).then_inc(s_bc, 1)

                spread(0)
                for s in range(STATES):
                    if s + 1 < STATES:
                        if s >= 1:
                            pe.wait_ge(s_hc, g * STATES + s)
                        spread(s + 1)
                    pe.wait_ge(s_hc, g * STATES + s + 1)
                    for i in range(IC):
                        mm = nc.tensor.matmul(Y[:, i, :], c.ident[:, :], hc[:, s % 2, i * GT:(i + 1) * GT], start=(s == 0),
                                              stop=(s == STATES - 1))
                    mm.then_inc(s_hcu, 1)
                pe.wait_ge(s_sq, g + 1)
                for j in range(TPG):
                    for i in range(IC):
                        at = i * GT + j * P
                        mm = nc.tensor.matmul(X[:, j:j + 1], soft[:, at:at + P], c.ones[:, 0:1], start=(i == 0), stop=(i == IC - 1))
                mm.then_inc(s_out, 1)
                for j in range(TPG):
                    for i in range(IC):
                        at = i * GT + j * P
                        mm = nc.tensor.matmul(BC[:, j // 2, (j % 2) * D:(j % 2 + 1) * D], pre[:, at:at + P],
                                              wo[:, i * D:(i + 1) * D], start=(i == 0), stop=(i == IC - 1))
                    if j % 2:
                        mm.then_inc(s_out, 1)
                pe.wait_ge(s_h, (g + 1) * (TPG * 2))



def feed_forward(nc, c, out):
    with Semaphores(nc) as pool, ExitStack() as ctx:
        def sb(name, shape, dt=F32):
            return ctx.enter_context(nc.sbuf_tensor("f_" + name, shape, dt))

        def sem(name):
            return pool.new("f_" + name)

        def ps(name, shape):
            return ctx.enter_context(nc.psum_tensor("f_" + name, shape, F32))

        n = sb("n", [P, TPG, D])
        xT = sb("xT", [DC, 2, GT])
        hT = sb("hT", [P, FC, GT])
        y = sb("y", [P, TPG, D])
        H, O = ps("H", [P, FC, 512]), ps("O", [P, 2, 512])
        w1, w2, b1 = weight(c, "f1"), col(c, "f2"), col(c, "f1b")
        s_dve, s_var, s_log, s_guess = [sem(x) for x in ("dve", "var", "log", "guess")]
        s_n, s_T, s_xT, s_up, s_gelu, s_o, s_y, s_out = [sem(x) for x in ("n", "T", "xT", "up", "gelu", "o", "y", "out")]
        block = ctx.enter_context(nc.Block())
        rows = out.rearrange("(t p) d -> p t d", p=P)

        @block.sync
        def _(sp):
            sp.sem_inc(s_out, 16)
            with sp.Fori(0, GROUPS) as g:
                sp.wait_ge(s_y, g * TPG + TPG)
                sp.dma_start(rows[:, bass.ds(g * TPG, TPG), :], y[:, :, :]).then_inc(s_out, 16)
            sp.wait_ge(s_out, GROUPS * 16 + 16)

        @block.vector
        def _(dve):
            own = Count(s_dve)
            token_stats(nc, dve, c, own.link, c.x1)
            norm_factors_dve(nc, dve, c, own.link, s_var, s_guess, twice=False)
            with dve.Fori(0, GROUPS) as g:
                for j in range(TPG):
                    nc.vector.tensor_scalar(n[:, j, :], tile_view(c.x1, g, j), factor(c, 0, g, j), factor(c, 1, g, j),
                                            ALU.mult, ALU.add).then_inc(s_n, 1)
                for cc in range(2):
                    dve.wait_ge(s_T, g * 2 + cc + 1)
                    nc.vector.tensor_scalar(xT[:, cc, :], O[0:DC, cc, :], col(c, "g2")[0:DC, cc:cc + 1],
                                            col(c, "b2")[0:DC, cc:cc + 1], ALU.mult, ALU.add).then_inc(s_xT, 1)
                dve.wait_ge(s_out, g * 16 + 16)
                for j in range(TPG):
                    if j % 2 == 0:
                        dve.wait_ge(s_o, g * 2 + j // 2 + 1)
                    nc.vector.tensor_tensor(y[:, j, :], O[:, j // 2, (j % 2) * D:(j % 2 + 1) * D], tile_view(c.h, g, j),
                                            ALU.add).then_inc(s_y, 1)

        @block.scalar
        def _(act):
            nc.scalar.preload_act_table_set(LOG_EXP)
            norm_factors_act(nc, act, c, s_var, s_log, s_guess, twice=False)
            nc.scalar.preload_act_table(ACT.Gelu)
            with act.Fori(0, GROUPS) as g:
                for f in range(FC):
                    act.wait_ge(s_up, g * FC + f + 1)
                    nc.scalar.activation(hT[:, f, :], H[:, f, :], ACT.Gelu, bias=b1[:, f:f + 1]).then_inc(s_gelu, 1)

        @block.tensor
        def _(pe):
            with pe.Fori(0, GROUPS) as g:
                pe.wait_ge(s_n, g * TPG + TPG)
                for cc in range(2):
                    for j in range(TPG):
                        mm = nc.tensor.transpose(O[0:DC, cc, j * P:(j + 1) * P], n[:, j, cc * DC:(cc + 1) * DC], c.ident[:, :])
                    mm.then_inc(s_T, 1)
                pe.wait_ge(s_xT, g * 2 + 2)

                def down(f):
                    pe.wait_ge(s_gelu, g * FC + f + 1)
                    for j in range(TPG):
                        o = O[:, j // 2, (j % 2) * D:(j % 2 + 1) * D]
                        if f == 0:
                            nc.tensor.matmul(o, c.ones[0:1, :], c.rowp[0:1, ROWP_BF2:ROWP_BF2 + D], start=(j % 2 == 0),
                                             stop=False, skip_group_check=True)
                        mm = nc.tensor.matmul(o, hT[:, f, j * P:(j + 1) * P], w2[:, f * D:(f + 1) * D], start=False,
                                              stop=(f == FC - 1), skip_group_check=True)
                        if f == FC - 1 and j % 2:
                            mm.then_inc(s_o, 1)

                for f in range(FC):
                    for cc in range(2):
                        mm = nc.tensor.matmul(H[:, f, :], w1[0:DC, cc, f * P:(f + 1) * P], xT[:, cc, :], start=(cc == 0),
                                              stop=(cc == 1))
                    mm.then_inc(s_up, 1)
                    if f >= 1:
                        down(f - 1)
                down(FC - 1)
                pe.wait_ge(s_y, g * TPG + TPG)



STOP = 99


def program(nc, patches, w_tok, w97, rows, cols, proj, e1, e2, eb1, eb2, extra, out):
    with ExitStack() as ctx:
        c = make_core(nc, ctx)
        scratch = nc.dram_tensor("attention", (IMAGES, HEADS, SEQ, DH), F32, kind="Internal").ap()
        tokenize(nc, c, patches, w_tok, w97, rows, cols, extra)
        if STOP > 0:
            performer(nc, c, proj, scratch)
            performer_out(nc, c, scratch)
        if STOP > 1:
            attention(nc, c, ("aq", "ak", "av", "ao"), "ln1g", "ln1b", mixing=False)
            experts(nc, c, e1, e2, eb1, eb2)
        if STOP > 2:
            scan_block(nc, c)
        if STOP > 3:
            attention(nc, c, ("mq", "mk", "mv", "mo"), "g1", "b1", mixing=True)
            feed_forward(nc, c, out)
            return
        with ExitStack() as c2:
            s_o = c2.enter_context(nc.semaphore("s_o"))
            block = c2.enter_context(nc.Block())

            @block.sync
            def _(sp):
                sp.dma_start(out.rearrange("(t p) d -> p t d", p=P), c.h[:, :, :]).then_inc(s_o, 16)
                sp.wait_ge(s_o, 16)


def two_chunks(w, bias, np):
    out = np.zeros((DC + 1, 2, w.shape[1]), w.dtype)
    out[0:DC, 0], out[0:DC, 1] = w[0:DC], w[DC:D]
    if bias is not None:
        out[DC, 0] = bias
    return out


def by_block(w):
    return w.reshape(w.shape[:-1] + (3, 2, 2 * DH)).swapaxes(-3, -2).reshape(w.shape)


def kernel(**inputs):
    import numpy as np
    import concourse.bacc as _bacc
    from concourse.bass_utils import run_bass_kernel_spmd as _run

    a = {k: np.asarray(v) for k, v in inputs.items()}
    patches = a["x"].reshape(GROUPS, IMAGES // GROUPS, 3, 8, 16, 8, 16).transpose(0, 2, 4, 6, 1, 3, 5)
    patches = patches.reshape(GROUPS, PKC, P, GT).transpose(0, 2, 1, 3).reshape(GROUPS, P, PKC * GT)
    w_tok = a["L0_tok_W"].reshape(D, PKC, P).transpose(2, 1, 0).reshape(P, PKC * D)
    qkv, qkvb = a["L0_ffn_in_proj_w"].T, a["L0_ffn_in_proj_b"]
    w97 = {
        "pq": (by_block(a["L0_attn_Wq"]), by_block(a["L0_attn_bq"])),
        "pk": (by_block(a["L0_attn_Wk"]), by_block(a["L0_attn_bk"])),
        "pv": (a["L0_attn_Wv"], a["L0_attn_bv"]), "po": (a["L0_attn_Wo"], a["L0_attn_bo"]),
        "aq": (by_block(qkv[:, 0:D]), by_block(qkvb[0:D])), "ak": (by_block(qkv[:, D:2 * D]), by_block(qkvb[D:2 * D])),
        "av": (qkv[:, 2 * D:], qkvb[2 * D:]), "ao": (a["L0_ffn_out_proj_w"].T, a["L0_ffn_out_proj_b"]),
        "router": (a["L0_ffn_router_w"].T, a["L0_ffn_router_b"]),
        "mq": (by_block(a["L1_ffn_Wq"]), by_block(a["L1_ffn_bq"])),
        "mk": (by_block(a["L1_ffn_Wk"]), by_block(a["L1_ffn_bk"])),
        "mv": (np.concatenate([a["L1_ffn_Wv"], a["L1_ffn_Wr"][:, None]], 1),
               np.concatenate([a["L1_ffn_bv"], a["L1_ffn_br"].reshape(1)])),
        "mo": (a["L1_ffn_Wo"], a["L1_ffn_bo"]), "mm": (a["L1_ffn_Wm"], a["L1_ffn_bm"]),
        "f1": (a["L1_ffn_W1"], None), "inproj": (a["L1_attn_in_proj_weight"].T, None),
    }
    w97 = np.concatenate([two_chunks(*w97[n], np) for n, _ in W97], axis=2)
    rows = np.concatenate([a["L0_tok_b"], a["L0_tok_alpha_w"].reshape(1), a["L0_tok_alpha_a"].reshape(1)])[None, :]

    def chan(x):
        return x.reshape(IC, P, -1).transpose(1, 0, 2).reshape(P, -1)

    def half(x):
        out = np.zeros((P, 2), x.dtype)
        out[0:DC] = x.reshape(2, DC).T
        return out

    cols = {
        "f2": a["L1_ffn_W2"].reshape(FC, P, D).transpose(1, 0, 2).reshape(P, FC * D),
        "outproj": chan(a["L1_attn_out_proj_weight"].T), "xproj": chan(a["L1_attn_x_proj_weight"].T),
        "f1b": a["L1_ffn_bf1"].reshape(FC, P).T, "conv": chan(a["L1_attn_conv_weight"].reshape(INNER, TAPS)),
        "convb": chan(a["L1_attn_conv_bias"]), "dtb": chan(a["L1_attn_dt_proj_bias"]),
        "alog": chan(a["L1_attn_A_log"]), "dskip": chan(a["L1_attn_D"]), "onorm": chan(a["L1_attn_out_norm_weight"]),
        "ln1g": half(a["L0_ffn_ln1_g"]), "ln1b": half(a["L0_ffn_ln1_b"]), "ln2g": half(a["L0_ffn_ln2_g"]),
        "ln2b": half(a["L0_ffn_ln2_b"]), "rmsw": half(a["L1_attn_norm_weight"]), "g1": half(a["L1_ffn_g1"]),
        "b1": half(a["L1_ffn_b1"]), "g2": half(a["L1_ffn_g2"]), "b2": half(a["L1_ffn_b2"]),
    }
    headsum = np.zeros((P, 3, 2), np.float32)
    for b in range(3):
        for r in range(2):
            headsum[32 * b + DH * r:32 * b + DH * (r + 1), b, r] = 0.5 / np.sqrt(DH)
    cols["headsum"] = headsum.reshape(P, 6)
    cols["half"] = np.tile(np.repeat(np.eye(2, dtype=np.float32), DH, axis=0), (4, 1))
    cols["tri"] = np.tile(np.tril(np.ones((EXPERTS, EXPERTS), np.float32), -1).reshape(1, -1), (P, 1))
    cols = np.concatenate([cols[n] for n, _ in COLS], axis=1)
    proj = np.zeros((3, 2, DH, 2, FEATURES), np.float32)
    for r in range(2):
        proj[:, r, :, r, :] = a["L0_attn_proj"].T
    proj = proj.reshape(DC, 2 * FEATURES)
    e1 = a["L0_ffn_w1"].reshape(EXPERTS, 2, DC, FF).transpose(0, 2, 1, 3)
    e2 = a["L0_ffn_w2"].reshape(EXPERTS, FC, P, D).transpose(0, 2, 1, 3)
    extra = np.concatenate([a["L1_attn_dt_proj_weight"].reshape(-1), a["L1_ffn_bf2"], a["L1_ffn_bm"]])[None, :]
    eb1 = a["L0_ffn_b1"].reshape(EXPERTS, FC, P).transpose(0, 2, 1)
    arrays = dict(patches=patches, w_tok=w_tok, w97=w97, rows=rows, cols=cols, proj=proj, e1=e1, e2=e2, eb1=eb1,
                  eb2=a["L0_ffn_b2"], extra=extra)
    arrays = {k: np.ascontiguousarray(v) for k, v in arrays.items()}
    nc = _bacc.Bacc("TRN2", target_bir_lowering=False, num_devices=1)
    args = [nc.dram_tensor(f"in_{k}", v.shape, F32, kind="ExternalInput").ap() for k, v in arrays.items()]
    out = nc.dram_tensor("out", (TOKENS, D), F32, kind="ExternalOutput").ap()
    program(nc, *args, out)
    r = _run(nc, [{f"in_{k}": v for k, v in arrays.items()}], core_ids=[0])
    return r.results[0]["out"].reshape(IMAGES, SEQ, D)
```

```python
from contextlib import ExitStack

import concourse.bass as bass
from concourse import mybir

F32 = mybir.dt.float32
BF16 = mybir.dt.bfloat16
ALU = mybir.AluOpType
ACT = mybir.ActivationFunctionType
AX = mybir.AxisListType

P = 128
IMAGES = 64
SEQ = 64
TOKENS = IMAGES * SEQ
D = 192
DC = D // 2
HEADS = 12
DH = D // HEADS
TILES = TOKENS // P
TPG = 4
GROUPS = TILES // TPG
GT = TPG * P
PATCH_K = 3 * 16 * 16
PKC = PATCH_K // P
FEATURES = 128
EXPERTS = 8
FF = 768
FC = FF // P
INNER = 384
IC = INNER // P
SLOT = 256
SLOTS = (TOKENS * 2 + EXPERTS * (SLOT - 1)) // SLOT
STATES = 16
TAPS = 4
ROUND = 12582912.0
LN_EPS = 1e-5
FEATURE_EPS = 1e-6
POOL_EPS = 1e-6
ROUTED = max(1, int(round(0.15 * SEQ)))
LOG_EXP = "natural_log_exp_and_others"

W97 = [("pq", D), ("pk", D), ("pv", D), ("po", D), ("aq", D), ("ak", D), ("av", D), ("ao", D), ("router", EXPERTS),
       ("mq", D), ("mk", D), ("mv", D + 1), ("mo", D), ("mm", D), ("f1", FF), ("inproj", 2 * INNER)]
ROWS = [("tok_b", D), ("alpha_w", 1), ("alpha_a", 1)]
COLS = [("f2", FC * D), ("outproj", IC * D), ("xproj", IC * 33), ("headsum", 6), ("half", 2), ("tri", EXPERTS * EXPERTS),
        ("starts", TOKENS // SLOT), ("slots", SLOTS), ("f1b", FC), ("conv", IC * TAPS), ("convb", IC),
        ("dtb", IC), ("alog", IC * STATES), ("dskip", IC), ("onorm", IC), 
        ("ln1g", 2), ("ln1b", 2), ("ln2g", 2), ("ln2b", 2), ("rmsw", 2), ("g1", 2), ("b1", 2), ("g2", 2), ("b2", 2)]


def offsets(parts):
    at, out = 0, {}
    for name, n in parts:
        out[name] = (at, n)
        at += n
    return out, at


W97_AT, W97_N = offsets(W97)
ROWS_AT, ROWS_N = offsets(ROWS)
COLS_AT, COLS_N = offsets(COLS)


ROWP_DT, ROWP_BF2, ROWP_BM, ROWP_N = 0, INNER, INNER + D, INNER + 2 * D


class Count:

    def __init__(self, sem, base=0):
        self.sem, self.base, self.n = sem, base, 0

    def inc(self, ins):
        self.n += 1
        return ins.then_inc(self.sem, 1)

    def link(self, eng, ins):
        self.inc(ins)
        eng.wait_ge(self.sem, self.base + self.n)


class Semaphores:

    def __init__(self, nc):
        self.nc, self.all = nc, []

    def __enter__(self):
        return self

    def new(self, name):
        self.all.append(self.nc.alloc_semaphore(name))
        return self.all[-1]

    def __exit__(self, *_):
        self.nc.clear_and_free_semaphores(self.all)
        self.nc.all_engine_barrier()


class Core:
    pass


def make_core(nc, ctx):
    c = Core()

    def sb(name, shape, dt=F32):
        return ctx.enter_context(nc.sbuf_tensor(name, shape, dt))

    c.h = sb("h", [P, TILES, D])
    c.x1 = sb("x1", [P, TILES, D])
    c.w = sb("w97", [DC + 1, 2, W97_N])
    c.cols = sb("cols", [P, COLS_N])
    c.rows = sb("rows", [P, ROWS_N])
    c.rowp = sb("rowp", [1, ROWP_N])
    c.ident = sb("ident", [P, P])
    c.same = sb("same", [P, P])
    c.lower = sb("lower", [P, P])
    c.ones = sb("ones", [P, P])
    c.st = sb("st", [P, TILES, 6])
    c.mv = sb("mv", [P, 2, TILES])
    c.rstd = sb("rstd", [P, 6, TILES])
    return c


def weight(c, name):
    at, n = W97_AT[name]
    return c.w[:, :, at:at + n]


def col(c, name):
    at, n = COLS_AT[name]
    return c.cols[:, at:at + n]


def tile_view(x, g, j):
    return x[:, bass.ds(g * TPG + j, 1), :].rearrange("p a d -> p (a d)")


def token_stats(nc, dve, c, link, x):
    with dve.Fori(0, TILES) as t:
        nc.vector.bn_stats(c.st[:, bass.ds(t, 1), :].rearrange("p a s -> p (a s)"),
                           x[:, bass.ds(t, 1), :].rearrange("p a d -> p (a d)"))
    link(dve, nc.vector.memset(c.rstd[:, 0, :], 0.0))
    mean, var, t = c.mv[:, 0, :], c.mv[:, 1, :], c.rstd[:, 0, :]
    even, odd, even2, odd2 = (c.st[:, :, i] for i in (1, 4, 2, 5))
    link(dve, nc.vector.tensor_tensor(mean, even, odd, ALU.add))
    link(dve, nc.vector.tensor_scalar(mean, mean, 0.5, None, ALU.mult))
    link(dve, nc.vector.tensor_tensor(var, even2, odd2, ALU.add))
    link(dve, nc.vector.tensor_scalar(var, var, 1.0 / D, None, ALU.mult))
    link(dve, nc.vector.tensor_tensor(t, even, odd, ALU.subtract))
    link(dve, nc.vector.scalar_tensor_tensor(out=t, in0=t, scalar=0.25, in1=t, op0=ALU.mult, op1=ALU.mult))
    link(dve, nc.vector.tensor_tensor(var, var, t, ALU.add))


def norm_factors_dve(nc, dve, c, link, s_var, s_guess, twice):
    mean, var = c.mv[:, 0, :], c.mv[:, 1, :]
    r, nm, r2, nm2, v, t = (c.rstd[:, i, :] for i in range(6))
    for turn in range(2 if twice else 1):
        if turn == 1:
            link(dve, nc.vector.tensor_tensor(t, r, r, ALU.mult))
            link(dve, nc.vector.tensor_tensor(t, t, var, ALU.mult))
        dve_in = var if turn == 0 else t
        out = r if turn == 0 else r2
        link(dve, nc.vector.tensor_scalar(v, dve_in, LN_EPS, None, ALU.add))
        nc.vector.tensor_copy(out, v).then_inc(s_var, 1)
        dve.wait_ge(s_guess, turn + 1)
        link(dve, nc.vector.tensor_tensor(t, out, out, ALU.mult))
        link(dve, nc.vector.tensor_tensor(t, t, v, ALU.mult))
        link(dve, nc.vector.tensor_scalar(t, t, -0.5, 1.5, ALU.mult, ALU.add))
        link(dve, nc.vector.tensor_tensor(out, out, t, ALU.mult))
    link(dve, nc.vector.scalar_tensor_tensor(out=nm, in0=mean, scalar=-1.0, in1=r, op0=ALU.mult, op1=ALU.mult))
    if twice:
        link(dve, nc.vector.tensor_tensor(r2, r2, r, ALU.mult))
        link(dve, nc.vector.scalar_tensor_tensor(out=nm2, in0=mean, scalar=-1.0, in1=r2, op0=ALU.mult, op1=ALU.mult))


def norm_factors_act(nc, act, c, s_var, s_log, s_guess, twice):
    for turn in range(2 if twice else 1):
        out = c.rstd[:, 2 * turn, :]
        act.wait_ge(s_var, turn + 1)
        nc.scalar.activation(out, out, ACT.Ln).then_inc(s_log, 1)
        act.wait_ge(s_log, turn + 1)
        nc.scalar.activation(out, out, ACT.Exp, scale=-0.5).then_inc(s_guess, 1)


def factor(c, i, g, j):
    return c.rstd[:, i, bass.ds(g * TPG + j, 1)]



def tokenize(nc, c, patches, w_tok, w97, rows, cols, rowp):
    with Semaphores(nc) as pool, ExitStack() as ctx:
        def sb(name, shape, dt=F32):
            return ctx.enter_context(nc.sbuf_tensor(name, shape, dt))

        def sem(name):
            return pool.new(name)

        NB = 2
        xin = sb("xin", [P, NB, PKC * GT])
        xr = sb("xr", [P, NB, PKC * GT])
        xq = sb("xq", [P, NB, PKC * GT], BF16)
        wt = sb("wt", [P, PKC * D])
        wq = sb("wq", [P, PKC * D], BF16)
        sc = sb("sc", [P, 4])
        acc = ctx.enter_context(nc.psum_tensor("acc", [P, TPG, 512], F32))
        s_small, s_wt, s_rest, s_bigcols = sem("s_small"), sem("s_wt"), sem("s_rest"), sem("s_bigcols")
        s_x = [sem(f"s_x{b}") for b in range(NB)]
        s_dve, s_scale, s_wq = sem("s_dve0"), sem("s_scale"), sem("s_wq")
        s_rounded, s_quant, s_acc, s_tok = sem("s_rounded"), sem("s_quant"), sem("s_acc"), sem("s_tok")
        s_const, s_masks = sem("s_const"), sem("s_masks")
        block = ctx.enter_context(nc.Block())

        @block.sync
        def _(sp):
            sp.dma_start(c.rows[:, :], rows[0:1, :].broadcast_to([P, ROWS_N])).then_inc(s_small, 16)
            sp.dma_start(wt[:, :], w_tok).then_inc(s_wt, 16)
            for b in range(NB):
                sp.dma_start(xin[:, b, :], patches[b]).then_inc(s_x[b], 16)
            with sp.Fori(0, GROUPS // NB - 1) as i:
                for b in range(NB):
                    sp.wait_ge(s_rounded, i * NB + b + 1)
                    sp.dma_start(xin[:, b, :], patches[i * NB + (b + NB)]).then_inc(s_x[b], 16)
            sp.dma_start(c.w[:, :, :], w97).then_inc(s_rest, 16)
            sp.dma_start(c.cols[:, :], cols).then_inc(s_rest, 16)
            sp.dma_start(c.rowp[:, :], rowp).then_inc(s_rest, 16)
            sp.wait_ge(s_rest, 48)

        @block.gpsimd
        def _(gp):
            nc.gpsimd.memset(c.ones[:, :], 1.0).then_inc(s_const, 1)
            for i in range(2):
                for k in range(2):
                    gp.wait_ge(s_const, i * 2 + k + 1)
                    nc.gpsimd.memset(c.same[i * SEQ:(i + 1) * SEQ, k * SEQ:(k + 1) * SEQ],
                                     float(i == k)).then_inc(s_const, 1)
            gp.wait_ge(s_const, 5)
            nc.gpsimd.affine_select(out=c.ident[:, :], in_=c.ones[:, :], compare_op=ALU.is_equal, fill=0.0,
                                    base=0, pattern=[[-1, P]], channel_multiplier=1).then_inc(s_masks, 1)
            nc.gpsimd.affine_select(out=c.lower[:, :], in_=c.same[:, :], compare_op=ALU.is_gt, fill=0.0,
                                    base=0, pattern=[[-1, P]], channel_multiplier=1).then_inc(s_masks, 1)
            gp.wait_ge(s_masks, 2)

        @block.scalar
        def _(act):
            nc.scalar.preload_act_table_set(LOG_EXP)
            act.wait_ge(s_scale, 1)
            with act.Fori(0, GROUPS // NB) as i:
                for b in range(NB):
                    act.wait_ge(s_x[b], i * 16 + 16)
                    act.wait_ge(s_quant, i * NB + b + 1)
                    nc.scalar.activation(xr[:, b, :], xin[:, b, :], ACT.Copy, bias=ROUND,
                                         scale=sc[:, 1:2]).then_inc(s_rounded, 1)

        @block.vector
        def _(dve):
            cnt = Count(s_dve)
            dve.wait_ge(s_small, 16)
            a = ROWS_AT["alpha_w"][0]
            nc.vector.reciprocal(sc[:, 0:2], c.rows[:, a:a + 2]).then_inc(s_scale, 1)
            cnt.link(dve, nc.vector.tensor_tensor(sc[:, 2:3], c.rows[:, a:a + 1], c.rows[:, a + 1:a + 2], ALU.mult))
            dve.wait_ge(s_scale, 1)
            dve.wait_ge(s_wt, 16)
            cnt.link(dve, nc.vector.tensor_scalar(wt[:, :], wt[:, :], sc[:, 0:1], ROUND, ALU.mult, ALU.add))
            cnt.link(dve, nc.vector.tensor_scalar(wt[:, :], wt[:, :], ROUND - 128, ROUND + 127, ALU.max, ALU.min))
            nc.vector.tensor_scalar(wq[:, :], wt[:, :], ROUND, None, ALU.subtract).then_inc(s_wq, 1)
            dve.sem_inc(s_quant, NB)
            with dve.Fori(0, GROUPS // NB) as i:
                for b in range(NB):
                    dve.wait_ge(s_rounded, i * NB + b + 1)
                    own = Count(s_dve, i * NB + b + 3)
                    own.link(dve, nc.vector.tensor_scalar(xr[:, b, :], xr[:, b, :], ROUND - 128, ROUND + 127,
                                                          ALU.max, ALU.min))
                    nc.vector.tensor_scalar(xq[:, b, :], xr[:, b, :], ROUND, None, ALU.subtract).then_inc(s_quant, 1)
                    for j in range(TPG):
                        dve.wait_ge(s_acc, (i * NB + b) * TPG + j + 1)
                        tile = c.h[:, bass.ds((i * NB + b) * TPG + j, 1), :].rearrange("p a d -> p (a d)")
                        nc.vector.scalar_tensor_tensor(out=tile, in0=acc[:, j, 0:D], scalar=sc[:, 2:3],
                                                       in1=c.rows[:, 0:D], op0=ALU.mult, op1=ALU.add).then_inc(s_tok, 1)

        @block.tensor
        def _(pe):
            pe.wait_ge(s_wq, 1)
            with pe.Fori(0, GROUPS // NB) as i:
                for b in range(NB):
                    pe.wait_ge(s_quant, (i * NB + b) + NB + 1)
                    for j in range(TPG):
                        if b == 1:
                            pe.wait_ge(s_tok, (i * NB) * TPG + j + 1)
                        for k in range(PKC):
                            mm = nc.tensor.matmul(acc[:, j, 0:D], xq[:, b, k * GT + j * P:k * GT + (j + 1) * P],
                                                  wq[:, k * D:(k + 1) * D], start=(k == 0), stop=(k == PKC - 1))
                        mm.then_inc(s_acc, 1)
                pe.wait_ge(s_tok, (i + 1) * (NB * TPG))



def performer(nc, c, proj, scratch):
    with Semaphores(nc) as pool, ExitStack() as ctx:
        def sb(name, shape, dt=F32):
            return ctx.enter_context(nc.sbuf_tensor(name, shape, dt))

        def sem(name):
            return pool.new("p_" + name)

        N17 = DH + 1
        projn = sb("projn", [DC, 3, 2 * FEATURES])
        qk_all = sb("qk_all", [DC, 4, TOKENS])
        va_all = sb("va_all", [P, TILES, HEADS * N17])
        diag = sb("diag", [P, TILES, 2, HEADS])
        room = c.x1[:, :, :].rearrange("p t d -> p (t d)")
        n = room[:, 0:2 * TPG * D].rearrange("p (b j d) -> p b j d", b=2, d=D)
        xT = room[0:DC + 1, 2 * TPG * D:2 * TPG * D + 4 * GT].rearrange("p (b c t) -> p b c t", b=2, c=2)
        sq = room[0:DC, 2 * TPG * D + 4 * GT:2 * TPG * D + 8 * GT].rearrange("p (i t) -> p i t", i=4)
        feat = room.rearrange("p (b k h m) -> p b k h m", b=2, k=2, m=FEATURES)
        qk = sb("qk", [DC, 2, 4, P])
        va = sb("va", [P, 2, 2, HEADS * N17])
        qT = sb("qT", [P, HEADS, P])
        kvs = sb("kvs", [P, 2, 2, HEADS * N17])
        epsv = c.rstd[:, 2:6, :].rearrange("p a t -> p (a t)")
        small = c.mv[:, :, :].rearrange("p a t -> p (a t)")
        mx, den = small[:, 0:2 * HEADS].rearrange("p (k h) -> p k h", k=2), small[:, 2 * HEADS:3 * HEADS]
        att = [c.st[:, :, :].rearrange("p t s -> p (t s)").rearrange("p (h d) -> p h d", d=DH), sb("att", [P, HEADS, DH])[:, :, :]]
        banks = ctx.enter_context(nc.psum_tensor("banks", [P, 8, 512], F32))
        T, Q, V = banks[:, 0:2], banks[:, 2:6], banks[:, 6:8]
        sets, KV = [banks[:, 0:3], banks[:, 3:6]], banks[:, 6, 0:2 * HEADS * N17].rearrange("p (i e) -> p i e", i=2)
        num_ps = banks[:, 7, 0:HEADS * N17]

        num_he = num_ps.rearrange("p (h e) -> p h e", e=N17)

        def diag_ps(b):
            return V[:, b, 2 * D:2 * D + 4 * HEADS]

        s_ld, s_dve, s_var, s_log, s_guess = [sem(x) for x in ("ld", "dve", "var", "log", "guess")]
        s_n, s_T, s_xT, s_q, s_qs, s_sq, s_v, s_va, s_ready = [sem(x) for x in ("n", "T", "xT", "q", "qs", "sq", "v", "va", "ready")]
        s_lq, s_lv = [sem("lq0"), sem("lq1")], [sem("lv0"), sem("lv1")]
        s_dd, s_sub, s_exp = ([sem(x + "q"), sem(x + "k")] for x in ("dd", "sub", "exp"))
        s_kv, s_kvs, s_tr, s_qT, s_num, s_att = [sem(x) for x in ("kv", "kvs", "tr", "qT", "num", "att")]
        s_out = [sem("out0"), sem("out1")]
        block = ctx.enter_context(nc.Block())
        Q_, K_ = 0, 1

        def steps(eng, step):
            for t in range(4):
                step(t, t % 2)
            with eng.Fori(2, TILES // 2) as i:
                for p in range(2):
                    step(i * 2 + p, p)
            for t in range(TILES, TILES + 2):
                step(t, t % 2)

        def inner(t):
            return not isinstance(t, int)

        @block.sync
        def _(sp):
            sp.dma_start(projn[:, :, :], proj).then_inc(s_ld, 16)
            for b in range(2):
                sp.sem_inc(s_out[b], 32)
            sp.wait_ge(s_ready, 2)

            def load(t, p):
                sp.dma_start(qk[:, p], qk_all[:, :, bass.ds(t * P, P)]).then_inc(s_lq[p], 16)
                for i in range(2):
                    rows = slice(i * SEQ, (i + 1) * SEQ)
                    sp.dma_start(va[rows, p, i], va_all[rows, bass.ds(t, 1), :].rearrange("p a e -> p (a e)")
                                 ).then_inc(s_lv[p], 16)

            for p in range(2):
                load(p, p)

            def store(t, p):
                sp.wait_ge(s_att, t + 1)
                for i in range(2):
                    sp.dma_start(scratch[bass.ds(t * 2 + i, 1)].rearrange("a h l d -> l (a h) d"),
                                 att[p][i * SEQ:(i + 1) * SEQ]).then_inc(s_out[p], 16)

            for p in range(2):
                sp.wait_ge(s_kv, p + 1)
                load(p + 2, p)
            with sp.Fori(1, TILES // 2 - 1) as i:
                for p in range(2):
                    t = i * 2 + p
                    sp.wait_ge(s_kv, t + 1)
                    load(t + 2, p)
                    store(t - 2, p)
            for t in range(TILES - 4, TILES):
                store(t, t % 2)
            for b in range(2):
                sp.wait_ge(s_out[b], TILES // 2 * 32 + 32)

        @block.vector
        def _(dve):
            own = Count(s_dve)
            token_stats(nc, dve, c, own.link, c.h)
            norm_factors_dve(nc, dve, c, own.link, s_var, s_guess, twice=False)
            own.link(dve, nc.vector.memset(epsv, FEATURE_EPS))
            own.link(dve, nc.vector.memset(va[:, :, :, :], 0.0))
            own.link(dve, nc.vector.memset(va_all[:, :, :].rearrange("p t (h e) -> p (t h) e", e=N17)[:, :, DH:N17], 1.0))
            own.link(dve, nc.vector.memset(xT[DC:DC + 1, :, 0, :], 1.0))
            dve.wait_ge(s_ld, 16)
            own.link(dve, nc.vector.tensor_scalar(projn[:, :, :], projn[:, :, :], float(DH) ** -0.25, None, ALU.mult))
            done = own.n

            def rows(g, b):
                for j in range(TPG):
                    nc.vector.tensor_scalar(n[:, b, j, :], tile_view(c.h, g, j), factor(c, 0, g, j), factor(c, 1, g, j),
                                            ALU.mult, ALU.add).then_inc(s_n, 1)

            def group(g, b, last=False):
                if not last:
                    rows(g + 1, 1 - b)
                for i in range(4):
                    dve.wait_ge(s_q, g * 4 + i + 1)
                    nc.vector.tensor_scalar(qk_all[:, i, bass.ds(g * GT, GT)], Q[0:DC, i, :], 1.0, None,
                                            ALU.mult).then_inc(s_qs, 1)
                for a in range(2):
                    dve.wait_ge(s_v, g * 2 + a + 1)
                    nc.vector.tensor_scalar(
                        va_all[:, bass.ds(g * TPG + 2 * a, 2), :].rearrange("p j (h e) -> p j h e", e=N17)[:, :, :, 0:DH],
                        V[:, a, 0:2 * D].rearrange("p (j h d) -> p j h d", j=2, d=DH), 1.0, None, ALU.mult).then_inc(s_va, 1)
                    nc.vector.tensor_scalar(diag[:, bass.ds(g * TPG + 2 * a, 2), :, :].rearrange("p j k h -> p (j k h)"),
                                            diag_ps(a), 1.0, None, ALU.mult).then_inc(s_va, 1)

            rows(0, 0)
            with dve.Fori(0, GROUPS // 2 - 1) as i:
                for b in range(2):
                    group(i * 2 + b, b)
            group(GROUPS - 2, 0)
            group(GROUPS - 1, 1, last=True)
            dve.wait_ge(s_va, GROUPS * 4)
            dve.wait_ge(s_qs, GROUPS * 4)
            dve.wait_ge(s_sq, GROUPS * 4)
            dve.sem_inc(s_ready, 2)

            def features(t, p, kind, own):
                dve.wait_ge(s_dd[kind], t + 1)
                s = sets[(p + 1 - kind) % 2]
                own.link(dve, nc.vector.tensor_reduce(mx[:, kind, :].rearrange("p (b s) -> p b s", b=3),
                                                      s.rearrange("p b (s m) -> p b s m", s=4), AX.X, ALU.max))
                own.link(dve, nc.vector.tensor_tensor(mx[:, kind, :], mx[:, kind, :],
                                                      diag[:, bass.ds(t, 1), kind, :].rearrange("p a h -> p (a h)"), ALU.add))
                nc.vector.tensor_tensor(feat[:, p, kind].rearrange("p (b s) m -> p b s m", b=3),
                                        s.rearrange("p b (s m) -> p b s m", s=4),
                                        mx[:, kind, :].rearrange("p (b s o) -> p b s o", b=3, o=1).broadcast_to([P, 3, 4, FEATURES]),
                                        ALU.subtract).then_inc(s_sub[kind], 1)

            def step(t, p):
                base = done + (t * 5 - 2 if inner(t) or t >= 2 else t * 4)
                own = Count(s_dve, base)
                if inner(t) or t < TILES:
                    features(t, p, K_, own)
                    features(t, p, Q_, own)
                else:
                    own = Count(s_dve, done + TILES * 5 - 2 + (t - TILES))
                if inner(t) or t >= 2:
                    dve.wait_ge(s_num, t - 1)
                    own.link(dve, nc.vector.reciprocal(den, num_he[:, :, DH]))
                    dve.wait_ge(s_out[p], (t - p) * 16)
                    nc.vector.tensor_tensor(att[p], num_he[:, :, 0:DH],
                                            den.rearrange("p (h o) -> p h o", o=1).broadcast_to([P, HEADS, DH]),
                                            ALU.mult).then_inc(s_att, 1)

            steps(dve, step)

        @block.scalar
        def _(act):
            nc.scalar.preload_act_table_set(LOG_EXP)
            norm_factors_act(nc, act, c, s_var, s_log, s_guess, twice=False)

            def turned(g, b):
                for cc in range(2):
                    act.wait_ge(s_T, g * 2 + cc + 1)
                    nc.scalar.activation(xT[0:DC, b, cc, :], T[0:DC, cc, :], ACT.Copy).then_inc(s_xT, 1)

            def group(g, b, last=False):
                if inner(g) or g > 0:
                    act.wait_ge(s_v, g * 2)
                for i in range(4):
                    act.wait_ge(s_qs, g * 4 + i + 1)
                    nc.scalar.activation(sq[:, i, :], Q[0:DC, i, :], ACT.Square).then_inc(s_sq, 1)
                    if i == 2 and not last:
                        turned(g + 1, 1 - b)

            turned(0, 0)
            with act.Fori(0, GROUPS // 2 - 1) as i:
                for b in range(2):
                    group(i * 2 + b, b)
            group(GROUPS - 2, 0)
            group(GROUPS - 1, 1, last=True)

            def step(t, p):
                if inner(t) or 1 <= t <= TILES:
                    act.wait_ge(s_kv, t)
                    nc.scalar.activation(kvs[:, 1 - p], KV,
                                         ACT.Copy).then_inc(s_kvs, 1)
                if inner(t) or t < TILES:
                    act.wait_ge(s_sub[K_], t + 1)
                    e = feat[:, p, K_].rearrange("p h m -> p (h m)")
                    nc.scalar.activation(e, e, ACT.Exp).then_inc(s_exp[K_], 1)
                if inner(t) or 1 <= t <= TILES:
                    act.wait_ge(s_tr, t)
                    if inner(t) or t >= 2:
                        act.wait_ge(s_num, t - 1)
                    nc.scalar.activation(qT[:, :, :].rearrange("p (b s) m -> p b (s m)", b=3), sets[p],
                                         ACT.Copy, bias=FEATURE_EPS).then_inc(s_qT, 1)
                if inner(t) or t < TILES:
                    act.wait_ge(s_sub[Q_], t + 1)
                    e = feat[:, p, Q_].rearrange("p h m -> p (h m)")
                    nc.scalar.activation(e, e, ACT.Exp).then_inc(s_exp[Q_], 1)

            steps(act, step)

        @block.tensor
        def _(pe):
            wq, wk, wv = weight(c, "pq"), weight(c, "pk"), weight(c, "pv")
            blk = col(c, "headsum")[0:DC, :]

            def turn(g, b):
                pe.wait_ge(s_n, (g + 1) * TPG)
                for cc in range(2):
                    for j in range(TPG):
                        mm = nc.tensor.transpose(T[0:DC, cc, j * P:(j + 1) * P], n[:, b, j, cc * DC:(cc + 1) * DC], c.ident[:, :])
                    mm.then_inc(s_T, 1)

            def group(g, b, last=False):
                pe.wait_ge(s_xT, g * 2 + 2)
                if inner(g) or g > 0:
                    pe.wait_ge(s_sq, g * 4)
                for i in range(4):
                    w = (wq if i < 2 else wk)[:, :, (i % 2) * DC:(i % 2 + 1) * DC]
                    nc.tensor.matmul(Q[0:DC, i, :], w[:, 0, :], xT[:, b, 0, :], start=True, stop=False)
                    nc.tensor.matmul(Q[0:DC, i, :], w[0:DC, 1, :], xT[0:DC, b, 1, :], start=False, stop=True).then_inc(s_q, 1)
                if not last:
                    turn(g + 1, 1 - b)
                if inner(g) or g > 0:
                    pe.wait_ge(s_va, g * 4)
                pe.wait_ge(s_sq, g * 4 + 4)
                for a in range(2):
                    for jj in range(2):
                        j = 2 * a + jj
                        o = V[:, a, jj * D:(jj + 1) * D]
                        nc.tensor.matmul(o, xT[:, b, 0, j * P:(j + 1) * P], wv[:, 0, :], start=True, stop=False)
                        mm = nc.tensor.matmul(o, xT[0:DC, b, 1, j * P:(j + 1) * P], wv[0:DC, 1, :], start=False, stop=True)
                    for jj in range(2):
                        j = 2 * a + jj
                        for kind in range(2):
                            for cc in range(2):
                                at = (jj * 2 + kind) * HEADS
                                o = diag_ps(a)[:, at:at + HEADS].rearrange("p (b c r) -> p b c r", b=3, c=2)[:, :, cc, :]
                                mm = nc.tensor.matmul(o, sq[:, 2 * kind + cc, j * P:(j + 1) * P], blk, start=True, stop=True)
                    mm.then_inc(s_v, 1)

            turn(0, 0)
            with pe.Fori(0, GROUPS // 2 - 1) as i:
                for b in range(2):
                    group(i * 2 + b, b)
            group(GROUPS - 2, 0)
            group(GROUPS - 1, 1, last=True)
            pe.wait_ge(s_ready, 2)

            def products(t, p, kind, b):
                for cc in range(2):
                    mm = nc.tensor.matmul(sets[(p + 1 - kind) % 2][:, b, cc * 256:cc * 256 + 256],
                                          qk[:, p, 2 * kind + cc, :], projn[:, b, :], start=True, stop=True)
                if b == 2:
                    mm.then_inc(s_dd[kind], 1)

            def step(t, p):
                enters, second, third = inner(t) or t < TILES, inner(t) or 1 <= t <= TILES, inner(t) or t >= 2
                if enters:
                    pe.wait_ge(s_lq[p], (t - p) * 8 + 16)
                    if inner(t) or t >= 1:
                        pe.wait_ge(s_sub[Q_], t)
                    for b in range(3):
                        products(t, p, K_, b)
                if third:
                    pe.wait_ge(s_qT, t - 1)
                for b in range(3):
                    if enters:
                        products(t, p, Q_, b)
                    if second:
                        if b == 0:
                            pe.wait_ge(s_exp[K_], t)
                            pe.wait_ge(s_lv[1 - p], (t - 1 - (1 - p)) * 16 + 32)
                            if inner(t) or t >= 2:
                                pe.wait_ge(s_kvs, t - 1)
                            nc.tensor.matmul(KV, epsv, va[:, 1 - p], start=True, stop=False, skip_group_check=True)
                        for h in range(4 * b, 4 * b + 4):
                            e = slice(h * N17, (h + 1) * N17)
                            mm = nc.tensor.matmul(KV[:, :, e], feat[:, 1 - p, K_, h, :], va[:, 1 - p, :, e], start=False,
                                                  stop=(h == HEADS - 1), skip_group_check=True)
                        if b == 2:
                            mm.then_inc(s_kv, 1)
                if second:
                    if enters:
                        pe.wait_ge(s_sub[K_], t + 1)
                    pe.wait_ge(s_exp[Q_], t)
                if third:
                    pe.wait_ge(s_kvs, t - 1)
                    if inner(t) or t >= 3:
                        pe.wait_ge(s_att, t - 2)
                for h in range(HEADS):
                    if third:
                        for i in range(2):
                            mm = nc.tensor.matmul(num_ps[i * SEQ:(i + 1) * SEQ, h * N17:(h + 1) * N17],
                                                  qT[:, h, i * SEQ:(i + 1) * SEQ],
                                                  kvs[:, p, i, h * N17:(h + 1) * N17], start=True, stop=True)
                        if h == HEADS - 1:
                            mm.then_inc(s_num, 1)
                    if second:
                        mm = nc.tensor.transpose(sets[p][:, h // 4, (h % 4) * P:(h % 4 + 1) * P], feat[:, 1 - p, Q_, h, :],
                                                 c.ident[:, :])
                        if h == HEADS - 1:
                            mm.then_inc(s_tr, 1)

            steps(pe, step)


def performer_out(nc, c, scratch):
    with Semaphores(nc) as pool, ExitStack() as ctx:
        def sb(name, shape, dt=F32):
            return ctx.enter_context(nc.sbuf_tensor(name, shape, dt))

        def sem(name):
            return pool.new(name)

        NB = 2
        cat = sb("cat", [P, NB, TPG, D])
        xT = sb("cT", [DC + 1, 2, 2, GT])
        tp = ctx.enter_context(nc.psum_tensor("tp", [P, NB, 2, 512], F32))
        op = ctx.enter_context(nc.psum_tensor("op", [P, NB, 2, 512], F32))
        s_in = [sem("o_in0"), sem("o_in1")]
        s_dve, s_T, s_xT0, s_xT1, s_o, s_h, s_one = [sem(f"o_{x}") for x in ("dve", "T", "xT0", "xT1", "o", "h", "one")]
        block = ctx.enter_context(nc.Block())
        rows = scratch.rearrange("(t i) h l d -> t (i h l d)", i=2).rearrange("t (p e) -> p t e", e=D)

        @block.sync
        def _(sp):
            sp.sem_inc(s_T, NB * 2)
            with sp.Fori(0, GROUPS // NB) as i:
                for b in range(NB):
                    sp.wait_ge(s_T, (i * NB + b) * 2 + 2)
                    sp.dma_start(cat[:, b], rows[:, bass.ds((i * NB + b) * TPG, TPG), :]).then_inc(s_in[b], 16)

        @block.tensor
        def _(pe):
            wo = weight(c, "po")
            pe.wait_ge(s_one, 1)
            with pe.Fori(0, GROUPS // NB) as i:
                for b in range(NB):
                    g = i * NB + b
                    pe.wait_ge(s_in[b], i * 16 + 16)
                    for cc in range(2):
                        for j in range(TPG):
                            mm = nc.tensor.transpose(tp[0:DC, b, cc, j * P:(j + 1) * P], cat[:, b, j, cc * DC:(cc + 1) * DC],
                                                     c.ident[:, :])
                        mm.then_inc(s_T, 1)
                    pe.wait_ge(s_xT0, g + 1)
                    pe.wait_ge(s_xT1, g + 1)
                    pe.wait_ge(s_h, g * 2 + 2)
                    for j in range(TPG):
                        o = op[:, b, j // 2, (j % 2) * D:(j % 2 + 1) * D]
                        nc.tensor.matmul(o, xT[:, b, 0, j * P:(j + 1) * P], wo[:, 0, :], start=True, stop=False)
                        mm = nc.tensor.matmul(o, xT[0:DC, b, 1, j * P:(j + 1) * P], wo[0:DC, 1, :], start=False, stop=True)
                        if j % 2:
                            mm.then_inc(s_o, 1)

        @block.scalar
        def _(act):
            act.wait_ge(s_one, 1)
            with act.Fori(0, GROUPS // NB) as i:
                for b in range(NB):
                    act.wait_ge(s_T, (i * NB + b) * 2 + NB * 2 + 1)
                    nc.scalar.activation(xT[0:DC, b, 0, :], tp[0:DC, b, 0, :], ACT.Copy).then_inc(s_xT0, 1)

        @block.vector
        def _(dve):
            nc.vector.memset(xT[DC:DC + 1, :, 0, :], 1.0).then_inc(s_one, 1)
            dve.sem_inc(s_h, 2 * NB)
            with dve.Fori(0, GROUPS // NB) as i:
                for b in range(NB):
                    g = i * NB + b
                    dve.wait_ge(s_T, g * 2 + NB * 2 + 2)
                    nc.vector.tensor_scalar(xT[0:DC, b, 1, :], tp[0:DC, b, 1, :], 1.0, None, ALU.mult).then_inc(s_xT1, 1)
                    for j in range(TPG):
                        if j % 2 == 0:
                            dve.wait_ge(s_o, g * 2 + j // 2 + 1)
                        ins = nc.vector.tensor_tensor(tile_view(c.h, g, j), op[:, b, j // 2, (j % 2) * D:(j % 2 + 1) * D],
                                                      tile_view(c.h, g, j), ALU.add)
                        if j % 2:
                            ins.then_inc(s_h, 1)



def attention(nc, c, names, gain, shift, mixing):
    wq, wk, wv, wo = (weight(c, x) for x in names)
    wm = weight(c, "mm")
    VW = D + 1 if mixing else D
    tag = "m" if mixing else "a"
    with Semaphores(nc) as pool, ExitStack() as ctx:
        def sb(name, shape, dt=F32):
            return ctx.enter_context(nc.sbuf_tensor(tag + "_" + name, shape, dt))

        def sem(name):
            return pool.new(tag + "_" + name)

        def ps(name, shape):
            return ctx.enter_context(nc.psum_tensor(tag + "_" + name, shape, F32))

        N17 = DH + 1
        n = sb("n", [P, TPG, D])
        n1 = sb("n1", [P, TPG, D])
        xT = sb("xT", [DC + 1, 2, GT])
        qT = sb("qT", [DC, 2, GT])
        kT = sb("kT", [DC, 2, 2, GT])
        va = sb("va", [P, TPG, HEADS, N17])
        mx = sb("mx", [P, HEADS])
        sc = sb("sc", [P, 2, HEADS, SEQ])
        prob = sb("prob", [P, 2, HEADS, P])
        pT = sb("pT", [P, HEADS, P])
        den = sb("den", [P, HEADS])
        ao = sb("ao", [P, TPG, HEADS, DH])
        aT = sb("aT", [DC + 1, 2, GT])
        S, T, F = ps("S", [P, 3, 512]), ps("T", [P, 3, 512]), ps("F", [P, 2, 512])
        if mixing:
            es, score, share, ssum = (sb(x, [P, TPG]) for x in ("es", "score", "share", "ssum"))
            sel, nsel, rank = (sb(x, [P, TPG]) for x in ("sel", "nsel", "rank"))
            pm = sb("pm", [P, TPG, D])
            spread, sT, mixer, before = (sb(x, [P, TPG, P]) for x in ("spread", "sT", "mixer", "before"))
            mixed = sb("mixed", [P, TPG, D])
        s_dve, s_var, s_log, s_guess = [sem(x) for x in ("dve", "var", "log", "guess")]
        s_n, s_T, s_xT, s_q, s_qT, s_kTa, s_kTd, s_v, s_va = [sem(x) for x in ("n", "T", "xT", "q", "qT", "kTa", "kTd", "v", "va")]
        s_S, s_sub, s_exp, s_tr, s_pTa, s_pTd, s_o, s_ao = [sem(x) for x in ("S", "sub", "exp", "tr", "pTa", "pTd", "o", "ao")]
        s_at, s_aTa, s_aTd, s_out, s_h = [sem(x) for x in ("at", "aTa", "aTd", "out", "h")]
        s_pm, s_pms, s_es, s_score, s_tot, s_share, s_sT, s_mixer, s_mix = [
            sem(x) for x in ("pm", "pms", "es", "score", "tot", "share", "sT", "mixer", "mix")]
        block = ctx.enter_context(nc.Block())
        bank = [S[0:DC, 0, :], S[0:DC, 1, :], S[0:DC, 2, :], T[0:DC, 0, :]]

        def o_ps(j):
            return F[:, j % 2, 0:HEADS * N17].rearrange("p (h e) -> p h e", e=N17)

        @block.vector
        def _(dve):
            own = Count(s_dve)
            token_stats(nc, dve, c, own.link, c.h)
            norm_factors_dve(nc, dve, c, own.link, s_var, s_guess, twice=True)
            own.link(dve, nc.vector.memset(va[:, :, :, DH:N17], 1.0))
            own.link(dve, nc.vector.memset(xT[DC:DC + 1, 0, :], 1.0))
            own.link(dve, nc.vector.memset(aT[DC:DC + 1, 0, :], 1.0))
            own.link(dve, nc.vector.memset(prob[:, :, :, :], 0.0))
            done = own.n

            def scores(g, own, j):
                view = S[:, :, 0:4 * SEQ].rearrange("p b (s k) -> p b s k", s=4)
                dve.wait_ge(s_S, g * TPG + j + 1)
                own.link(dve, nc.vector.tensor_reduce(mx[:, :].rearrange("p (b s) -> p b s", b=3), view, AX.X, ALU.max))
                nc.vector.tensor_tensor(sc[:, j % 2].rearrange("p (b s) k -> p b s k", b=3), view,
                                        mx[:, :].rearrange("p (b s o) -> p b s o", b=3, o=1).broadcast_to([P, 3, 4, SEQ]),
                                        ALU.subtract).then_inc(s_sub, 1)

            def divide(g, own, j):
                dve.wait_ge(s_o, g * TPG + j + 1)
                own.link(dve, nc.vector.reciprocal(den[:, :], o_ps(j)[:, :, DH]))
                nc.vector.tensor_tensor(ao[:, j], o_ps(j)[:, :, 0:DH],
                                        den[:, :].rearrange("p (h o) -> p h o", o=1).broadcast_to([P, HEADS, DH]),
                                        ALU.mult).then_inc(s_ao, 1)

            def turned(g, own, j):
                dve.wait_ge(s_tr, g * TPG + j + 1)
                nc.vector.tensor_scalar(pT[:, 8:12, :].rearrange("p h m -> p (h m)"), T[:, 2, :], 1.0, None,
                                        ALU.mult).then_inc(s_pTd, 1)

            def routing(g, own):
                for b in range(2):
                    dve.wait_ge(s_pm, g * 2 + b + 1)
                    nc.vector.tensor_scalar(pm[:, 2 * b:2 * b + 2, :].rearrange("p a d -> p (a d)"), F[:, b, 0:2 * D], 1.0,
                                            None, ALU.mult).then_inc(s_pms, 1)
                dve.wait_ge(s_es, g * 2 + 2)
                own.link(dve, nc.vector.tensor_scalar(score[:, :], es[:, :], 1.0, None, ALU.add))
                own.link(dve, nc.vector.reciprocal(score[:, :], score[:, :]))
                for j in range(TPG):
                    own.link(dve, nc.vector.tensor_scalar(spread[:, j, :], c.ones[:, :], score[:, j:j + 1], None, ALU.mult))
                dve.sem_inc(s_score, 1)
                dve.wait_ge(s_tot, g + 1)
                own.link(dve, nc.vector.tensor_scalar(ssum[:, :], F[:, 0, 0:TPG], POOL_EPS, None, ALU.add))
                own.link(dve, nc.vector.reciprocal(ssum[:, :], ssum[:, :]))
                own.link(dve, nc.vector.tensor_tensor(share[:, :], score[:, :], ssum[:, :], ALU.mult))
                own.link(dve, nc.vector.tensor_scalar(sT[:, :, :].rearrange("p j k -> p (j k)"), F[:, 1, :], 1.0, None,
                                                      ALU.mult))
                dve.sem_inc(s_share, 1)
                for j in range(TPG):
                    one = score[:, j:j + 1]
                    own.link(dve, nc.vector.scalar_tensor_tensor(out=before[:, j, :], in0=sT[:, j, :], scalar=one,
                                                                 in1=c.same[:, :], op0=ALU.is_lt, op1=ALU.mult))
                    own.link(dve, nc.vector.scalar_tensor_tensor(out=spread[:, j, :], in0=sT[:, j, :], scalar=one,
                                                                 in1=c.lower[:, :], op0=ALU.is_equal, op1=ALU.mult))
                    own.link(dve, nc.vector.scalar_tensor_tensor(out=mixer[:, j, :], in0=sT[:, j, :], scalar=share[:, j:j + 1],
                                                                 in1=c.same[:, :], op0=ALU.mult, op1=ALU.mult))
                    own.link(dve, nc.vector.tensor_tensor(mixer[:, j, :], mixer[:, j, :], c.ident[:, :], ALU.add))
                own.link(dve, nc.vector.tensor_tensor(before[:, :, :], before[:, :, :], spread[:, :, :], ALU.add))
                own.link(dve, nc.vector.tensor_reduce(rank[:, :], before[:, :, :], AX.X, ALU.add))
                own.link(dve, nc.vector.tensor_scalar(sel[:, :], rank[:, :], ROUTED - 0.5, None, ALU.is_lt))
                own.link(dve, nc.vector.tensor_scalar(nsel[:, :], rank[:, :], ROUTED - 0.5, None, ALU.is_gt))
                dve.sem_inc(s_mixer, 1)

            per_group = TPG * 2 + TPG + (30 + 2 * TPG if mixing else 0)
            with dve.Fori(0, GROUPS) as g:
                own = Count(s_dve, g * per_group + done)
                for j in range(TPG):
                    nc.vector.tensor_scalar(n[:, j, :], tile_view(c.h, g, j), factor(c, 2, g, j), factor(c, 3, g, j),
                                            ALU.mult, ALU.add).then_inc(s_n, 1)
                for j in range(TPG):
                    own.link(dve, nc.vector.tensor_scalar(n1[:, j, :], tile_view(c.h, g, j), factor(c, 0, g, j),
                                                          factor(c, 1, g, j), ALU.mult, ALU.add))
                for j in range(TPG):
                    nc.vector.tensor_tensor(tile_view(c.h, g, j), n1[:, j, :], tile_view(c.h, g, j), ALU.add).then_inc(s_h, 1)
                dve.wait_ge(s_T, g * 2 + 2)
                nc.vector.tensor_scalar(xT[0:DC, 1, :], F[0:DC, 1, :], col(c, gain)[0:DC, 1:2], col(c, shift)[0:DC, 1:2],
                                        ALU.mult, ALU.add).then_inc(s_xT, 1)
                for i in range(2):
                    dve.wait_ge(s_q, g * 4 + i + 1)
                    nc.vector.tensor_scalar(qT[:, i, :], bank[i], 1.0, None, ALU.mult).then_inc(s_qT, 1)
                dve.wait_ge(s_q, g * 4 + 4)
                for r in range(2):
                    nc.vector.tensor_scalar(kT[:, 1, r, :], bank[3], col(c, "half")[0:DC, r:r + 1], None,
                                            ALU.mult).then_inc(s_kTd, 1)
                if mixing:
                    routing(g, own)
                for step in range(TPG + 2):
                    if step < TPG:
                        scores(g, own, step)
                    if step >= 2:
                        divide(g, own, step - 2)
                    if 1 <= step <= TPG:
                        turned(g, own, step - 1)
                dve.wait_ge(s_at, g * 2 + 2)
                nc.vector.tensor_scalar(aT[0:DC, 1, :], T[0:DC, 1, :], 1.0, None, ALU.mult).then_inc(s_aTd, 1)
                if mixing:
                    for j in range(TPG):
                        if j % 2 == 0:
                            dve.wait_ge(s_mix, g * 2 + j // 2 + 1)
                        own.link(dve, nc.vector.tensor_scalar(mixed[:, j, :], F[:, j // 2, (j % 2) * D:(j % 2 + 1) * D],
                                                              nsel[:, j:j + 1], None, ALU.mult))
                dve.wait_ge(s_h, g * (TPG * 3) + TPG)
                for j in range(TPG):
                    if j % 2 == 0:
                        dve.wait_ge(s_out, g * 2 + j // 2 + 1)
                    block_out = S[:, j // 2, (j % 2) * D:(j % 2 + 1) * D]
                    if mixing:
                        own.link(dve, nc.vector.scalar_tensor_tensor(out=mixed[:, j, :], in0=block_out, scalar=sel[:, j:j + 1],
                                                                     in1=mixed[:, j, :], op0=ALU.mult, op1=ALU.add))
                        block_out = mixed[:, j, :]
                    nc.vector.tensor_tensor(tile_view(c.x1, g, j), block_out, n1[:, j, :], ALU.add).then_inc(s_h, 1)
                    nc.vector.tensor_tensor(tile_view(c.h, g, j), block_out, tile_view(c.h, g, j), ALU.add).then_inc(s_h, 1)
                dve.wait_ge(s_h, (g + 1) * (TPG * 3))
                assert own.n == per_group, (own.n, per_group)

        @block.scalar
        def _(act):
            nc.scalar.preload_act_table_set(LOG_EXP)
            norm_factors_act(nc, act, c, s_var, s_log, s_guess, twice=True)
            with act.Fori(0, GROUPS) as g:
                act.wait_ge(s_T, g * 2 + 1)
                nc.scalar.activation(xT[0:DC, 0, :], F[0:DC, 0, :], ACT.Identity, scale=col(c, gain)[0:DC, 0:1],
                                     bias=col(c, shift)[0:DC, 0:1]).then_inc(s_xT, 1)
                act.wait_ge(s_q, g * 4 + 3)
                for r in range(2):
                    nc.scalar.activation(kT[:, 0, r, :], bank[2], ACT.Copy,
                                         scale=col(c, "half")[0:DC, r:r + 1]).then_inc(s_kTa, 1)
                for b in range(2):
                    act.wait_ge(s_v, g * 2 + b + 1)
                    src = T[:, 1 + b, 0:2 * VW].rearrange("p (a w) -> p a w", a=2)
                    if mixing:
                        nc.scalar.activation(es[:, 2 * b:2 * b + 2], src[:, :, D], ACT.Exp, scale=-1.0).then_inc(s_es, 1)
                    nc.scalar.activation(va[:, 2 * b:2 * b + 2, :, 0:DH],
                                         src[:, :, 0:D].rearrange("p a (h d) -> p a h d", d=DH), ACT.Copy).then_inc(s_va, 1)
                for step in range(TPG + 1):
                    if step < TPG:
                        act.wait_ge(s_sub, g * TPG + step + 1)
                        for i in range(2):
                            rows = slice(i * SEQ, (i + 1) * SEQ)
                            nc.scalar.activation(prob[rows, step % 2, :, rows], sc[rows, step % 2], ACT.Exp,
                                                 scale=float(DH) ** -0.5).then_inc(s_exp, 1)
                    if step >= 1:
                        act.wait_ge(s_tr, g * TPG + step)
                        nc.scalar.activation(pT[:, 0:8, :].rearrange("p (b s) m -> p b (s m)", b=2), T[:, 0:2, :],
                                             ACT.Copy).then_inc(s_pTa, 1)
                act.wait_ge(s_at, g * 2 + 1)
                nc.scalar.activation(aT[0:DC, 0, :], T[0:DC, 0, :], ACT.Copy).then_inc(s_aTa, 1)

        @block.tensor
        def _(pe):
            with pe.Fori(0, GROUPS) as g:
                pe.wait_ge(s_n, g * TPG + TPG)
                for cc in range(2):
                    for j in range(TPG):
                        mm = nc.tensor.transpose(F[0:DC, cc, j * P:(j + 1) * P], n[:, j, cc * DC:(cc + 1) * DC], c.ident[:, :])
                    mm.then_inc(s_T, 1)
                pe.wait_ge(s_xT, g * 2 + 2)
                for i in range(4):
                    w = (wq if i < 2 else wk)[:, :, (i % 2) * DC:(i % 2 + 1) * DC]
                    nc.tensor.matmul(bank[i], w[:, 0, :], xT[:, 0, :], start=True, stop=False)
                    nc.tensor.matmul(bank[i], w[0:DC, 1, :], xT[0:DC, 1, :], start=False, stop=True).then_inc(s_q, 1)
                for b in range(2):
                    for a in range(2):
                        j = 2 * b + a
                        o = T[:, 1 + b, a * VW:(a + 1) * VW]
                        nc.tensor.matmul(o, xT[:, 0, j * P:(j + 1) * P], wv[:, 0, :], start=True, stop=False)
                        mm = nc.tensor.matmul(o, xT[0:DC, 1, j * P:(j + 1) * P], wv[0:DC, 1, :], start=False, stop=True)
                    mm.then_inc(s_v, 1)
                if mixing:
                    for b in range(2):
                        for a in range(2):
                            j = 2 * b + a
                            o = F[:, b, a * D:(a + 1) * D]
                            nc.tensor.matmul(o, xT[0:DC, 0, j * P:(j + 1) * P], wm[0:DC, 0, :], start=True, stop=False)
                            mm = nc.tensor.matmul(o, xT[0:DC, 1, j * P:(j + 1) * P], wm[0:DC, 1, :], start=False, stop=True)
                        mm.then_inc(s_pm, 1)
                    pe.wait_ge(s_pms, g * 2 + 2)
                    pe.wait_ge(s_score, g + 1)
                    nc.tensor.matmul(F[:, 0, 0:TPG], c.same[:, :], score[:, :], start=True, stop=True)
                    for j in range(TPG):
                        mm = nc.tensor.transpose(F[:, 1, j * P:(j + 1) * P], spread[:, j, :], c.ident[:, :])
                    mm.then_inc(s_tot, 1)
                pe.wait_ge(s_qT, g * 2 + 2)
                pe.wait_ge(s_kTa, g * 2 + 2)
                pe.wait_ge(s_kTd, g * 2 + 2)
                for step in range(TPG + 2):
                    if step < TPG:
                        if step >= 1:
                            pe.wait_ge(s_sub, g * TPG + step)
                        for b in range(3):
                            rows = slice(32 * b, 32 * b + 32)
                            for cc in range(2):
                                for i in range(2):
                                    at = step * P + i * SEQ
                                    mm = nc.tensor.matmul(
                                        S[i * SEQ:(i + 1) * SEQ, b, cc * 2 * SEQ:(cc + 1) * 2 * SEQ].rearrange(
                                            "p (r k) -> p r k", r=2),
                                        qT[rows, cc, at:at + SEQ], kT[rows, cc, :, at:at + SEQ], start=True, stop=True)
                        mm.then_inc(s_S, 1)
                    if step >= 2:
                        j = step - 2
                        pe.wait_ge(s_pTa, g * TPG + j + 1)
                        pe.wait_ge(s_pTd, g * TPG + j + 1)
                        if j >= 2:
                            pe.wait_ge(s_ao, g * TPG + j - 1)
                        elif mixing:
                            pe.wait_ge(s_share, g + 1)
                        for h in range(HEADS):
                            mm = nc.tensor.matmul(o_ps(j)[:, h, :], pT[:, h, :], va[:, j, h, :], start=True, stop=True)
                        mm.then_inc(s_o, 1)
                    if 1 <= step <= TPG:
                        j = step - 1
                        if j == 0:
                            pe.wait_ge(s_va, g * 2 + 2)
                        pe.wait_ge(s_exp, (g * TPG + j) * 2 + 2)
                        for h in range(HEADS):
                            mm = nc.tensor.transpose(T[:, h // 4, (h % 4) * P:(h % 4 + 1) * P], prob[:, j % 2, h, :],
                                                     c.ident[:, :])
                        mm.then_inc(s_tr, 1)
                pe.wait_ge(s_ao, g * TPG + TPG)
                for cc in range(2):
                    for j in range(TPG):
                        mm = nc.tensor.transpose(T[0:DC, cc, j * P:(j + 1) * P],
                                                 ao[:, j].rearrange("p h d -> p (h d)")[:, cc * DC:(cc + 1) * DC], c.ident[:, :])
                    mm.then_inc(s_at, 1)
                if mixing:
                    pe.wait_ge(s_mixer, g + 1)
                    for j in range(TPG):
                        o = F[:, j // 2, (j % 2) * D:(j % 2 + 1) * D]
                        nc.tensor.matmul(o, mixer[:, j, :], pm[:, j, :], start=True, stop=False)
                        mm = nc.tensor.matmul(o, c.ones[0:1, :], c.rowp[0:1, ROWP_BM:ROWP_BM + D], start=False, stop=True)
                        if j % 2:
                            mm.then_inc(s_mix, 1)
                pe.wait_ge(s_aTa, g + 1)
                pe.wait_ge(s_aTd, g + 1)
                for j in range(TPG):
                    o = S[:, j // 2, (j % 2) * D:(j % 2 + 1) * D]
                    nc.tensor.matmul(o, aT[:, 0, j * P:(j + 1) * P], wo[:, 0, :], start=True, stop=False)
                    mm = nc.tensor.matmul(o, aT[0:DC, 1, j * P:(j + 1) * P], wo[0:DC, 1, :], start=False, stop=True)
                    if j % 2:
                        mm.then_inc(s_out, 1)
                pe.wait_ge(s_h, (g + 1) * (TPG * 3))



def experts(nc, c, e1, e2, eb2, xs, ys):
    with Semaphores(nc) as pool, ExitStack() as ctx:
        def sb(name, shape, dt=F32):
            return ctx.enter_context(nc.sbuf_tensor("e_" + name, shape, dt))

        def sem(name):
            return pool.new("e_" + name)

        def ps(name, shape):
            return ctx.enter_context(nc.psum_tensor("e_" + name, shape, F32))

        NB = 3
        ST = SLOT // P
        ZR = 13
        QUARTERS = 4
        second = sb("second", [P, TILES, D])
        room = second[:, :, :].rearrange("p t d -> p (t d)")
        zero = room[:, 0:ZR * D]
        n = room[:, ZR * D:(ZR + 2 * TPG) * D].rearrange("p (b j d) -> p b j d", b=2, d=D)
        cmp1 = room[:, (ZR + 2 * TPG) * D:(ZR + 2 * TPG) * D + TILES * EXPERTS * EXPERTS].rearrange("p (t k) -> p t k", t=TILES)
        xT = sb("xT", [DC + 1, 2, 2, GT])
        logit = sb("logit", [P, TILES, EXPERTS])
        ex = sb("ex", [P, TILES, EXPERTS])
        top = sb("top", [P, TILES])
        cmp2 = sb("cmp2", [P, TILES, EXPERTS * EXPERTS])
        rank = sb("rank", [P, TILES, EXPERTS])
        pick = sb("pick", [P, 3, TILES, EXPERTS])
        tmp = sb("tmp", [P, TILES, EXPERTS])
        total = sb("total", [P, EXPERTS, TILES])
        inc = sb("inc", [P, EXPERTS, TILES])
        pos = sb("pos", [P, EXPERTS, TILES])
        full = sb("full", [P, EXPERTS, TOKENS // SLOT])
        tiles = sb("tiles", [P, EXPERTS])
        ends = sb("ends", [P, EXPERTS])
        base = sb("base", [P, EXPERTS])
        gate = sb("gate", [P, 2, TILES])
        place = sb("place", [P, 2, TILES])
        place32 = sb("place32", [P, 2, TILES], mybir.dt.int32)
        owner = sb("owner", [1, SLOTS, EXPERTS])
        owned = sb("owned", [1, SLOTS])
        owned32 = sb("owned32", [1, SLOTS], mybir.dt.int32)
        before = sb("before", [P, P])
        w1 = sb("w1", [DC, NB, 2, FF])
        w2 = sb("w2", [P, NB, FC * D + FC])
        b2 = sb("b2", [P, NB, D])
        xin = sb("xin", [P, NB, ST, D])
        sT = sb("sT", [DC, NB, 2, SLOT])
        hT = sb("hT", [P, FC, SLOT])
        y = sb("y", [P, NB, ST, D])
        H, T, O = ps("H", [P, FC, 512]), ps("T", [P, 512]), ps("O", [P, 512])
        s_dve, s_var, s_log, s_guess = [sem(x) for x in ("dve", "var", "log", "guess")]
        s_zero, s_zeroed, s_before, s_n, s_T, s_xTa, s_xTd = [sem(x) for x in ("zero", "zeroed", "before", "n", "T", "xTa", "xTd")]
        s_lg, s_z, s_ex, s_pick, s_count, s_place, s_owned = [sem(x) for x in ("lg", "z", "ex", "pick", "count", "place", "owned")]
        s_sent = sem("sent")
        s_x, s_w, s_out = [[sem(f"{x}{b}") for b in range(NB)] for x in ("x", "w", "out")]
        s_turn, s_sT, s_up, s_gelu, s_down, s_y = [sem(x) for x in ("turn", "sT", "up", "gelu", "down", "y")]
        s_back = [sem(f"back{q}") for q in range(QUARTERS)]
        s_h = sem("h")
        block = ctx.enter_context(nc.Block())
        slot_rows = xs.rearrange("(s t p) d -> s p t d", t=ST, p=P)
        result_rows = ys.rearrange("(s t p) d -> s p t d", t=ST, p=P)

        @block.sync
        def _(sp):
            zero_rows = xs.rearrange("(k p r) d -> k p (r d)", p=P, r=ZR)
            sp.wait_ge(s_zero, 1)
            for k in range(SLOTS * ST // ZR):
                sp.dma_start(zero_rows[k], zero).then_inc(s_zeroed, 16)
            sp.wait_ge(s_zeroed, SLOTS * ST // ZR * 16)

            def load(i, b):
                sp.dma_start(xin[:, b], slot_rows[bass.ds(i, 1)].rearrange("a p t d -> p (a t) d")).then_inc(s_x[b], 16)
                e = sp.value_load(owned32[0:1, bass.ds(i, 1)], min_val=0, max_val=EXPERTS - 1)
                sp.dma_start(w1[:, b], e1[bass.ds(e, 1)].rearrange("a p c f -> p (a c) f")).then_inc(s_w[b], 16)
                sp.dma_start(w2[:, b], e2[bass.ds(e, 1)].rearrange("a p f -> p (a f)")).then_inc(s_w[b], 16)
                sp.dma_start(b2[:, b], eb2[bass.ds(e, 1)].broadcast_to([P, D])).then_inc(s_w[b], 16)

            def store(i, b):
                sp.dma_start(result_rows[bass.ds(i, 1)].rearrange("a p t d -> p (a t) d"), y[:, b]).then_inc(s_out[b], 16)

            sp.wait_ge(s_owned, 1)
            sp.wait_ge(s_sent, TILES * 2 * 16)
            for b in range(NB):
                load(b, b)
            with sp.Fori(0, SLOTS // NB - 1) as r:
                for b in range(NB):
                    sp.wait_ge(s_y, r * NB + b + 1)
                    load(r * NB + (b + NB), b)
                    store(r * NB + b, b)
            for b in range(NB):
                sp.wait_ge(s_y, SLOTS - NB + b + 1)
                sp.dma_start(result_rows[SLOTS - NB + b], y[:, b]).then_inc(s_out[b], 16)
            for b in range(NB):
                sp.wait_ge(s_out[b], SLOTS // NB * 16 + 16)

        @block.gpsimd
        def _(gp):
            nc.gpsimd.affine_select(out=before[:, :], in_=c.ones[:, :], compare_op=ALU.is_gt, fill=0.0,
                                    base=0, pattern=[[1, P]], channel_multiplier=-1).then_inc(s_before, 1)
            gp.wait_ge(s_zeroed, SLOTS * ST // ZR * 16)
            gp.wait_ge(s_place, 1)
            for t in range(TILES):
                for k in range(2):
                    nc.gpsimd.indirect_dma_start(xs, bass.IndirectOffsetOnAxis(place32[:, k, t:t + 1], 0),
                                                 c.x1[:, t, :], None).then_inc(s_sent, 16)
            gp.wait_ge(s_sent, TILES * 2 * 16)
            for b in range(NB):
                gp.wait_ge(s_out[b], SLOTS // NB * 16 + 16)
            for t in range(TILES):
                for k in range(2):
                    nc.gpsimd.indirect_dma_start((second if k else c.x1)[:, t, :], None, ys,
                                                 bass.IndirectOffsetOnAxis(place32[:, k, t:t + 1], 0)
                                                 ).then_inc(s_back[t // (TILES // QUARTERS)], 16)

        @block.vector
        def _(dve):
            own = Count(s_dve)
            nc.vector.memset(zero, 0.0).then_inc(s_zero, 1)
            token_stats(nc, dve, c, own.link, c.x1)
            norm_factors_dve(nc, dve, c, own.link, s_var, s_guess, twice=False)
            own.link(dve, nc.vector.memset(xT[DC:DC + 1, :, 0, :], 1.0))
            with dve.Fori(0, GROUPS // 2) as i:
                for b in range(2):
                    g = i * 2 + b
                    for j in range(TPG):
                        nc.vector.tensor_scalar(n[:, b, j, :], tile_view(c.x1, g, j), factor(c, 0, g, j), factor(c, 1, g, j),
                                                ALU.mult, ALU.add).then_inc(s_n, 1)
                for b in range(2):
                    g = i * 2 + b
                    dve.wait_ge(s_n, (g + 1) * TPG)
                    for j in range(TPG):
                        nc.vector.tensor_scalar(tile_view(c.x1, g, j), n[:, b, j, :], 1.0, None, ALU.mult)
                    dve.wait_ge(s_T, g * 2 + 2)
                    nc.vector.tensor_scalar(xT[0:DC, b, 1, :], H[0:DC, 2 * b + 1, :], col(c, "ln2g")[0:DC, 1:2],
                                            col(c, "ln2b")[0:DC, 1:2], ALU.mult, ALU.add).then_inc(s_xTd, 1)
                dve.wait_ge(s_xTd, i * 2 + 2)
            dve.wait_ge(s_lg, GROUPS)
            own.link(dve, nc.vector.tensor_scalar(logit[:, :, :].rearrange("p t e -> p (t e)"), O[:, 0:TILES * EXPERTS], 1.0,
                                                  None, ALU.mult))

            own.link(dve, nc.vector.tensor_reduce(top[:, :], logit[:, :, :], AX.X, ALU.max))
            nc.vector.tensor_tensor(ex[:, :, :], logit[:, :, :],
                                    top[:, :].rearrange("p (t o) -> p t o", o=1).broadcast_to([P, TILES, EXPERTS]),
                                    ALU.subtract).then_inc(s_z, 1)
            shape = [P, TILES, EXPERTS, EXPERTS]
            other = logit[:, :, :].rearrange("p t (o f) -> p t o f", o=1).broadcast_to(shape)
            this = logit[:, :, :].rearrange("p t (e o) -> p t e o", o=1).broadcast_to(shape)
            c1, c2 = (x[:, :, :].rearrange("p t (e f) -> p t e f", e=EXPERTS) for x in (cmp1, cmp2))
            own.link(dve, nc.vector.tensor_tensor(c1, other, this, ALU.is_gt))
            own.link(dve, nc.vector.tensor_tensor(c2, other, this, ALU.is_equal))
            tri = col(c, "tri").rearrange("p (o k) -> p o k", o=1).broadcast_to([P, TILES, EXPERTS * EXPERTS])
            own.link(dve, nc.vector.tensor_tensor(cmp2[:, :, :], cmp2[:, :, :], tri, ALU.mult))
            own.link(dve, nc.vector.tensor_tensor(cmp1[:, :, :], cmp1[:, :, :], cmp2[:, :, :], ALU.add))
            own.link(dve, nc.vector.tensor_reduce(rank[:, :, :], c1, AX.X, ALU.add))
            first, later, both = (pick[:, k] for k in range(3))
            own.link(dve, nc.vector.tensor_scalar(first, rank[:, :, :], 0.5, None, ALU.is_lt))
            own.link(dve, nc.vector.tensor_scalar(both, rank[:, :, :], 1.5, None, ALU.is_lt))
            dve.sem_inc(s_pick, 1)
            own.link(dve, nc.vector.tensor_tensor(later, both, first, ALU.subtract))
            own.link(dve, nc.vector.memset(pos[:, :, :], 1.0))
            own.link(dve, nc.vector.memset(pos[:, :, 0:1], 0.0))

            def te(x):
                return x[:, :, :].rearrange("p e t -> p t e")

            def over(x, n):
                return x[:, :].rearrange("p (e o) -> p e o", o=1).broadcast_to([P, EXPERTS, n])

            def per_tile(x):
                return x.rearrange("p (t e) -> p t e", e=EXPERTS)

            dve.wait_ge(s_count, 1)
            own.link(dve, nc.vector.tensor_scalar(te(total), per_tile(H[:, 1, 0:TILES * EXPERTS]), 1.0, None, ALU.mult))
            own.link(dve, nc.vector.tensor_tensor_scan(inc[:, :, :].rearrange("p e t -> p (e t)"),
                                                       pos[:, :, :].rearrange("p e t -> p (e t)"),
                                                       total[:, :, :].rearrange("p e t -> p (e t)"), 0.0, ALU.mult, ALU.add))
            starts = col(c, "starts").rearrange("p (o k) -> p o k", o=1).broadcast_to([P, EXPERTS, TOKENS // SLOT])
            own.link(dve, nc.vector.tensor_tensor(full[:, :, :], inc[:, :, TILES - 1:TILES].broadcast_to(
                [P, EXPERTS, TOKENS // SLOT]), starts, ALU.is_gt))
            own.link(dve, nc.vector.tensor_reduce(tiles[:, :], full[:, :, :], AX.X, ALU.add))
            own.link(dve, nc.vector.tensor_tensor_scan(ends[:, :], c.ones[:, 0:EXPERTS], tiles[:, :], 0.0, ALU.mult, ALU.add))
            slots = col(c, "slots")[0:1, :].rearrange("p (s o) -> p s o", o=1).broadcast_to([1, SLOTS, EXPERTS])
            own.link(dve, nc.vector.tensor_tensor(owner[:, :, :], slots, ends[0:1, :].rearrange("p (o e) -> p o e", o=1)
                                                  .broadcast_to([1, SLOTS, EXPERTS]), ALU.is_ge))
            own.link(dve, nc.vector.tensor_reduce(owned[:, :], owner[:, :, :], AX.X, ALU.add))
            own.link(dve, nc.vector.tensor_scalar(owned32[:, :], owned[:, :], EXPERTS - 1.0, None, ALU.min))
            dve.sem_inc(s_owned, 1)
            own.link(dve, nc.vector.tensor_tensor(base[:, :], ends[:, :], tiles[:, :], ALU.subtract))
            own.link(dve, nc.vector.tensor_scalar(base[:, :], base[:, :], float(SLOT), None, ALU.mult))
            own.link(dve, nc.vector.tensor_tensor(pos[:, :, :], inc[:, :, :], total[:, :, :], ALU.subtract))
            own.link(dve, nc.vector.tensor_tensor(pos[:, :, :], pos[:, :, :], over(base, TILES), ALU.add))
            own.link(dve, nc.vector.tensor_tensor(te(pos), te(pos), per_tile(H[:, 0, 0:TILES * EXPERTS]), ALU.add))
            for k in range(2):
                own.link(dve, nc.vector.tensor_tensor(tmp[:, :, :], te(pos), pick[:, k], ALU.mult))
                own.link(dve, nc.vector.tensor_reduce(place[:, k], tmp[:, :, :], AX.X, ALU.add))
            own.link(dve, nc.vector.tensor_scalar(place32[:, :, :], place[:, :, :], 1.0, None, ALU.mult))
            dve.sem_inc(s_place, 1)
            dve.wait_ge(s_ex, 1)
            for k in range(2):
                own.link(dve, nc.vector.tensor_tensor(tmp[:, :, :], ex[:, :, :], pick[:, k], ALU.mult))
                own.link(dve, nc.vector.tensor_reduce(gate[:, k], tmp[:, :, :], AX.X, ALU.add))
            own.link(dve, nc.vector.tensor_tensor(top[:, :], gate[:, 0], gate[:, 1], ALU.add))
            own.link(dve, nc.vector.reciprocal(top[:, :], top[:, :]))
            for k in range(2):
                own.link(dve, nc.vector.tensor_tensor(gate[:, k], gate[:, k], top[:, :], ALU.mult))

            def turned(i, b):
                dve.wait_ge(s_turn, i + 1)
                for cc in range(2):
                    nc.vector.tensor_scalar(sT[:, b, cc, :], T[0:DC, cc * SLOT:(cc + 1) * SLOT], col(c, "ln2g")[0:DC, cc:cc + 1],
                                            col(c, "ln2b")[0:DC, cc:cc + 1], ALU.mult, ALU.add).then_inc(s_sT, 1)

            turned(0, 0)
            for b in range(NB):
                dve.sem_inc(s_out[b], 16)

            def finish(i, b, round_):
                dve.wait_ge(s_w[b], (round_ + 1) * 48)
                dve.wait_ge(s_down, (i + 2) * FC)
                dve.wait_ge(s_out[b], round_ * 16 + 16)
                nc.vector.tensor_tensor(y[:, b], O[:, 0:ST * D].rearrange("p (t d) -> p t d", t=ST),
                                        b2[:, b:b + 1, :].broadcast_to([P, ST, D]), ALU.add).then_inc(s_y, 1)

            with dve.Fori(0, SLOTS // NB - 1) as r:
                for b in range(NB):
                    turned(r * NB + (b + 1), (b + 1) % NB)
                    finish(r * NB + b, b, r)
            for b in range(NB):
                if b + 1 < NB:
                    turned(SLOTS - NB + b + 1, b + 1)
                finish(SLOTS - NB + b, b, SLOTS // NB - 1)
            for q in range(QUARTERS):
                dve.wait_ge(s_back[q], TILES // QUARTERS * 2 * 16)
                for k in range(2):
                    src = second if k else c.x1
                    with dve.Fori(q * (TILES // QUARTERS), (q + 1) * (TILES // QUARTERS)) as t:
                        here = c.h[:, bass.ds(t, 1), :].rearrange("p a d -> p (a d)")
                        nc.vector.scalar_tensor_tensor(out=here, in0=src[:, bass.ds(t, 1), :].rearrange("p a d -> p (a d)"),
                                                       scalar=gate[:, k, bass.ds(t, 1)], in1=here, op0=ALU.mult,
                                                       op1=ALU.add).then_inc(s_h, 1)
                    dve.wait_ge(s_h, (q * 2 + k + 1) * (TILES // QUARTERS))

        @block.scalar
        def _(act):
            nc.scalar.preload_act_table_set(LOG_EXP)
            norm_factors_act(nc, act, c, s_var, s_log, s_guess, twice=False)
            with act.Fori(0, GROUPS // 2) as i:
                for b in range(2):
                    act.wait_ge(s_T, i * 4 + 2 * b + 1)
                    nc.scalar.activation(xT[0:DC, b, 0, :], H[0:DC, 2 * b, :], ACT.Identity, scale=col(c, "ln2g")[0:DC, 0:1],
                                         bias=col(c, "ln2b")[0:DC, 0:1]).then_inc(s_xTa, 1)
            act.wait_ge(s_z, 1)
            nc.scalar.activation(ex[:, :, :], ex[:, :, :], ACT.Exp).then_inc(s_ex, 1)
            nc.scalar.preload_act_table(ACT.Gelu)
            act.sem_inc(s_down, FC)
            with act.Fori(0, SLOTS // NB) as r:
                for b in range(NB):
                    i = r * NB + b
                    act.wait_ge(s_w[b], (r + 1) * 48)
                    for f in range(FC):
                        act.wait_ge(s_up, i * FC + f + 1)
                        act.wait_ge(s_down, i * FC + f + 1)
                        nc.scalar.activation(hT[:, f, :], H[:, f, 0:SLOT], ACT.Gelu,
                                             bias=w2[:, b, FC * D + f:FC * D + f + 1]).then_inc(s_gelu, 1)

        @block.tensor
        def _(pe):
            router = weight(c, "router")
            with pe.Fori(0, GROUPS // 2) as i:
                for b in range(2):
                    pe.wait_ge(s_n, (i * 2 + b) * TPG + TPG)
                    for cc in range(2):
                        for j in range(TPG):
                            mm = nc.tensor.transpose(H[0:DC, 2 * b + cc, j * P:(j + 1) * P],
                                                     n[:, b, j, cc * DC:(cc + 1) * DC], c.ident[:, :])
                        mm.then_inc(s_T, 1)
                for b in range(2):
                    g = i * 2 + b
                    pe.wait_ge(s_xTa, g + 1)
                    pe.wait_ge(s_xTd, g + 1)
                    for j in range(TPG):
                        o = O[:, bass.ds((g * TPG + j) * EXPERTS, EXPERTS)]
                        nc.tensor.matmul(o, xT[:, b, 0, j * P:(j + 1) * P], router[:, 0, :], start=True, stop=False)
                        mm = nc.tensor.matmul(o, xT[0:DC, b, 1, j * P:(j + 1) * P], router[0:DC, 1, :], start=False, stop=True)
                    mm.then_inc(s_lg, 1)
            pe.wait_ge(s_before, 1)
            pe.wait_ge(s_pick, 1)
            both = pick[:, 2].rearrange("p t e -> p (t e)")
            nc.tensor.matmul(H[:, 0, 0:TILES * EXPERTS], before[:, :], both, start=True, stop=True)
            nc.tensor.matmul(H[:, 1, 0:TILES * EXPERTS], c.ones[:, :], both, start=True, stop=True).then_inc(s_count, 1)
            pe.wait_ge(s_place, 1)

            def turn(i, b, round_):
                pe.wait_ge(s_x[b], (round_ + 1) * 16)
                if b or not (isinstance(round_, int) and round_ == 0):
                    pe.wait_ge(s_sT, i * 2)
                for cc in range(2):
                    for t in range(ST):
                        mm = nc.tensor.transpose(T[0:DC, cc * SLOT + t * P:cc * SLOT + (t + 1) * P],
                                                 xin[:, b, t, cc * DC:(cc + 1) * DC], c.ident[:, :])
                mm.then_inc(s_turn, 1)

            def slot_tile(i, b, round_, last=False):
                pe.wait_ge(s_w[b], (round_ + 1) * 48)
                pe.wait_ge(s_sT, i * 2 + 2)

                def down(f):
                    pe.wait_ge(s_gelu, i * FC + f + 1)
                    if f == 0 and (b or not isinstance(round_, int) or round_ > 0):
                        pe.wait_ge(s_y, i)
                    for t in range(ST):
                        mm = nc.tensor.matmul(O[:, t * D:(t + 1) * D], hT[:, f, t * P:(t + 1) * P],
                                              w2[:, b, f * D:(f + 1) * D], start=(f == 0 and t == 0), stop=(f == FC - 1),
                                              skip_group_check=True)
                    mm.then_inc(s_down, 1)

                for f in range(FC):
                    for cc in range(2):
                        mm = nc.tensor.matmul(H[:, f, 0:SLOT], w1[:, b, cc, f * P:(f + 1) * P], sT[:, b, cc, :],
                                              start=(cc == 0), stop=(cc == 1))
                    mm.then_inc(s_up, 1)
                    if f == FC - 2 and not last:
                        turn(i + 1, (b + 1) % NB, round_ + (b + 1) // NB)
                    if f >= 1:
                        down(f - 1)
                down(FC - 1)

            turn(0, 0, 0)
            for b in range(NB):
                slot_tile(b, b, 0)
            with pe.Fori(1, SLOTS // NB - 1) as r:
                for b in range(NB):
                    slot_tile(r * NB + b, b, r)
            for b in range(NB):
                slot_tile(SLOTS - NB + b, b, SLOTS // NB - 1, last=(b == NB - 1))



def scan_block(nc, c):
    with Semaphores(nc) as pool, ExitStack() as ctx:
        def sb(name, shape, dt=F32):
            return ctx.enter_context(nc.sbuf_tensor("s_" + name, shape, dt))

        def sem(name):
            return pool.new("scan_" + name)

        def ps(name, shape):
            return ctx.enter_context(nc.psum_tensor("s_" + name, shape, F32))

        W = IC * GT
        IMG = GT // SEQ
        FIRST = 1e30
        n = sb("n", [P, TPG, D])
        n1 = sb("n1", [P, TPG, D])
        xT = sb("xT", [DC, 2, GT])
        xpad = sb("xpad", [P, IC, IMG, SEQ + TAPS - 1])
        pool4 = c.x1[:, :, :].rearrange("p t d -> p (t d)")
        xc, sz, delta, u = (pool4[:, i * W:(i + 1) * W] for i in range(4))
        pre = sb("pre", [P, W])
        soft = sb("soft", [P, W])
        dbc = sb("dbc", [2 * STATES + 1, GT])
        dA = sb("dA", [P, 2, W])
        hs = sb("hs", [P, 2, W])
        hc = sb("hc", [P, 2, W])
        A = sb("A", [P, IC * STATES])
        wo = sb("wo", [P, IC * D])
        part = sb("part", [P, 2])
        scale = sb("scale", [P, 4])
        ss, rs, rt = sb("ss", [P, TPG]), sb("rs", [P, TPG]), sb("rt", [P, TPG])
        BC, Y, X = ps("BC", [P, 4, 512]), ps("Y", [P, IC, 512]), ps("X", [P, 512])
        s_dve, s_var, s_log, s_guess = [sem(x) for x in ("dve", "var", "log", "guess")]
        s_part, s_tot, s_alog, s_A = [sem(x) for x in ("part", "tot", "alog", "A")]
        s_n, s_h, s_T, s_xTa, s_xTd, s_in, s_sz, s_conv, s_xc = [sem(x) for x in ("n", "h", "T", "xTa", "xTd", "in", "sz", "conv", "xc")]
        s_dbc, s_dbcs, s_dt, s_pre, s_abs, s_soft, s_u = [sem(x) for x in ("dbc", "dbcs", "dt", "pre", "abs", "soft", "u")]
        s_bc, s_dA, s_scan, s_hc, s_hcu, s_y, s_yg, s_sq, s_out, s_v, s_r0, s_rg = [
            sem(x) for x in ("bc", "dA", "scan", "hc", "hcu", "y", "yg", "sq", "out", "v", "r0", "rg")]
        block = ctx.enter_context(nc.Block())
        win = weight(c, "inproj")
        bank = [BC[:, 0, :], BC[:, 1, :], BC[:, 2, :], BC[:, 3, :], Y[:, 0, :], Y[:, 1, :]]

        def chunk(x, i):
            return x[:, i * GT:(i + 1) * GT]

        @block.vector
        def _(dve):
            own = Count(s_dve)
            token_stats(nc, dve, c, own.link, c.h)
            norm_factors_dve(nc, dve, c, own.link, s_var, s_guess, twice=True)
            woraw = col(c, "outproj")
            own.link(dve, nc.vector.memset(part[:, :], 0.0))
            own.link(dve, nc.vector.tensor_reduce(part[0:DC, 0:1], win[0:DC], AX.XY, ALU.add, apply_absolute_value=True))
            own.link(dve, nc.vector.tensor_reduce(part[:, 1:2], woraw, AX.X, ALU.add, apply_absolute_value=True))
            dve.sem_inc(s_part, 1)
            dve.wait_ge(s_tot, 1)
            own.link(dve, nc.vector.tensor_scalar(scale[:, 0:1], X[:, 0:1], 1.0 / (2 * INNER * D), 1e-5, ALU.mult, ALU.max))
            own.link(dve, nc.vector.tensor_scalar(scale[:, 1:2], X[:, 1:2], 1.0 / (INNER * D), 1e-5, ALU.mult, ALU.max))
            own.link(dve, nc.vector.reciprocal(scale[:, 2:4], scale[:, 0:2]))
            for w, k, m in ((win[0:DC], 2, DC), (woraw, 3, P)):
                own.link(dve, nc.vector.tensor_scalar(w, w, scale[0:m, k:k + 1], 1.0, ALU.mult, ALU.min))
                own.link(dve, nc.vector.tensor_scalar(w, w, -1.0, ROUND, ALU.max, ALU.add))
                own.link(dve, nc.vector.tensor_scalar(w, w, ROUND, None, ALU.subtract))
            for i in range(IC):
                own.link(dve, nc.vector.tensor_scalar(wo[:, i * D:(i + 1) * D], woraw[:, i * D:(i + 1) * D],
                                                      col(c, "onorm")[:, i:i + 1], None, ALU.mult))
            nc.vector.tensor_scalar(A[:, :], col(c, "alog"), -20.0, 2.0, ALU.max, ALU.min).then_inc(s_alog, 1)
            dve.wait_ge(s_A, 1)
            own.link(dve, nc.vector.tensor_scalar(A[:, :], A[:, :], -1.0, None, ALU.mult))
            own.link(dve, nc.vector.memset(xpad[:, :, :, 0:TAPS - 1], 0.0))
            dve.sem_inc(s_part, 1)
            dve.sem_inc(s_scan, 4)
            done = own.n
            per_group = TPG + IC * TAPS + 1 + 2 + IC + 1 + 4
            with dve.Fori(0, GROUPS) as g:
                own = Count(s_dve, g * per_group + done)
                for j in range(TPG):
                    nc.vector.tensor_scalar(n[:, j, :], tile_view(c.h, g, j), factor(c, 2, g, j), factor(c, 3, g, j),
                                            ALU.mult, ALU.add).then_inc(s_n, 1)
                for j in range(TPG):
                    own.link(dve, nc.vector.tensor_scalar(n1[:, j, :], tile_view(c.h, g, j), factor(c, 0, g, j),
                                                          factor(c, 1, g, j), ALU.mult, ALU.add))
                for j in range(TPG):
                    nc.vector.tensor_tensor(tile_view(c.h, g, j), n1[:, j, :], tile_view(c.h, g, j), ALU.add).then_inc(s_h, 1)
                dve.wait_ge(s_T, g * 2 + 2)
                nc.vector.tensor_scalar(xT[:, 1, :], Y[0:DC, 1, :], col(c, "rmsw")[0:DC, 1:2], None, ALU.mult).then_inc(s_xTd, 1)
                for i in range(IC):
                    dve.wait_ge(s_in, g * 6 + i + 1)
                    own.link(dve, nc.vector.tensor_scalar(xpad[:, i, :, TAPS - 1:], bank[i].rearrange("p (m t) -> p m t", t=SEQ),
                                                          scale[:, 0:1], None, ALU.mult))
                    out = chunk(pre, i).rearrange("p (m t) -> p m t", t=SEQ)
                    for k in range(TAPS):
                        w = col(c, "conv")[:, i * TAPS + k:i * TAPS + k + 1]
                        src = xpad[:, i, :, k:k + SEQ]
                        if k == 0:
                            own.link(dve, nc.vector.tensor_scalar(out, src, w, col(c, "convb")[:, i:i + 1], ALU.mult, ALU.add))
                        else:
                            ins = nc.vector.scalar_tensor_tensor(out=out, in0=src, scalar=w, in1=out, op0=ALU.mult, op1=ALU.add)
                            if k < TAPS - 1:
                                own.link(dve, ins)
                            else:
                                ins.then_inc(s_conv, 1)
                dve.wait_ge(s_dbc, g + 1)
                own.link(dve, nc.vector.tensor_scalar(dbc[:, :], X[0:2 * STATES + 1, :], 1.0, None, ALU.mult))
                dve.sem_inc(s_dbcs, 1)
                for i in range(IC):
                    dve.wait_ge(s_dt, g * IC + i + 1)
                    nc.vector.tensor_scalar(chunk(pre, i), BC[:, i, :], col(c, "dtb")[:, i:i + 1], None, ALU.add).then_inc(s_pre, 1)
                dve.wait_ge(s_soft, g + 1)
                own.link(dve, nc.vector.scalar_tensor_tensor(out=delta, in0=pre[:, :], scalar=0.0, in1=soft[:, :],
                                                             op0=ALU.max, op1=ALU.add))
                own.link(dve, nc.vector.tensor_tensor(u, delta, xc, ALU.mult))
                nc.vector.memset(delta.rearrange("p (m t) -> p m t", t=SEQ)[:, :, 0:1], FIRST).then_inc(s_u, 1)
                for s in range(STATES):
                    b = s % 2
                    dve.wait_ge(s_bc, (g * STATES + s) * 2 + 1)
                    nc.vector.tensor_tensor(hs[:, b].rearrange("p (i t) -> p i t", i=IC), u.rearrange("p (i t) -> p i t", i=IC),
                                            BC[:, b:b + 1, :].broadcast_to([P, IC, GT]), ALU.mult).then_inc(s_scan, 1)
                    dve.wait_ge(s_scan, (g * STATES + s) * 2 + 5)
                    dve.wait_ge(s_dA, (g * STATES + s) * IC + IC)
                    nc.vector.tensor_tensor_scan(hs[:, b], dA[:, b], hs[:, b], 0.0, ALU.mult, ALU.add).then_inc(s_scan, 1)
                    dve.wait_ge(s_scan, (g * STATES + s) * 2 + 6)
                    dve.wait_ge(s_bc, (g * STATES + s) * 2 + 2)
                    dve.wait_ge(s_hcu, (g * STATES + s) + 1)
                    nc.vector.tensor_tensor(hc[:, b].rearrange("p (i t) -> p i t", i=IC), hs[:, b].rearrange("p (i t) -> p i t", i=IC),
                                            BC[:, 2 + b:3 + b, :].broadcast_to([P, IC, GT]), ALU.mult).then_inc(s_hc, 1)
                dve.wait_ge(s_hc, (g + 1) * STATES)
                dve.wait_ge(s_hcu, (g + 1) * STATES + 2)
                for i in range(IC):
                    own.link(dve, nc.vector.scalar_tensor_tensor(out=chunk(pre, i), in0=chunk(xc, i),
                                                                 scalar=col(c, "dskip")[:, i:i + 1], in1=Y[:, i, :],
                                                                 op0=ALU.mult, op1=ALU.add))
                nc.vector.tensor_tensor(pre[:, :], pre[:, :], sz, ALU.mult).then_inc(s_yg, 1)
                dve.wait_ge(s_out, g * 3 + 1)
                own.link(dve, nc.vector.tensor_scalar(ss[:, :], X[:, 0:TPG], 1.0 / INNER, LN_EPS, ALU.mult, ALU.add))
                dve.sem_inc(s_v, 1)
                dve.wait_ge(s_rg, g + 1)
                own.link(dve, nc.vector.tensor_tensor(rt[:, :], rs[:, :], rs[:, :], ALU.mult))
                own.link(dve, nc.vector.tensor_tensor(rt[:, :], rt[:, :], ss[:, :], ALU.mult))
                own.link(dve, nc.vector.tensor_scalar(rt[:, :], rt[:, :], -0.5, 1.5, ALU.mult, ALU.add))
                own.link(dve, nc.vector.scalar_tensor_tensor(out=rt[:, :], in0=rs[:, :], scalar=scale[:, 1:2], in1=rt[:, :],
                                                             op0=ALU.mult, op1=ALU.mult))
                dve.wait_ge(s_h, g * (TPG * 2) + TPG)
                for j in range(TPG):
                    if j % 2 == 0:
                        dve.wait_ge(s_out, g * 3 + 2 + j // 2)
                    nc.vector.scalar_tensor_tensor(out=tile_view(c.h, g, j), in0=BC[:, j // 2, (j % 2) * D:(j % 2 + 1) * D],
                                                   scalar=rt[:, j:j + 1], in1=tile_view(c.h, g, j), op0=ALU.mult,
                                                   op1=ALU.add).then_inc(s_h, 1)
                dve.wait_ge(s_h, (g + 1) * (TPG * 2))
                assert own.n == per_group, (own.n, per_group)

        @block.scalar
        def _(act):
            nc.scalar.preload_act_table_set(LOG_EXP)
            norm_factors_act(nc, act, c, s_var, s_log, s_guess, twice=True)
            act.wait_ge(s_alog, 1)
            nc.scalar.activation(A[:, :], A[:, :], ACT.Exp).then_inc(s_A, 1)
            act.wait_ge(s_part, 2)
            with act.Fori(0, GROUPS) as g:
                act.wait_ge(s_T, g * 2 + 1)
                nc.scalar.activation(xT[:, 0, :], Y[0:DC, 0, :], ACT.Copy, scale=col(c, "rmsw")[0:DC, 0:1]).then_inc(s_xTa, 1)
                for i in range(IC):
                    act.wait_ge(s_in, g * 6 + 4 + i)
                    nc.scalar.activation(chunk(sz, i), bank[3 + i], ACT.Silu, scale=scale[:, 0:1]).then_inc(s_sz, 1)
                for i in range(IC):
                    act.wait_ge(s_conv, g * IC + i + 1)
                    nc.scalar.activation(chunk(xc, i), chunk(pre, i), ACT.Silu).then_inc(s_xc, 1)
                act.wait_ge(s_pre, g * IC + IC)
                nc.scalar.activation(soft[:, :], pre[:, :], ACT.Abs).then_inc(s_abs, 1)
                act.wait_ge(s_abs, g * 2 + 1)
                nc.scalar.activation(soft[:, :], soft[:, :], ACT.Exp, scale=-1.0).then_inc(s_abs, 1)
                act.wait_ge(s_abs, g * 2 + 2)
                nc.scalar.activation(soft[:, :], soft[:, :], ACT.Ln, bias=1.0).then_inc(s_soft, 1)
                act.wait_ge(s_u, g + 1)
                for s in range(STATES):
                    act.wait_ge(s_scan, (g * STATES + s) * 2 + 2)
                    for i in range(IC):
                        nc.scalar.activation(dA[:, s % 2, i * GT:(i + 1) * GT], chunk(delta, i), ACT.Exp,
                                             scale=A[:, i * STATES + s:i * STATES + s + 1]).then_inc(s_dA, 1)
                act.wait_ge(s_yg, g + 1)
                nc.scalar.activation(soft[:, :], pre[:, :], ACT.Square).then_inc(s_sq, 1)
                act.wait_ge(s_v, g + 1)
                nc.scalar.activation(rs[:, :], ss[:, :], ACT.Ln).then_inc(s_r0, 1)
                act.wait_ge(s_r0, g + 1)
                nc.scalar.activation(rs[:, :], rs[:, :], ACT.Exp, scale=-0.5).then_inc(s_rg, 1)

        @block.tensor
        def _(pe):
            pe.wait_ge(s_part, 1)
            mm = nc.tensor.matmul(X[:, 0:2], c.ones[:, :], part[:, :], start=True, stop=True).then_inc(s_tot, 1)
            pe.wait_ge(s_part, 2)
            pe.sem_inc(s_hcu, 2)
            with pe.Fori(0, GROUPS) as g:
                pe.wait_ge(s_n, g * TPG + TPG)
                for cc in range(2):
                    for j in range(TPG):
                        mm = nc.tensor.transpose(Y[0:DC, cc, j * P:(j + 1) * P], n[:, j, cc * DC:(cc + 1) * DC], c.ident[:, :])
                    mm.then_inc(s_T, 1)
                pe.wait_ge(s_xTa, g + 1)
                pe.wait_ge(s_xTd, g + 1)
                for i in range(2 * IC):
                    for cc in range(2):
                        mm = nc.tensor.matmul(bank[i], win[0:DC, cc, i * P:(i + 1) * P], xT[:, cc, :], start=(cc == 0), stop=(cc == 1))
                    mm.then_inc(s_in, 1)
                for i in range(IC):
                    pe.wait_ge(s_xc, g * IC + i + 1)
                    mm = nc.tensor.matmul(X[0:2 * STATES + 1, :], col(c, "xproj")[:, i * 33:(i + 1) * 33], chunk(xc, i),
                                          start=(i == 0), stop=(i == IC - 1))
                mm.then_inc(s_dbc, 1)
                pe.wait_ge(s_dbcs, g + 1)
                for i in range(IC):
                    nc.tensor.matmul(BC[:, i, :], c.rowp[0:1, ROWP_DT + i * P:ROWP_DT + (i + 1) * P], dbc[0:1, :],
                                     start=True, stop=True).then_inc(s_dt, 1)
                pe.wait_ge(s_pre, g * IC + IC)
                pe.wait_ge(s_sz, g * IC + IC)

                def spread(s):
                    b = s % 2
                    for k in range(2):
                        row = 1 + k * STATES + s
                        nc.tensor.matmul(BC[:, 2 * k + b, :],
                                         c.ident[0:2 * STATES + 1, row:row + 1].broadcast_to([2 * STATES + 1, P]),
                                         dbc[:, :], start=True, stop=True).then_inc(s_bc, 1)

                spread(0)
                for s in range(STATES):
                    if s + 1 < STATES:
                        if s >= 1:
                            pe.wait_ge(s_hc, g * STATES + s)
                        spread(s + 1)
                    pe.wait_ge(s_hc, g * STATES + s + 1)
                    for i in range(IC):
                        mm = nc.tensor.matmul(Y[:, i, :], c.ident[:, :], hc[:, s % 2, i * GT:(i + 1) * GT], start=(s == 0),
                                              stop=(s == STATES - 1))
                    mm.then_inc(s_hcu, 1)
                pe.wait_ge(s_sq, g + 1)
                for j in range(TPG):
                    for i in range(IC):
                        at = i * GT + j * P
                        mm = nc.tensor.matmul(X[:, j:j + 1], soft[:, at:at + P], c.ones[:, 0:1], start=(i == 0), stop=(i == IC - 1))
                mm.then_inc(s_out, 1)
                for j in range(TPG):
                    for i in range(IC):
                        at = i * GT + j * P
                        mm = nc.tensor.matmul(BC[:, j // 2, (j % 2) * D:(j % 2 + 1) * D], pre[:, at:at + P],
                                              wo[:, i * D:(i + 1) * D], start=(i == 0), stop=(i == IC - 1))
                    if j % 2:
                        mm.then_inc(s_out, 1)
                pe.wait_ge(s_h, (g + 1) * (TPG * 2))



def feed_forward(nc, c, out):
    with Semaphores(nc) as pool, ExitStack() as ctx:
        def sb(name, shape, dt=F32):
            return ctx.enter_context(nc.sbuf_tensor("f_" + name, shape, dt))

        def sem(name):
            return pool.new("f_" + name)

        def ps(name, shape):
            return ctx.enter_context(nc.psum_tensor("f_" + name, shape, F32))

        n = sb("n", [P, TPG, D])
        xT = sb("xT", [DC, 2, GT])
        hT = sb("hT", [P, FC, GT])
        y = sb("y", [P, TPG, D])
        H, O = ps("H", [P, FC, 512]), ps("O", [P, 2, 512])
        w1, w2, b1 = weight(c, "f1"), col(c, "f2"), col(c, "f1b")
        s_dve, s_var, s_log, s_guess = [sem(x) for x in ("dve", "var", "log", "guess")]
        s_n, s_T, s_xT, s_up, s_gelu, s_o, s_y, s_out = [sem(x) for x in ("n", "T", "xT", "up", "gelu", "o", "y", "out")]
        block = ctx.enter_context(nc.Block())
        rows = out.rearrange("(t p) d -> p t d", p=P)

        @block.sync
        def _(sp):
            sp.sem_inc(s_out, 16)
            with sp.Fori(0, GROUPS) as g:
                sp.wait_ge(s_y, g * TPG + TPG)
                sp.dma_start(rows[:, bass.ds(g * TPG, TPG), :], y[:, :, :]).then_inc(s_out, 16)
            sp.wait_ge(s_out, GROUPS * 16 + 16)

        @block.vector
        def _(dve):
            own = Count(s_dve)
            token_stats(nc, dve, c, own.link, c.x1)
            norm_factors_dve(nc, dve, c, own.link, s_var, s_guess, twice=False)
            with dve.Fori(0, GROUPS) as g:
                for j in range(TPG):
                    nc.vector.tensor_scalar(n[:, j, :], tile_view(c.x1, g, j), factor(c, 0, g, j), factor(c, 1, g, j),
                                            ALU.mult, ALU.add).then_inc(s_n, 1)
                for cc in range(2):
                    dve.wait_ge(s_T, g * 2 + cc + 1)
                    nc.vector.tensor_scalar(xT[:, cc, :], O[0:DC, cc, :], col(c, "g2")[0:DC, cc:cc + 1],
                                            col(c, "b2")[0:DC, cc:cc + 1], ALU.mult, ALU.add).then_inc(s_xT, 1)
                dve.wait_ge(s_out, g * 16 + 16)
                for j in range(TPG):
                    if j % 2 == 0:
                        dve.wait_ge(s_o, g * 2 + j // 2 + 1)
                    nc.vector.tensor_tensor(y[:, j, :], O[:, j // 2, (j % 2) * D:(j % 2 + 1) * D], tile_view(c.h, g, j),
                                            ALU.add).then_inc(s_y, 1)

        @block.scalar
        def _(act):
            nc.scalar.preload_act_table_set(LOG_EXP)
            norm_factors_act(nc, act, c, s_var, s_log, s_guess, twice=False)
            nc.scalar.preload_act_table(ACT.Gelu)
            with act.Fori(0, GROUPS) as g:
                for f in range(FC):
                    act.wait_ge(s_up, g * FC + f + 1)
                    nc.scalar.activation(hT[:, f, :], H[:, f, :], ACT.Gelu, bias=b1[:, f:f + 1]).then_inc(s_gelu, 1)

        @block.tensor
        def _(pe):
            with pe.Fori(0, GROUPS) as g:
                pe.wait_ge(s_n, g * TPG + TPG)
                for cc in range(2):
                    for j in range(TPG):
                        mm = nc.tensor.transpose(O[0:DC, cc, j * P:(j + 1) * P], n[:, j, cc * DC:(cc + 1) * DC], c.ident[:, :])
                    mm.then_inc(s_T, 1)
                pe.wait_ge(s_xT, g * 2 + 2)

                def down(f):
                    pe.wait_ge(s_gelu, g * FC + f + 1)
                    for j in range(TPG):
                        o = O[:, j // 2, (j % 2) * D:(j % 2 + 1) * D]
                        if f == 0:
                            nc.tensor.matmul(o, c.ones[0:1, :], c.rowp[0:1, ROWP_BF2:ROWP_BF2 + D], start=(j % 2 == 0),
                                             stop=False, skip_group_check=True)
                        mm = nc.tensor.matmul(o, hT[:, f, j * P:(j + 1) * P], w2[:, f * D:(f + 1) * D], start=False,
                                              stop=(f == FC - 1), skip_group_check=True)
                        if f == FC - 1 and j % 2:
                            mm.then_inc(s_o, 1)

                for f in range(FC):
                    for cc in range(2):
                        mm = nc.tensor.matmul(H[:, f, :], w1[0:DC, cc, f * P:(f + 1) * P], xT[:, cc, :], start=(cc == 0),
                                              stop=(cc == 1))
                    mm.then_inc(s_up, 1)
                    if f >= 1:
                        down(f - 1)
                down(FC - 1)
                pe.wait_ge(s_y, g * TPG + TPG)



STOP = 99


def program(nc, patches, w_tok, w97, rows, cols, proj, e1, e2, eb2, extra, out):
    with ExitStack() as ctx:
        c = make_core(nc, ctx)
        scratch = nc.dram_tensor("attention", (IMAGES, HEADS, SEQ, DH), F32, kind="Internal").ap()
        xs, ys = (nc.dram_tensor(x, (SLOTS * SLOT, D), F32, kind="Internal").ap() for x in ("expert_rows", "expert_results"))
        tokenize(nc, c, patches, w_tok, w97, rows, cols, extra)
        if STOP > 0:
            performer(nc, c, proj, scratch)
            performer_out(nc, c, scratch)
        if STOP > 1:
            attention(nc, c, ("aq", "ak", "av", "ao"), "ln1g", "ln1b", mixing=False)
            experts(nc, c, e1, e2, eb2, xs, ys)
        if STOP > 2:
            scan_block(nc, c)
        if STOP > 3:
            attention(nc, c, ("mq", "mk", "mv", "mo"), "g1", "b1", mixing=True)
            feed_forward(nc, c, out)
            return
        with ExitStack() as c2:
            s_o = c2.enter_context(nc.semaphore("s_o"))
            block = c2.enter_context(nc.Block())

            @block.sync
            def _(sp):
                sp.dma_start(out.rearrange("(t p) d -> p t d", p=P), c.h[:, :, :]).then_inc(s_o, 16)
                sp.wait_ge(s_o, 16)


def two_chunks(w, bias, np):
    out = np.zeros((DC + 1, 2, w.shape[1]), w.dtype)
    out[0:DC, 0], out[0:DC, 1] = w[0:DC], w[DC:D]
    if bias is not None:
        out[DC, 0] = bias
    return out


def by_block(w):
    return w.reshape(w.shape[:-1] + (3, 2, 2 * DH)).swapaxes(-3, -2).reshape(w.shape)


def kernel(**inputs):
    import numpy as np
    import concourse.bacc as _bacc
    from concourse.bass_utils import run_bass_kernel_spmd as _run

    a = {k: np.asarray(v) for k, v in inputs.items()}
    patches = a["x"].reshape(GROUPS, IMAGES // GROUPS, 3, 8, 16, 8, 16).transpose(0, 2, 4, 6, 1, 3, 5)
    patches = patches.reshape(GROUPS, PKC, P, GT).transpose(0, 2, 1, 3).reshape(GROUPS, P, PKC * GT)
    w_tok = a["L0_tok_W"].reshape(D, PKC, P).transpose(2, 1, 0).reshape(P, PKC * D)
    qkv, qkvb = a["L0_ffn_in_proj_w"].T, a["L0_ffn_in_proj_b"]
    w97 = {
        "pq": (by_block(a["L0_attn_Wq"]), by_block(a["L0_attn_bq"])),
        "pk": (by_block(a["L0_attn_Wk"]), by_block(a["L0_attn_bk"])),
        "pv": (a["L0_attn_Wv"], a["L0_attn_bv"]), "po": (a["L0_attn_Wo"], a["L0_attn_bo"]),
        "aq": (by_block(qkv[:, 0:D]), by_block(qkvb[0:D])), "ak": (by_block(qkv[:, D:2 * D]), by_block(qkvb[D:2 * D])),
        "av": (qkv[:, 2 * D:], qkvb[2 * D:]), "ao": (a["L0_ffn_out_proj_w"].T, a["L0_ffn_out_proj_b"]),
        "router": (a["L0_ffn_router_w"].T, a["L0_ffn_router_b"]),
        "mq": (by_block(a["L1_ffn_Wq"]), by_block(a["L1_ffn_bq"])),
        "mk": (by_block(a["L1_ffn_Wk"]), by_block(a["L1_ffn_bk"])),
        "mv": (np.concatenate([a["L1_ffn_Wv"], a["L1_ffn_Wr"][:, None]], 1),
               np.concatenate([a["L1_ffn_bv"], a["L1_ffn_br"].reshape(1)])),
        "mo": (a["L1_ffn_Wo"], a["L1_ffn_bo"]), "mm": (a["L1_ffn_Wm"], a["L1_ffn_bm"]),
        "f1": (a["L1_ffn_W1"], None), "inproj": (a["L1_attn_in_proj_weight"].T, None),
    }
    w97 = np.concatenate([two_chunks(*w97[n], np) for n, _ in W97], axis=2)
    rows = np.concatenate([a["L0_tok_b"], a["L0_tok_alpha_w"].reshape(1), a["L0_tok_alpha_a"].reshape(1)])[None, :]

    def chan(x):
        return x.reshape(IC, P, -1).transpose(1, 0, 2).reshape(P, -1)

    def half(x):
        out = np.zeros((P, 2), x.dtype)
        out[0:DC] = x.reshape(2, DC).T
        return out

    cols = {
        "f2": a["L1_ffn_W2"].reshape(FC, P, D).transpose(1, 0, 2).reshape(P, FC * D),
        "outproj": chan(a["L1_attn_out_proj_weight"].T), "xproj": chan(a["L1_attn_x_proj_weight"].T),
        "f1b": a["L1_ffn_bf1"].reshape(FC, P).T, "conv": chan(a["L1_attn_conv_weight"].reshape(INNER, TAPS)),
        "convb": chan(a["L1_attn_conv_bias"]), "dtb": chan(a["L1_attn_dt_proj_bias"]),
        "alog": chan(a["L1_attn_A_log"]), "dskip": chan(a["L1_attn_D"]), "onorm": chan(a["L1_attn_out_norm_weight"]),
        "ln1g": half(a["L0_ffn_ln1_g"]), "ln1b": half(a["L0_ffn_ln1_b"]), "ln2g": half(a["L0_ffn_ln2_g"]),
        "ln2b": half(a["L0_ffn_ln2_b"]), "rmsw": half(a["L1_attn_norm_weight"]), "g1": half(a["L1_ffn_g1"]),
        "b1": half(a["L1_ffn_b1"]), "g2": half(a["L1_ffn_g2"]), "b2": half(a["L1_ffn_b2"]),
    }
    headsum = np.zeros((P, 3, 2), np.float32)
    for b in range(3):
        for r in range(2):
            headsum[32 * b + DH * r:32 * b + DH * (r + 1), b, r] = 0.5 / np.sqrt(DH)
    cols["headsum"] = headsum.reshape(P, 6)
    cols["half"] = np.tile(np.repeat(np.eye(2, dtype=np.float32), DH, axis=0), (4, 1))
    cols["tri"] = np.tile(np.tril(np.ones((EXPERTS, EXPERTS), np.float32), -1).reshape(1, -1), (P, 1))
    cols["starts"] = np.tile(np.arange(TOKENS // SLOT, dtype=np.float32) * SLOT, (P, 1))
    cols["slots"] = np.tile(np.arange(SLOTS, dtype=np.float32), (P, 1))
    cols = np.concatenate([cols[n] for n, _ in COLS], axis=1)
    proj = np.zeros((3, 2, DH, 3, 2, FEATURES), np.float32)
    for b in range(3):
        for r in range(2):
            proj[b, r, :, b, r, :] = a["L0_attn_proj"].T
    proj = proj.reshape(DC, 3, 2 * FEATURES)
    e1 = a["L0_ffn_w1"].reshape(EXPERTS, 2, DC, FF).transpose(0, 2, 1, 3)
    e2 = a["L0_ffn_w2"].reshape(EXPERTS, FC, P, D).transpose(0, 2, 1, 3).reshape(EXPERTS, P, FC * D)
    e2 = np.concatenate([e2, a["L0_ffn_b1"].reshape(EXPERTS, FC, P).transpose(0, 2, 1)], axis=2)
    extra = np.concatenate([a["L1_attn_dt_proj_weight"].reshape(-1), a["L1_ffn_bf2"], a["L1_ffn_bm"]])[None, :]
    arrays = dict(patches=patches, w_tok=w_tok, w97=w97, rows=rows, cols=cols, proj=proj, e1=e1, e2=e2,
                  eb2=a["L0_ffn_b2"], extra=extra)
    arrays = {k: np.ascontiguousarray(v) for k, v in arrays.items()}
    nc = _bacc.Bacc("TRN2", target_bir_lowering=False, num_devices=1)
    args = [nc.dram_tensor(f"in_{k}", v.shape, F32, kind="ExternalInput").ap() for k, v in arrays.items()]
    out = nc.dram_tensor("out", (TOKENS, D), F32, kind="ExternalOutput").ap()
    program(nc, *args, out)
    r = _run(nc, [{f"in_{k}": v for k, v in arrays.items()}], core_ids=[0])
    return r.results[0]["out"].reshape(IMAGES, SEQ, D)
```

```python
from contextlib import ExitStack

import concourse.bass as bass
from concourse import mybir

F32 = mybir.dt.float32
BF16 = mybir.dt.bfloat16
ALU = mybir.AluOpType
ACT = mybir.ActivationFunctionType
AX = mybir.AxisListType

P = 128
IMAGES = 64
SEQ = 64
TOKENS = IMAGES * SEQ
D = 192
DC = D // 2
HEADS = 12
DH = D // HEADS
TILES = TOKENS // P
TPG = 4
GROUPS = TILES // TPG
GT = TPG * P
PATCH_K = 3 * 16 * 16
PKC = PATCH_K // P
FEATURES = 128
EXPERTS = 8
FF = 768
FC = FF // P
INNER = 384
IC = INNER // P
SLOT = 256
SLOTS = (TOKENS * 2 + EXPERTS * (SLOT - 1)) // SLOT
STATES = 16
XP = 3 * 2 * STATES + 1
TAPS = 4
ROUND = 12582912.0
LN_EPS = 1e-5
FEATURE_EPS = 1e-6
POOL_EPS = 1e-6
ROUTED = max(1, int(round(0.15 * SEQ)))
LOG_EXP = "natural_log_exp_and_others"

W97 = [("pq", D), ("pk", D), ("pv", D), ("po", D), ("aq", D), ("ak", D), ("av", D), ("ao", D), ("router", EXPERTS),
       ("mq", D), ("mk", D), ("mv", D + 1), ("mo", D), ("mm", D), ("f1", FF), ("inproj", 2 * INNER)]
ROWS = [("tok_b", D), ("alpha_w", 1), ("alpha_a", 1)]
COLS = [("f2", FC * D), ("outproj", IC * D), ("xproj", IC * 33), ("headsum", 6), ("half", 2), ("tri", EXPERTS * EXPERTS),
        ("starts", TOKENS // SLOT), ("slots", SLOTS), ("f1b", FC), ("conv", IC * TAPS), ("convb", IC),
        ("dtb", IC), ("alog", IC * STATES), ("dskip", IC), ("onorm", IC), 
        ("ln1g", 2), ("ln1b", 2), ("ln2g", 2), ("ln2b", 2), ("rmsw", 2), ("g1", 2), ("b1", 2), ("g2", 2), ("b2", 2)]


def offsets(parts):
    at, out = 0, {}
    for name, n in parts:
        out[name] = (at, n)
        at += n
    return out, at


W97_AT, W97_N = offsets(W97)
ROWS_AT, ROWS_N = offsets(ROWS)
COLS_AT, COLS_N = offsets(COLS)


ROWP_DT, ROWP_BF2, ROWP_BM, ROWP_N = 0, INNER, INNER + D, INNER + 2 * D


class Count:

    def __init__(self, sem, base=0):
        self.sem, self.base, self.n = sem, base, 0

    def inc(self, ins):
        self.n += 1
        return ins.then_inc(self.sem, 1)

    def link(self, eng, ins):
        self.inc(ins)
        eng.wait_ge(self.sem, self.base + self.n)


class Semaphores:

    def __init__(self, nc):
        self.nc, self.all = nc, []

    def __enter__(self):
        return self

    def new(self, name):
        self.all.append(self.nc.alloc_semaphore(name))
        return self.all[-1]

    def __exit__(self, *_):
        self.nc.clear_and_free_semaphores(self.all)
        self.nc.all_engine_barrier()


class Core:
    pass


def make_core(nc, ctx):
    c = Core()

    def sb(name, shape, dt=F32):
        return ctx.enter_context(nc.sbuf_tensor(name, shape, dt))

    c.h = sb("h", [P, TILES, D])
    c.x1 = sb("x1", [P, TILES, D])
    c.w = sb("w97", [DC + 1, 2, W97_N])
    c.cols = sb("cols", [P, COLS_N])
    c.rows = sb("rows", [P, ROWS_N])
    c.rowp = sb("rowp", [1, ROWP_N])
    c.ident = sb("ident", [P, P])
    c.same = sb("same", [P, P])
    c.lower = sb("lower", [P, P])
    c.ones = sb("ones", [P, P])
    c.st = sb("st", [P, TILES, 6])
    c.mv = sb("mv", [P, 2, TILES])
    c.rstd = sb("rstd", [P, 6, TILES])
    return c


def weight(c, name):
    at, n = W97_AT[name]
    return c.w[:, :, at:at + n]


def col(c, name):
    at, n = COLS_AT[name]
    return c.cols[:, at:at + n]


def tile_view(x, g, j):
    return x[:, bass.ds(g * TPG + j, 1), :].rearrange("p a d -> p (a d)")


def token_stats(nc, dve, c, link, x):
    STEP = 8
    with dve.Fori(0, TILES // STEP) as i:
        for j in range(STEP):
            t = bass.ds(i * STEP + j, 1)
            nc.vector.bn_stats(c.st[:, t, :].rearrange("p a s -> p (a s)"), x[:, t, :].rearrange("p a d -> p (a d)"))
    link(dve, nc.vector.memset(c.rstd[:, 0, :], 0.0))
    mean, var, t = c.mv[:, 0, :], c.mv[:, 1, :], c.rstd[:, 0, :]
    even, odd, even2, odd2 = (c.st[:, :, i] for i in (1, 4, 2, 5))
    link(dve, nc.vector.tensor_tensor(mean, even, odd, ALU.add))
    link(dve, nc.vector.tensor_scalar(mean, mean, 0.5, None, ALU.mult))
    link(dve, nc.vector.tensor_tensor(var, even2, odd2, ALU.add))
    link(dve, nc.vector.tensor_scalar(var, var, 1.0 / D, None, ALU.mult))
    link(dve, nc.vector.tensor_tensor(t, even, odd, ALU.subtract))
    link(dve, nc.vector.scalar_tensor_tensor(out=t, in0=t, scalar=0.25, in1=t, op0=ALU.mult, op1=ALU.mult))
    link(dve, nc.vector.tensor_tensor(var, var, t, ALU.add))


def norm_factors_dve(nc, dve, c, link, s_var, s_guess, twice):
    mean, var = c.mv[:, 0, :], c.mv[:, 1, :]
    r, nm, r2, nm2, v, t = (c.rstd[:, i, :] for i in range(6))
    for turn in range(2 if twice else 1):
        if turn == 1:
            link(dve, nc.vector.tensor_tensor(t, r, r, ALU.mult))
            link(dve, nc.vector.tensor_tensor(t, t, var, ALU.mult))
        dve_in = var if turn == 0 else t
        out = r if turn == 0 else r2
        link(dve, nc.vector.tensor_scalar(v, dve_in, LN_EPS, None, ALU.add))
        nc.vector.tensor_copy(out, v).then_inc(s_var, 1)
        dve.wait_ge(s_guess, turn + 1)
        link(dve, nc.vector.tensor_tensor(t, out, out, ALU.mult))
        link(dve, nc.vector.tensor_tensor(t, t, v, ALU.mult))
        link(dve, nc.vector.tensor_scalar(t, t, -0.5, 1.5, ALU.mult, ALU.add))
        link(dve, nc.vector.tensor_tensor(out, out, t, ALU.mult))
    link(dve, nc.vector.scalar_tensor_tensor(out=nm, in0=mean, scalar=-1.0, in1=r, op0=ALU.mult, op1=ALU.mult))
    if twice:
        link(dve, nc.vector.tensor_tensor(r2, r2, r, ALU.mult))
        link(dve, nc.vector.scalar_tensor_tensor(out=nm2, in0=mean, scalar=-1.0, in1=r2, op0=ALU.mult, op1=ALU.mult))


def norm_factors_act(nc, act, c, s_var, s_log, s_guess, twice):
    for turn in range(2 if twice else 1):
        out = c.rstd[:, 2 * turn, :]
        act.wait_ge(s_var, turn + 1)
        nc.scalar.activation(out, out, ACT.Ln).then_inc(s_log, 1)
        act.wait_ge(s_log, turn + 1)
        nc.scalar.activation(out, out, ACT.Exp, scale=-0.5).then_inc(s_guess, 1)


def factor(c, i, g, j):
    return c.rstd[:, i, bass.ds(g * TPG + j, 1)]



def tokenize(nc, c, patches, w_tok, w97, rows, cols, rowp):
    with Semaphores(nc) as pool, ExitStack() as ctx:
        def sb(name, shape, dt=F32):
            return ctx.enter_context(nc.sbuf_tensor(name, shape, dt))

        def sem(name):
            return pool.new(name)

        NB = 2
        xin = sb("xin", [P, NB, PKC * GT])
        xr = sb("xr", [P, NB, PKC * GT])
        xq = sb("xq", [P, NB, PKC * GT], BF16)
        wt = sb("wt", [P, PKC * D])
        wq = sb("wq", [P, PKC * D], BF16)
        sc = sb("sc", [P, 4])
        acc = ctx.enter_context(nc.psum_tensor("acc", [P, TPG, 512], F32))
        s_small, s_wt, s_rest, s_bigcols = sem("s_small"), sem("s_wt"), sem("s_rest"), sem("s_bigcols")
        s_x = [sem(f"s_x{b}") for b in range(NB)]
        s_dve, s_scale, s_wq = sem("s_dve0"), sem("s_scale"), sem("s_wq")
        s_rounded, s_quant, s_acc, s_tok = sem("s_rounded"), sem("s_quant"), sem("s_acc"), sem("s_tok")
        s_const, s_masks = sem("s_const"), sem("s_masks")
        block = ctx.enter_context(nc.Block())

        @block.sync
        def _(sp):
            sp.dma_start(c.rows[:, :], rows[0:1, :].broadcast_to([P, ROWS_N])).then_inc(s_small, 16)
            sp.dma_start(wt[:, :], w_tok).then_inc(s_wt, 16)
            for b in range(NB):
                sp.dma_start(xin[:, b, :], patches[b]).then_inc(s_x[b], 16)
            with sp.Fori(0, GROUPS // NB - 1) as i:
                for b in range(NB):
                    sp.wait_ge(s_rounded, i * NB + b + 1)
                    sp.dma_start(xin[:, b, :], patches[i * NB + (b + NB)]).then_inc(s_x[b], 16)
            sp.dma_start(c.w[:, :, :], w97).then_inc(s_rest, 16)
            sp.dma_start(c.cols[:, :], cols).then_inc(s_rest, 16)
            sp.dma_start(c.rowp[:, :], rowp).then_inc(s_rest, 16)
            sp.wait_ge(s_rest, 48)

        @block.gpsimd
        def _(gp):
            nc.gpsimd.memset(c.ones[:, :], 1.0).then_inc(s_const, 1)
            for i in range(2):
                for k in range(2):
                    gp.wait_ge(s_const, i * 2 + k + 1)
                    nc.gpsimd.memset(c.same[i * SEQ:(i + 1) * SEQ, k * SEQ:(k + 1) * SEQ],
                                     float(i == k)).then_inc(s_const, 1)
            gp.wait_ge(s_const, 5)
            nc.gpsimd.affine_select(out=c.ident[:, :], in_=c.ones[:, :], compare_op=ALU.is_equal, fill=0.0,
                                    base=0, pattern=[[-1, P]], channel_multiplier=1).then_inc(s_masks, 1)
            nc.gpsimd.affine_select(out=c.lower[:, :], in_=c.same[:, :], compare_op=ALU.is_gt, fill=0.0,
                                    base=0, pattern=[[-1, P]], channel_multiplier=1).then_inc(s_masks, 1)
            gp.wait_ge(s_masks, 2)

        @block.scalar
        def _(act):
            nc.scalar.preload_act_table_set(LOG_EXP)
            act.wait_ge(s_scale, 1)
            with act.Fori(0, GROUPS // NB) as i:
                for b in range(NB):
                    act.wait_ge(s_x[b], i * 16 + 16)
                    act.wait_ge(s_quant, i * NB + b + 1)
                    nc.scalar.activation(xr[:, b, :], xin[:, b, :], ACT.Copy, bias=ROUND,
                                         scale=sc[:, 1:2]).then_inc(s_rounded, 1)

        @block.vector
        def _(dve):
            cnt = Count(s_dve)
            dve.wait_ge(s_small, 16)
            a = ROWS_AT["alpha_w"][0]
            nc.vector.reciprocal(sc[:, 0:2], c.rows[:, a:a + 2]).then_inc(s_scale, 1)
            cnt.link(dve, nc.vector.tensor_tensor(sc[:, 2:3], c.rows[:, a:a + 1], c.rows[:, a + 1:a + 2], ALU.mult))
            dve.wait_ge(s_scale, 1)
            dve.wait_ge(s_wt, 16)
            cnt.link(dve, nc.vector.tensor_scalar(wt[:, :], wt[:, :], sc[:, 0:1], ROUND, ALU.mult, ALU.add))
            cnt.link(dve, nc.vector.tensor_scalar(wt[:, :], wt[:, :], ROUND - 128, ROUND + 127, ALU.max, ALU.min))
            nc.vector.tensor_scalar(wq[:, :], wt[:, :], ROUND, None, ALU.subtract).then_inc(s_wq, 1)
            dve.sem_inc(s_quant, NB)
            with dve.Fori(0, GROUPS // NB) as i:
                for b in range(NB):
                    dve.wait_ge(s_rounded, i * NB + b + 1)
                    own = Count(s_dve, i * NB + b + 3)
                    own.link(dve, nc.vector.tensor_scalar(xr[:, b, :], xr[:, b, :], ROUND - 128, ROUND + 127,
                                                          ALU.max, ALU.min))
                    nc.vector.tensor_scalar(xq[:, b, :], xr[:, b, :], ROUND, None, ALU.subtract).then_inc(s_quant, 1)
                    for j in range(TPG):
                        dve.wait_ge(s_acc, (i * NB + b) * TPG + j + 1)
                        tile = c.h[:, bass.ds((i * NB + b) * TPG + j, 1), :].rearrange("p a d -> p (a d)")
                        nc.vector.scalar_tensor_tensor(out=tile, in0=acc[:, j, 0:D], scalar=sc[:, 2:3],
                                                       in1=c.rows[:, 0:D], op0=ALU.mult, op1=ALU.add).then_inc(s_tok, 1)

        @block.tensor
        def _(pe):
            pe.wait_ge(s_wq, 1)
            with pe.Fori(0, GROUPS // NB) as i:
                for b in range(NB):
                    pe.wait_ge(s_quant, (i * NB + b) + NB + 1)
                    for j in range(TPG):
                        if b == 1:
                            pe.wait_ge(s_tok, (i * NB) * TPG + j + 1)
                        for k in range(PKC):
                            mm = nc.tensor.matmul(acc[:, j, 0:D], xq[:, b, k * GT + j * P:k * GT + (j + 1) * P],
                                                  wq[:, k * D:(k + 1) * D], start=(k == 0), stop=(k == PKC - 1))
                        mm.then_inc(s_acc, 1)
                pe.wait_ge(s_tok, (i + 1) * (NB * TPG))



def performer(nc, c, proj, scratch):
    with Semaphores(nc) as pool, ExitStack() as ctx:
        def sb(name, shape, dt=F32):
            return ctx.enter_context(nc.sbuf_tensor(name, shape, dt))

        def sem(name):
            return pool.new("p_" + name)

        N17 = DH + 1
        projn = sb("projn", [DC, 3, 2 * FEATURES])
        qk_all = sb("qk_all", [DC, 4, TOKENS])
        va_all = sb("va_all", [P, TILES, HEADS * N17])
        diag = sb("diag", [P, TILES, 2, HEADS])
        room = c.x1[:, :, :].rearrange("p t d -> p (t d)")
        n = room[:, 0:2 * TPG * D].rearrange("p (b j d) -> p b j d", b=2, d=D)
        xT = room[0:DC + 1, 2 * TPG * D:2 * TPG * D + 4 * GT].rearrange("p (b c t) -> p b c t", b=2, c=2)
        sq = room[0:DC, 2 * TPG * D + 4 * GT:2 * TPG * D + 8 * GT].rearrange("p (i t) -> p i t", i=4)
        feat = room.rearrange("p (b k h m) -> p b k h m", b=2, k=2, m=FEATURES)
        qk = sb("qk", [DC, 2, 4, P])
        va = sb("va", [P, 2, 2, HEADS * N17])
        qT = sb("qT", [P, HEADS, P])
        kvs = sb("kvs", [P, 2, 2, HEADS * N17])
        epsv = c.rstd[:, 2:6, :].rearrange("p a t -> p (a t)")
        small = c.mv[:, :, :].rearrange("p a t -> p (a t)")
        mx, den = small[:, 0:2 * HEADS].rearrange("p (k h) -> p k h", k=2), small[:, 2 * HEADS:3 * HEADS]
        att = [c.st[:, :, :].rearrange("p t s -> p (t s)").rearrange("p (h d) -> p h d", d=DH), sb("att", [P, HEADS, DH])[:, :, :]]
        banks = ctx.enter_context(nc.psum_tensor("banks", [P, 8, 512], F32))
        T, Q, V = banks[:, 0:2], banks[:, 2:6], banks[:, 6:8]
        sets, KV = [banks[:, 0:3], banks[:, 3:6]], banks[:, 6, 0:2 * HEADS * N17].rearrange("p (i e) -> p i e", i=2)
        num_ps = banks[:, 7, 0:HEADS * N17]

        num_he = num_ps.rearrange("p (h e) -> p h e", e=N17)

        def diag_ps(b):
            return V[:, b, 2 * D:2 * D + 4 * HEADS]

        s_ld, s_dve, s_var, s_log, s_guess = [sem(x) for x in ("ld", "dve", "var", "log", "guess")]
        s_n, s_T, s_xT, s_q, s_qs, s_sq, s_v, s_va, s_ready = [sem(x) for x in ("n", "T", "xT", "q", "qs", "sq", "v", "va", "ready")]
        s_lq, s_lv = [sem("lq0"), sem("lq1")], [sem("lv0"), sem("lv1")]
        s_dd, s_sub, s_exp = ([sem(x + "q"), sem(x + "k")] for x in ("dd", "sub", "exp"))
        s_kv, s_kvs, s_tr, s_qT, s_num, s_att = [sem(x) for x in ("kv", "kvs", "tr", "qT", "num", "att")]
        s_out = [sem("out0"), sem("out1")]
        block = ctx.enter_context(nc.Block())
        Q_, K_ = 0, 1

        def steps(eng, step):
            for t in range(4):
                step(t, t % 2)
            with eng.Fori(2, TILES // 2) as i:
                for p in range(2):
                    step(i * 2 + p, p)
            for t in range(TILES, TILES + 2):
                step(t, t % 2)

        def inner(t):
            return not isinstance(t, int)

        @block.sync
        def _(sp):
            sp.dma_start(projn[:, :, :], proj).then_inc(s_ld, 16)
            for b in range(2):
                sp.sem_inc(s_out[b], 32)
            sp.wait_ge(s_ready, 2)

            def load(t, p):
                sp.dma_start(qk[:, p], qk_all[:, :, bass.ds(t * P, P)]).then_inc(s_lq[p], 16)
                for i in range(2):
                    rows = slice(i * SEQ, (i + 1) * SEQ)
                    sp.dma_start(va[rows, p, i], va_all[rows, bass.ds(t, 1), :].rearrange("p a e -> p (a e)")
                                 ).then_inc(s_lv[p], 16)

            for p in range(2):
                load(p, p)

            def store(t, p):
                sp.wait_ge(s_att, t + 1)
                for i in range(2):
                    sp.dma_start(scratch[bass.ds(t * 2 + i, 1)].rearrange("a h l d -> l (a h) d"),
                                 att[p][i * SEQ:(i + 1) * SEQ]).then_inc(s_out[p], 16)

            for p in range(2):
                sp.wait_ge(s_kv, p + 1)
                load(p + 2, p)
            with sp.Fori(1, TILES // 2 - 1) as i:
                for p in range(2):
                    t = i * 2 + p
                    sp.wait_ge(s_kv, t + 1)
                    load(t + 2, p)
                    store(t - 2, p)
            for t in range(TILES - 4, TILES):
                store(t, t % 2)
            for b in range(2):
                sp.wait_ge(s_out[b], TILES // 2 * 32 + 32)

        @block.vector
        def _(dve):
            own = Count(s_dve)
            token_stats(nc, dve, c, own.link, c.h)
            norm_factors_dve(nc, dve, c, own.link, s_var, s_guess, twice=False)
            own.link(dve, nc.vector.memset(epsv, FEATURE_EPS))
            own.link(dve, nc.vector.memset(va[:, :, :, :], 0.0))
            own.link(dve, nc.vector.memset(va_all[:, :, :].rearrange("p t (h e) -> p (t h) e", e=N17)[:, :, DH:N17], 1.0))
            own.link(dve, nc.vector.memset(xT[DC:DC + 1, :, 0, :], 1.0))
            dve.wait_ge(s_ld, 16)
            own.link(dve, nc.vector.tensor_scalar(projn[:, :, :], projn[:, :, :], float(DH) ** -0.25, None, ALU.mult))
            done = own.n

            def rows(g, b):
                for j in range(TPG):
                    nc.vector.tensor_scalar(n[:, b, j, :], tile_view(c.h, g, j), factor(c, 0, g, j), factor(c, 1, g, j),
                                            ALU.mult, ALU.add).then_inc(s_n, 1)

            def group(g, b, last=False):
                if not last:
                    rows(g + 1, 1 - b)
                for i in range(4):
                    dve.wait_ge(s_q, g * 4 + i + 1)
                    nc.vector.tensor_scalar(qk_all[:, i, bass.ds(g * GT, GT)], Q[0:DC, i, :], 1.0, None,
                                            ALU.mult).then_inc(s_qs, 1)
                for a in range(2):
                    dve.wait_ge(s_v, g * 2 + a + 1)
                    nc.vector.tensor_scalar(
                        va_all[:, bass.ds(g * TPG + 2 * a, 2), :].rearrange("p j (h e) -> p j h e", e=N17)[:, :, :, 0:DH],
                        V[:, a, 0:2 * D].rearrange("p (j h d) -> p j h d", j=2, d=DH), 1.0, None, ALU.mult).then_inc(s_va, 1)
                    nc.vector.tensor_scalar(diag[:, bass.ds(g * TPG + 2 * a, 2), :, :].rearrange("p j k h -> p (j k h)"),
                                            diag_ps(a), 1.0, None, ALU.mult).then_inc(s_va, 1)

            rows(0, 0)
            with dve.Fori(0, GROUPS // 2 - 1) as i:
                for b in range(2):
                    group(i * 2 + b, b)
            group(GROUPS - 2, 0)
            group(GROUPS - 1, 1, last=True)
            dve.wait_ge(s_va, GROUPS * 4)
            dve.wait_ge(s_qs, GROUPS * 4)
            dve.wait_ge(s_sq, GROUPS * 4)
            dve.sem_inc(s_ready, 2)

            def features(t, p, kind, own):
                dve.wait_ge(s_dd[kind], t + 1)
                s = sets[(p + 1 - kind) % 2]
                own.link(dve, nc.vector.tensor_reduce(mx[:, kind, :].rearrange("p (b s) -> p b s", b=3),
                                                      s.rearrange("p b (s m) -> p b s m", s=4), AX.X, ALU.max))
                own.link(dve, nc.vector.tensor_tensor(mx[:, kind, :], mx[:, kind, :],
                                                      diag[:, bass.ds(t, 1), kind, :].rearrange("p a h -> p (a h)"), ALU.add))
                nc.vector.tensor_tensor(feat[:, p, kind].rearrange("p (b s) m -> p b s m", b=3),
                                        s.rearrange("p b (s m) -> p b s m", s=4),
                                        mx[:, kind, :].rearrange("p (b s o) -> p b s o", b=3, o=1).broadcast_to([P, 3, 4, FEATURES]),
                                        ALU.subtract).then_inc(s_sub[kind], 1)

            def step(t, p):
                base = done + (t * 5 - 2 if inner(t) or t >= 2 else t * 4)
                own = Count(s_dve, base)
                if inner(t) or t < TILES:
                    features(t, p, K_, own)
                    features(t, p, Q_, own)
                else:
                    own = Count(s_dve, done + TILES * 5 - 2 + (t - TILES))
                if inner(t) or t >= 2:
                    dve.wait_ge(s_num, t - 1)
                    own.link(dve, nc.vector.reciprocal(den, num_he[:, :, DH]))
                    dve.wait_ge(s_out[p], (t - p) * 16)
                    nc.vector.tensor_tensor(att[p], num_he[:, :, 0:DH],
                                            den.rearrange("p (h o) -> p h o", o=1).broadcast_to([P, HEADS, DH]),
                                            ALU.mult).then_inc(s_att, 1)

            steps(dve, step)

        @block.scalar
        def _(act):
            nc.scalar.preload_act_table_set(LOG_EXP)
            norm_factors_act(nc, act, c, s_var, s_log, s_guess, twice=False)

            def turned(g, b):
                for cc in range(2):
                    act.wait_ge(s_T, g * 2 + cc + 1)
                    nc.scalar.activation(xT[0:DC, b, cc, :], T[0:DC, cc, :], ACT.Copy).then_inc(s_xT, 1)

            def group(g, b, last=False):
                if inner(g) or g > 0:
                    act.wait_ge(s_v, g * 2)
                for i in range(4):
                    act.wait_ge(s_qs, g * 4 + i + 1)
                    nc.scalar.activation(sq[:, i, :], Q[0:DC, i, :], ACT.Square).then_inc(s_sq, 1)
                    if i == 2 and not last:
                        turned(g + 1, 1 - b)

            turned(0, 0)
            with act.Fori(0, GROUPS // 2 - 1) as i:
                for b in range(2):
                    group(i * 2 + b, b)
            group(GROUPS - 2, 0)
            group(GROUPS - 1, 1, last=True)

            def step(t, p):
                if inner(t) or 1 <= t <= TILES:
                    act.wait_ge(s_kv, t)
                    nc.scalar.activation(kvs[:, 1 - p], KV,
                                         ACT.Copy).then_inc(s_kvs, 1)
                if inner(t) or t < TILES:
                    act.wait_ge(s_sub[K_], t + 1)
                    e = feat[:, p, K_].rearrange("p h m -> p (h m)")
                    nc.scalar.activation(e, e, ACT.Exp).then_inc(s_exp[K_], 1)
                if inner(t) or 1 <= t <= TILES:
                    act.wait_ge(s_tr, t)
                    if inner(t) or t >= 2:
                        act.wait_ge(s_num, t - 1)
                    nc.scalar.activation(qT[:, :, :].rearrange("p (b s) m -> p b (s m)", b=3), sets[p],
                                         ACT.Copy, bias=FEATURE_EPS).then_inc(s_qT, 1)
                if inner(t) or t < TILES:
                    act.wait_ge(s_sub[Q_], t + 1)
                    e = feat[:, p, Q_].rearrange("p h m -> p (h m)")
                    nc.scalar.activation(e, e, ACT.Exp).then_inc(s_exp[Q_], 1)

            steps(act, step)

        @block.tensor
        def _(pe):
            wq, wk, wv = weight(c, "pq"), weight(c, "pk"), weight(c, "pv")
            blk = col(c, "headsum")[0:DC, :]

            def turn(g, b):
                pe.wait_ge(s_n, (g + 1) * TPG)
                for cc in range(2):
                    for j in range(TPG):
                        mm = nc.tensor.transpose(T[0:DC, cc, j * P:(j + 1) * P], n[:, b, j, cc * DC:(cc + 1) * DC], c.ident[:, :])
                    mm.then_inc(s_T, 1)

            def group(g, b, last=False):
                pe.wait_ge(s_xT, g * 2 + 2)
                if inner(g) or g > 0:
                    pe.wait_ge(s_sq, g * 4)
                for i in range(4):
                    w = (wq if i < 2 else wk)[:, :, (i % 2) * DC:(i % 2 + 1) * DC]
                    nc.tensor.matmul(Q[0:DC, i, :], w[:, 0, :], xT[:, b, 0, :], start=True, stop=False)
                    nc.tensor.matmul(Q[0:DC, i, :], w[0:DC, 1, :], xT[0:DC, b, 1, :], start=False, stop=True).then_inc(s_q, 1)
                if not last:
                    turn(g + 1, 1 - b)
                if inner(g) or g > 0:
                    pe.wait_ge(s_va, g * 4)
                for a in range(2):
                    for jj in range(2):
                        j = 2 * a + jj
                        o = V[:, a, jj * D:(jj + 1) * D]
                        nc.tensor.matmul(o, xT[:, b, 0, j * P:(j + 1) * P], wv[:, 0, :], start=True, stop=False)
                        nc.tensor.matmul(o, xT[0:DC, b, 1, j * P:(j + 1) * P], wv[0:DC, 1, :], start=False, stop=True)
                pe.wait_ge(s_sq, g * 4 + 4)
                for a in range(2):
                    for jj in range(2):
                        j = 2 * a + jj
                        for kind in range(2):
                            for cc in range(2):
                                at = (jj * 2 + kind) * HEADS
                                o = diag_ps(a)[:, at:at + HEADS].rearrange("p (b c r) -> p b c r", b=3, c=2)[:, :, cc, :]
                                mm = nc.tensor.matmul(o, sq[:, 2 * kind + cc, j * P:(j + 1) * P], blk, start=True, stop=True)
                    mm.then_inc(s_v, 1)

            turn(0, 0)
            with pe.Fori(0, GROUPS // 2 - 1) as i:
                for b in range(2):
                    group(i * 2 + b, b)
            group(GROUPS - 2, 0)
            group(GROUPS - 1, 1, last=True)
            pe.wait_ge(s_ready, 2)

            def products(t, p, kind, b):
                for cc in range(2):
                    mm = nc.tensor.matmul(sets[(p + 1 - kind) % 2][:, b, cc * 256:cc * 256 + 256],
                                          qk[:, p, 2 * kind + cc, :], projn[:, b, :], start=True, stop=True)
                if b == 2:
                    mm.then_inc(s_dd[kind], 1)

            def step(t, p):
                enters, second, third = inner(t) or t < TILES, inner(t) or 1 <= t <= TILES, inner(t) or t >= 2
                if enters:
                    pe.wait_ge(s_lq[p], (t - p) * 8 + 16)
                    if inner(t) or t >= 1:
                        pe.wait_ge(s_sub[Q_], t)
                    for b in range(3):
                        products(t, p, K_, b)
                if third:
                    pe.wait_ge(s_qT, t - 1)
                for b in range(3):
                    if enters:
                        products(t, p, Q_, b)
                    if second:
                        if b == 0:
                            pe.wait_ge(s_exp[K_], t)
                            pe.wait_ge(s_lv[1 - p], (t - 1 - (1 - p)) * 16 + 32)
                            if inner(t) or t >= 2:
                                pe.wait_ge(s_kvs, t - 1)
                            nc.tensor.matmul(KV, epsv, va[:, 1 - p], start=True, stop=False, skip_group_check=True)
                        for h in range(4 * b, 4 * b + 4):
                            e = slice(h * N17, (h + 1) * N17)
                            mm = nc.tensor.matmul(KV[:, :, e], feat[:, 1 - p, K_, h, :], va[:, 1 - p, :, e], start=False,
                                                  stop=(h == HEADS - 1), skip_group_check=True)
                        if b == 2:
                            mm.then_inc(s_kv, 1)
                if second:
                    if enters:
                        pe.wait_ge(s_sub[K_], t + 1)
                    pe.wait_ge(s_exp[Q_], t)
                if third:
                    pe.wait_ge(s_kvs, t - 1)
                    if inner(t) or t >= 3:
                        pe.wait_ge(s_att, t - 2)
                for h in range(HEADS):
                    if third:
                        for i in range(2):
                            mm = nc.tensor.matmul(num_ps[i * SEQ:(i + 1) * SEQ, h * N17:(h + 1) * N17],
                                                  qT[:, h, i * SEQ:(i + 1) * SEQ],
                                                  kvs[:, p, i, h * N17:(h + 1) * N17], start=True, stop=True)
                        if h == HEADS - 1:
                            mm.then_inc(s_num, 1)
                    if second:
                        mm = nc.tensor.transpose(sets[p][:, h // 4, (h % 4) * P:(h % 4 + 1) * P], feat[:, 1 - p, Q_, h, :],
                                                 c.ident[:, :])
                        if h == HEADS - 1:
                            mm.then_inc(s_tr, 1)

            steps(pe, step)


def performer_out(nc, c, scratch):
    with Semaphores(nc) as pool, ExitStack() as ctx:
        def sb(name, shape, dt=F32):
            return ctx.enter_context(nc.sbuf_tensor(name, shape, dt))

        def sem(name):
            return pool.new(name)

        NB = 2
        cat = sb("cat", [P, NB, TPG, D])
        xT = sb("cT", [DC + 1, 2, 2, GT])
        tp = ctx.enter_context(nc.psum_tensor("tp", [P, NB, 2, 512], F32))
        op = ctx.enter_context(nc.psum_tensor("op", [P, NB, 2, 512], F32))
        s_in = [sem("o_in0"), sem("o_in1")]
        s_dve, s_T, s_xT0, s_xT1, s_o, s_h, s_one = [sem(f"o_{x}") for x in ("dve", "T", "xT0", "xT1", "o", "h", "one")]
        block = ctx.enter_context(nc.Block())
        rows = scratch.rearrange("(t i) h l d -> t (i h l d)", i=2).rearrange("t (p e) -> p t e", e=D)

        @block.sync
        def _(sp):
            sp.sem_inc(s_T, NB * 2)
            with sp.Fori(0, GROUPS // NB) as i:
                for b in range(NB):
                    sp.wait_ge(s_T, (i * NB + b) * 2 + 2)
                    sp.dma_start(cat[:, b], rows[:, bass.ds((i * NB + b) * TPG, TPG), :]).then_inc(s_in[b], 16)

        @block.tensor
        def _(pe):
            wo = weight(c, "po")
            pe.wait_ge(s_one, 1)
            with pe.Fori(0, GROUPS // NB) as i:
                for b in range(NB):
                    g = i * NB + b
                    pe.wait_ge(s_in[b], i * 16 + 16)
                    for cc in range(2):
                        for j in range(TPG):
                            mm = nc.tensor.transpose(tp[0:DC, b, cc, j * P:(j + 1) * P], cat[:, b, j, cc * DC:(cc + 1) * DC],
                                                     c.ident[:, :])
                        mm.then_inc(s_T, 1)
                    pe.wait_ge(s_xT0, g + 1)
                    pe.wait_ge(s_xT1, g + 1)
                    pe.wait_ge(s_h, g * 2 + 2)
                    for j in range(TPG):
                        o = op[:, b, j // 2, (j % 2) * D:(j % 2 + 1) * D]
                        nc.tensor.matmul(o, xT[:, b, 0, j * P:(j + 1) * P], wo[:, 0, :], start=True, stop=False)
                        mm = nc.tensor.matmul(o, xT[0:DC, b, 1, j * P:(j + 1) * P], wo[0:DC, 1, :], start=False, stop=True)
                        if j % 2:
                            mm.then_inc(s_o, 1)

        @block.scalar
        def _(act):
            act.wait_ge(s_one, 1)
            with act.Fori(0, GROUPS // NB) as i:
                for b in range(NB):
                    act.wait_ge(s_T, (i * NB + b) * 2 + NB * 2 + 1)
                    nc.scalar.activation(xT[0:DC, b, 0, :], tp[0:DC, b, 0, :], ACT.Copy).then_inc(s_xT0, 1)

        @block.vector
        def _(dve):
            nc.vector.memset(xT[DC:DC + 1, :, 0, :], 1.0).then_inc(s_one, 1)
            dve.sem_inc(s_h, 2 * NB)
            with dve.Fori(0, GROUPS // NB) as i:
                for b in range(NB):
                    g = i * NB + b
                    dve.wait_ge(s_T, g * 2 + NB * 2 + 2)
                    nc.vector.tensor_scalar(xT[0:DC, b, 1, :], tp[0:DC, b, 1, :], 1.0, None, ALU.mult).then_inc(s_xT1, 1)
                    for j in range(TPG):
                        if j % 2 == 0:
                            dve.wait_ge(s_o, g * 2 + j // 2 + 1)
                        ins = nc.vector.tensor_tensor(tile_view(c.h, g, j), op[:, b, j // 2, (j % 2) * D:(j % 2 + 1) * D],
                                                      tile_view(c.h, g, j), ALU.add)
                        if j % 2:
                            ins.then_inc(s_h, 1)



def attention(nc, c, names, gain, shift, mixing, qk_rows, v_rows):
    wq, wk, wv, wo = (weight(c, x) for x in names)
    wm = weight(c, "mm")
    VW = D + 1 if mixing else D
    tag = "m" if mixing else "a"
    with Semaphores(nc) as pool, ExitStack() as ctx:
        def sb(name, shape, dt=F32):
            return ctx.enter_context(nc.sbuf_tensor(tag + "_" + name, shape, dt))

        def sem(name):
            return pool.new(tag + "_" + name)

        N17 = DH + 1
        PAIR = HEADS // 2
        n = sb("n", [P, 2, TPG, D])
        xT = sb("xT", [DC + 1, 2, 2, GT])
        qkT = sb("qkT", [DC, 2, 4, GT])
        vv = sb("vv", [P, 2, TPG, HEADS * N17])
        qt = sb("qt", [DC, 2, 2, P])
        k6 = sb("k6", [DC, 2, 2, PAIR, P])
        vt = sb("vt", [P, 2, HEADS, N17])
        mx = sb("mx", [P, HEADS])
        sc = sb("sc", [P, HEADS, SEQ])
        prob = sb("prob", [P, 2, HEADS, P])
        pT = sb("pT", [P, HEADS, P])
        den = sb("den", [P, HEADS])
        ao = sb("ao", [P, 2, HEADS, DH])
        aT = sb("aT", [DC + 1, 2, P])
        banks = ctx.enter_context(nc.psum_tensor(tag + "_banks", [P, 8, 512], F32))
        T, Q, V = banks[:, 0:2], banks[:, 2:6], banks[:, 6:8]
        S, TP, O, AT, R = banks[:, 0:2, 0:PAIR * SEQ], banks[:, 2:5], banks[:, 5], banks[0:DC, 6, 0:2 * P], banks[:, 7, 0:D]
        o_he = O[:, 0:HEADS * N17].rearrange("p (h e) -> p h e", e=N17)
        if mixing:
            es, score, share, ssum, rank, nsel = (sb(x, [P, TPG]) for x in ("es", "score", "share", "ssum", "rank", "nsel"))
            sel = sb("sel", [P, TILES])
            pm = sb("pm", [P, TPG, D])
            spread, sT, mixer, before = (sb(x, [P, TPG, P]) for x in ("spread", "sT", "mixer", "before"))
            mixed = sb("mixed", [P, TPG, D])
            s_pm, s_pms, s_es, s_score, s_tot, s_mixer, s_mix, s_mixed, s_links = [
                sem(x) for x in ("pm", "pms", "es", "score", "tot", "mixer", "mix", "mixed", "links")]
        s_dve, s_var, s_log, s_guess = [sem(x) for x in ("dve", "var", "log", "guess")]
        s_n, s_T, s_xT, s_q, s_qs, s_v, s_vs, s_ready, s_zero = [sem(x) for x in ("n", "T", "xT", "q", "qs", "v", "vs", "ready", "zero")]
        s_sq, s_sv, s_lq, s_lv = [[sem(f"{x}{b}") for b in range(2)] for x in ("sq", "sv", "lq", "lv")]
        s_S, s_max, s_sub, s_exp, s_tr, s_pT, s_o, s_den, s_ao, s_at, s_aT, s_out, s_x = [
            sem(x) for x in ("S", "max", "sub", "exp", "tr", "pT", "o", "den", "ao", "at", "aT", "out", "x")]
        block = ctx.enter_context(nc.Block())
        LAST = TILES + 4

        def inner(t):
            return not isinstance(t, int)

        def at_work(t, lag):
            return inner(t) or lag <= t < TILES + lag

        def steps(eng, step):
            for t in range(6):
                step(t, t % 2)
            with eng.Fori(3, TILES // 2) as i:
                for p in range(2):
                    step(i * 2 + p, p)
            for t in range(TILES, LAST):
                step(t, t % 2)

        def groups(eng, group):
            group(0, 0, False)
            group(1, 1, False)
            with eng.Fori(1, GROUPS // 2 - 1) as i:
                for b in range(2):
                    group(i * 2 + b, b, False)
            group(GROUPS - 2, 0, False)
            group(GROUPS - 1, 1, True)

        @block.sync
        def _(sp):
            for b in range(2):
                sp.sem_inc(s_sq[b], 16)
                sp.sem_inc(s_sv[b], 16)
            with sp.Fori(0, GROUPS // 2) as i:
                for b in range(2):
                    g = i * 2 + b
                    sp.wait_ge(s_qs, g * 4 + 4)
                    sp.dma_start(qk_rows[:, :, bass.ds(g * GT, GT)], qkT[:, b]).then_inc(s_sq[b], 16)
                    sp.wait_ge(s_vs, g * 2 + 2)
                    sp.dma_start(v_rows[:, bass.ds(g * TPG, TPG), :], vv[:, b]).then_inc(s_sv[b], 16)
            for b in range(2):
                sp.wait_ge(s_sq[b], GROUPS // 2 * 16 + 16)
                sp.wait_ge(s_sv[b], GROUPS // 2 * 16 + 16)
            sp.wait_ge(s_zero, 2)

            def load(t, p):
                sp.dma_start(qt[:, p], qk_rows[:, 0:2, bass.ds(t * P, P)]).then_inc(s_lq[p], 16)
                for m in range(PAIR):
                    rows = slice(m * DH, (m + 1) * DH)
                    sp.dma_start(k6[rows, p, :, m, :], qk_rows[rows, 2:4, bass.ds(t * P, P)]).then_inc(s_lq[p], 16)

            def load_v(t, p):
                sp.dma_start(vt[:, p].rearrange("p h e -> p (h e)"),
                             v_rows[:, bass.ds(t, 1), :].rearrange("p a e -> p (a e)")).then_inc(s_lv[p], 16)

            for p in range(2):
                load(p, p)
                load_v(p, p)
            for t in range(2, 4):
                sp.wait_ge(s_S, t - 1)
                load(t, t % 2)
            with sp.Fori(2, TILES // 2) as i:
                for p in range(2):
                    t = i * 2 + p
                    sp.wait_ge(s_S, t - 1)
                    load(t, p)
                    sp.wait_ge(s_o, t - 3)
                    load_v(t - 2, p)
            for t in range(TILES - 2, TILES):
                sp.wait_ge(s_o, t - 1)
                load_v(t, t % 2)
            for p in range(2):
                sp.wait_ge(s_lv[p], TILES // 2 * 16)
                sp.wait_ge(s_lq[p], TILES // 2 * 16 * (PAIR + 1))

        @block.gpsimd
        def _(gp):
            nc.gpsimd.memset(prob[:, :, :, :], 0.0).then_inc(s_zero, 1)
            nc.gpsimd.memset(k6[:, :, :, :, :], 0.0).then_inc(s_zero, 1)
            gp.wait_ge(s_zero, 2)

        @block.vector
        def _(dve):
            own = Count(s_dve)
            token_stats(nc, dve, c, own.link, c.h)
            norm_factors_dve(nc, dve, c, own.link, s_var, s_guess, twice=True)
            own.link(dve, nc.vector.memset(vv[:, :, :, :].rearrange("p b j (h e) -> p (b j h) e", e=N17)[:, :, DH:N17], 1.0))
            own.link(dve, nc.vector.memset(xT[DC:DC + 1, :, 0, :], 1.0))
            own.link(dve, nc.vector.memset(aT[DC:DC + 1, 0, :], 1.0))
            done = own.n

            def rows(g, b):
                for j in range(TPG):
                    nc.vector.tensor_scalar(n[:, b, j, :], tile_view(c.h, g, j), factor(c, 2, g, j), factor(c, 3, g, j),
                                            ALU.mult, ALU.add).then_inc(s_n, 1)

            def routing(g, own):
                for b in range(2):
                    dve.wait_ge(s_pm, g * 2 + b + 1)
                    nc.vector.tensor_scalar(pm[:, 2 * b:2 * b + 2, :].rearrange("p a d -> p (a d)"), T[:, b, 0:2 * D], 1.0,
                                            None, ALU.mult).then_inc(s_pms, 1)
                dve.wait_ge(s_es, g * 2 + 2)
                own.link(dve, nc.vector.tensor_scalar(score[:, :], es[:, :], 1.0, None, ALU.add))
                own.link(dve, nc.vector.reciprocal(score[:, :], score[:, :]))
                own.link(dve, nc.vector.tensor_tensor(
                    spread[:, :, :], score[:, :].rearrange("p (j o) -> p j o", o=1).broadcast_to([P, TPG, P]),
                    c.ones[:, :].rearrange("p (o k) -> p o k", o=1).broadcast_to([P, TPG, P]), ALU.mult))
                dve.sem_inc(s_score, 1)
                dve.wait_ge(s_tot, g + 1)
                own.link(dve, nc.vector.tensor_scalar(ssum[:, :], T[:, 0, 0:TPG], POOL_EPS, None, ALU.add))
                own.link(dve, nc.vector.reciprocal(ssum[:, :], ssum[:, :]))
                own.link(dve, nc.vector.tensor_tensor(share[:, :], score[:, :], ssum[:, :], ALU.mult))
                own.link(dve, nc.vector.tensor_scalar(sT[:, :, :].rearrange("p j k -> p (j k)"), T[:, 1, :], 1.0, None,
                                                      ALU.mult))
                for j in range(TPG):
                    one = score[:, j:j + 1]
                    nc.vector.scalar_tensor_tensor(out=before[:, j, :], in0=sT[:, j, :], scalar=one,
                                                   in1=c.same[:, :], op0=ALU.is_lt, op1=ALU.mult)
                    nc.vector.scalar_tensor_tensor(out=spread[:, j, :], in0=sT[:, j, :], scalar=one,
                                                   in1=c.lower[:, :], op0=ALU.is_equal, op1=ALU.mult)
                    own.link(dve, nc.vector.scalar_tensor_tensor(out=mixer[:, j, :], in0=sT[:, j, :], scalar=share[:, j:j + 1],
                                                                 in1=c.same[:, :], op0=ALU.mult, op1=ALU.mult))
                own.link(dve, nc.vector.tensor_tensor(mixer[:, :, :], mixer[:, :, :], c.ident[:, :].rearrange(
                    "p (o k) -> p o k", o=1).broadcast_to([P, TPG, P]), ALU.add))
                dve.sem_inc(s_mixer, 1)
                own.link(dve, nc.vector.tensor_tensor(before[:, :, :], before[:, :, :], spread[:, :, :], ALU.add))
                own.link(dve, nc.vector.tensor_reduce(rank[:, :], before[:, :, :], AX.X, ALU.add))
                own.link(dve, nc.vector.tensor_scalar(sel[:, bass.ds(g * TPG, TPG)], rank[:, :], ROUTED - 0.5, None, ALU.is_lt))
                own.link(dve, nc.vector.tensor_scalar(nsel[:, :], rank[:, :], ROUTED - 0.5, None, ALU.is_gt))

            def mix_in(g):
                own = Count(s_links, g * (TPG + 2))
                for j in range(TPG):
                    if j % 2 == 0:
                        dve.wait_ge(s_mix, g * 2 + j // 2 + 1)
                    own.link(dve, nc.vector.tensor_scalar(mixed[:, j, :], T[:, j // 2, (j % 2) * D:(j % 2 + 1) * D],
                                                          nsel[:, j:j + 1], None, ALU.mult))
                    if j % 2:
                        dve.sem_inc(s_mixed, 1)
                here = bass.ds(g * TPG, TPG)
                own.link(dve, nc.vector.tensor_tensor(c.x1[:, here, :], c.x1[:, here, :], mixed[:, :, :], ALU.add))
                own.link(dve, nc.vector.tensor_tensor(c.h[:, here, :], c.h[:, here, :], mixed[:, :, :], ALU.add))

            per_group = 2 + (16 if mixing else 0)

            def group(g, b, last):
                own = Count(s_dve, g * per_group + done)
                if not last:
                    rows(g + 1, 1 - b)
                dve.wait_ge(s_sq[b], (g - b) * 8 + 16)
                for i in range(2):
                    dve.wait_ge(s_q, g * 4 + i + 1)
                    nc.vector.tensor_scalar(qkT[:, b, i, :], Q[0:DC, i, :], 1.0, None, ALU.mult).then_inc(s_qs, 1)
                if mixing and (inner(g) or g > 0):
                    mix_in(g - 1)
                for j in range(TPG):
                    ins = nc.vector.tensor_scalar(tile_view(c.x1, g, j), tile_view(c.h, g, j), factor(c, 0, g, j),
                                                  factor(c, 1, g, j), ALU.mult, ALU.add)
                own.link(dve, ins)
                here = bass.ds(g * TPG, TPG)
                own.link(dve, nc.vector.tensor_tensor(c.h[:, here, :], c.h[:, here, :], c.x1[:, here, :], ALU.add))
                if mixing:
                    routing(g, own)
                assert own.n == per_group, own.n

            rows(0, 0)
            groups(dve, group)
            if mixing:
                mix_in(GROUPS - 1)
            dve.wait_ge(s_qs, GROUPS * 4)
            dve.wait_ge(s_vs, GROUPS * 2)
            dve.wait_ge(s_zero, 2)
            dve.sem_inc(s_ready, 1)

            def step(t, p):
                if at_work(t, 0):
                    view = S.rearrange("p c (m k) -> p c m k", m=PAIR)
                    dve.wait_ge(s_S, t + 1)
                    nc.vector.tensor_reduce(mx[:, :].rearrange("p (c m) -> p c m", c=2), view, AX.X, ALU.max).then_inc(s_max, 1)
                    dve.wait_ge(s_max, t + 1)
                    if inner(t) or t >= 1:
                        dve.wait_ge(s_exp, t * 2)
                    nc.vector.tensor_tensor(sc[:, :, :].rearrange("p (c m) k -> p c m k", c=2), view,
                                            mx[:, :].rearrange("p (c m o) -> p c m o", c=2, o=1).broadcast_to([P, 2, PAIR, SEQ]),
                                            ALU.subtract).then_inc(s_sub, 1)
                if at_work(t, 2):
                    dve.wait_ge(s_o, t - 1)
                    nc.vector.reciprocal(den[:, :], o_he[:, :, DH]).then_inc(s_den, 1)
                    dve.wait_ge(s_den, t - 1)
                    nc.vector.tensor_tensor(ao[:, p], o_he[:, :, 0:DH],
                                            den[:, :].rearrange("p (h o) -> p h o", o=1).broadcast_to([P, HEADS, DH]),
                                            ALU.mult).then_inc(s_ao, 1)
                if at_work(t, 4):
                    dve.wait_ge(s_out, t - 3)
                    for x in (c.x1, c.h):
                        here = x[:, bass.ds(t - 4, 1), :].rearrange("p a d -> p (a d)")
                        if mixing:
                            ins = nc.vector.scalar_tensor_tensor(out=here, in0=R, scalar=sel[:, bass.ds(t - 4, 1)], in1=here,
                                                                 op0=ALU.mult, op1=ALU.add)
                        else:
                            ins = nc.vector.tensor_tensor(here, R, here, ALU.add)
                    ins.then_inc(s_x, 1)

            steps(dve, step)

        @block.scalar
        def _(act):
            nc.scalar.preload_act_table_set(LOG_EXP)
            norm_factors_act(nc, act, c, s_var, s_log, s_guess, twice=True)

            def turned(g, b):
                for cc in range(2):
                    act.wait_ge(s_T, g * 2 + cc + 1)
                    nc.scalar.activation(xT[0:DC, b, cc, :], T[0:DC, cc, :], ACT.Identity, scale=col(c, gain)[0:DC, cc:cc + 1],
                                         bias=col(c, shift)[0:DC, cc:cc + 1]).then_inc(s_xT, 1)

            def group(g, b, last):
                act.wait_ge(s_sq[b], (g - b) * 8 + 16)
                for i in range(2, 4):
                    act.wait_ge(s_q, g * 4 + i + 1)
                    nc.scalar.activation(qkT[:, b, i, :], Q[0:DC, i, :], ACT.Copy).then_inc(s_qs, 1)
                if not last:
                    turned(g + 1, 1 - b)
                act.wait_ge(s_sv[b], (g - b) * 8 + 16)
                for a in range(2):
                    act.wait_ge(s_v, g * 2 + a + 1)
                    src = V[:, a, 0:2 * VW].rearrange("p (j w) -> p j w", j=2)
                    if mixing:
                        nc.scalar.activation(es[:, 2 * a:2 * a + 2], src[:, :, D], ACT.Exp, scale=-1.0).then_inc(s_es, 1)
                    nc.scalar.activation(vv[:, b, 2 * a:2 * a + 2, :].rearrange("p j (h e) -> p j h e", e=N17)[:, :, :, 0:DH],
                                         src[:, :, 0:D].rearrange("p j (h d) -> p j h d", d=DH), ACT.Copy).then_inc(s_vs, 1)

            turned(0, 0)
            groups(act, group)

            def step(t, p):
                if at_work(t, 0):
                    act.wait_ge(s_sub, t + 1)
                    for i in range(2):
                        rows = slice(i * SEQ, (i + 1) * SEQ)
                        nc.scalar.activation(prob[rows, p, :, rows], sc[rows], ACT.Exp,
                                             scale=float(DH) ** -0.5).then_inc(s_exp, 1)
                if at_work(t, 3):
                    act.wait_ge(s_at, t - 2)
                    nc.scalar.activation(aT[0:DC], AT.rearrange("p (c k) -> p c k", c=2), ACT.Copy).then_inc(s_aT, 1)
                if at_work(t, 1):
                    act.wait_ge(s_tr, t)
                    if inner(t) or t >= 2:
                        act.wait_ge(s_o, t - 1)
                    nc.scalar.activation(pT[:, :, :].rearrange("p (b s) m -> p b (s m)", b=3), TP, ACT.Copy).then_inc(s_pT, 1)

            steps(act, step)

        @block.tensor
        def _(pe):
            def turn(g, b):
                pe.wait_ge(s_n, (g + 1) * TPG)
                for cc in range(2):
                    for j in range(TPG):
                        mm = nc.tensor.transpose(T[0:DC, cc, j * P:(j + 1) * P], n[:, b, j, cc * DC:(cc + 1) * DC], c.ident[:, :])
                    mm.then_inc(s_T, 1)

            def group(g, b, last):
                pe.wait_ge(s_xT, g * 2 + 2)
                if inner(g) or g > 0:
                    pe.wait_ge(s_qs, g * 4)
                for i in range(4):
                    w = (wq if i < 2 else wk)[:, :, (i % 2) * DC:(i % 2 + 1) * DC]
                    nc.tensor.matmul(Q[0:DC, i, :], w[:, 0, :], xT[:, b, 0, :], start=True, stop=False)
                    nc.tensor.matmul(Q[0:DC, i, :], w[0:DC, 1, :], xT[0:DC, b, 1, :], start=False, stop=True).then_inc(s_q, 1)
                if mixing and (inner(g) or g > 0):
                    mix(g - 1)
                    pe.wait_ge(s_mixed, g * 2)
                if not last:
                    turn(g + 1, 1 - b)
                if inner(g) or g > 0:
                    pe.wait_ge(s_vs, g * 2)
                for a in range(2):
                    for jj in range(2):
                        j = 2 * a + jj
                        o = V[:, a, jj * VW:(jj + 1) * VW]
                        nc.tensor.matmul(o, xT[:, b, 0, j * P:(j + 1) * P], wv[:, 0, :], start=True, stop=False)
                        mm = nc.tensor.matmul(o, xT[0:DC, b, 1, j * P:(j + 1) * P], wv[0:DC, 1, :], start=False, stop=True)
                    mm.then_inc(s_v, 1)
                if mixing:
                    if not last:
                        pe.wait_ge(s_xT, g * 2 + 4)
                    for a in range(2):
                        for jj in range(2):
                            j = 2 * a + jj
                            o = T[:, a, jj * D:(jj + 1) * D]
                            nc.tensor.matmul(o, xT[0:DC, b, 0, j * P:(j + 1) * P], wm[0:DC, 0, :], start=True, stop=False)
                            mm = nc.tensor.matmul(o, xT[0:DC, b, 1, j * P:(j + 1) * P], wm[0:DC, 1, :], start=False, stop=True)
                        mm.then_inc(s_pm, 1)
                    pe.wait_ge(s_pms, g * 2 + 2)
                    pe.wait_ge(s_score, g + 1)
                    nc.tensor.matmul(T[:, 0, 0:TPG], c.same[:, :], score[:, :], start=True, stop=True)
                    for j in range(TPG):
                        mm = nc.tensor.transpose(T[:, 1, j * P:(j + 1) * P], spread[:, j, :], c.ident[:, :])
                    mm.then_inc(s_tot, 1)

            def mix(g):
                pe.wait_ge(s_mixer, g + 1)
                for j in range(TPG):
                    o = T[:, j // 2, (j % 2) * D:(j % 2 + 1) * D]
                    nc.tensor.matmul(o, mixer[:, j, :], pm[:, j, :], start=True, stop=False)
                    mm = nc.tensor.matmul(o, c.ones[0:1, :], c.rowp[0:1, ROWP_BM:ROWP_BM + D], start=False, stop=True)
                    if j % 2:
                        mm.then_inc(s_mix, 1)

            turn(0, 0)
            groups(pe, group)
            if mixing:
                mix(GROUPS - 1)
            pe.wait_ge(s_ready, 1)

            def step(t, p):
                if at_work(t, 0):
                    pe.wait_ge(s_lq[p], (t - p) * (8 * (PAIR + 1)) + 16 * (PAIR + 1))
                    if inner(t) or t >= 1:
                        pe.wait_ge(s_sub, t)
                    for cc in range(2):
                        for i in range(2):
                            keys = slice(i * SEQ, (i + 1) * SEQ)
                            mm = nc.tensor.matmul(S[keys, cc, :].rearrange("p (m k) -> p m k", m=PAIR), qt[:, p, cc, keys],
                                                  k6[:, p, cc, :, keys], start=True, stop=True)
                    mm.then_inc(s_S, 1)
                if at_work(t, 1):
                    pe.wait_ge(s_exp, t * 2)
                    if inner(t) or t >= 2:
                        pe.wait_ge(s_pT, t - 1)
                    for h in range(HEADS):
                        mm = nc.tensor.transpose(TP[:, h // 4, (h % 4) * P:(h % 4 + 1) * P], prob[:, 1 - p, h, :], c.ident[:, :])
                    mm.then_inc(s_tr, 1)
                if at_work(t, 2):
                    pe.wait_ge(s_pT, t - 1)
                    pe.wait_ge(s_lv[p], (t - p) * 8)
                    if inner(t) or t >= 3:
                        pe.wait_ge(s_ao, t - 2)
                    for cc in range(2):
                        for m in range(PAIR):
                            h = 4 * (m // 2) + 2 * cc + m % 2
                            mm = nc.tensor.matmul(o_he[:, h, :], pT[:, cc * PAIR + m, :], vt[:, p, h, :], start=True, stop=True)
                    mm.then_inc(s_o, 1)
                if at_work(t, 4):
                    pe.wait_ge(s_aT, t - 3)
                    if inner(t) or t >= 5:
                        pe.wait_ge(s_x, t - 4)
                    nc.tensor.matmul(R, aT[:, 0, :], wo[:, 0, :], start=True, stop=False)
                    nc.tensor.matmul(R, aT[0:DC, 1, :], wo[0:DC, 1, :], start=False, stop=True).then_inc(s_out, 1)
                if at_work(t, 3):
                    pe.wait_ge(s_ao, t - 2)
                    if inner(t) or t >= 4:
                        pe.wait_ge(s_aT, t - 3)
                    for cc in range(2):
                        mm = nc.tensor.transpose(AT[:, cc * P:(cc + 1) * P],
                                                 ao[:, 1 - p].rearrange("p h d -> p (h d)")[:, cc * DC:(cc + 1) * DC], c.ident[:, :])
                    mm.then_inc(s_at, 1)

            steps(pe, step)



def experts(nc, c, e1, e2, eb2, xs, ys):
    with Semaphores(nc) as pool, ExitStack() as ctx:
        def sb(name, shape, dt=F32):
            return ctx.enter_context(nc.sbuf_tensor("e_" + name, shape, dt))

        def sem(name):
            return pool.new("e_" + name)

        def ps(name, shape):
            return ctx.enter_context(nc.psum_tensor("e_" + name, shape, F32))

        NB = 3
        ST = SLOT // P
        ZR = 13
        QUARTERS = 4
        second = sb("second", [P, TILES, D])
        room = second[:, :, :].rearrange("p t d -> p (t d)")
        zero = room[:, 0:ZR * D]
        n = room[:, ZR * D:(ZR + 2 * TPG) * D].rearrange("p (b j d) -> p b j d", b=2, d=D)
        cmp1 = room[:, (ZR + 2 * TPG) * D:(ZR + 2 * TPG) * D + TILES * EXPERTS * EXPERTS].rearrange("p (t k) -> p t k", t=TILES)
        xT = sb("xT", [DC + 1, 2, 2, GT])
        logit = sb("logit", [P, TILES, EXPERTS])
        ex = sb("ex", [P, TILES, EXPERTS])
        top = sb("top", [P, TILES])
        cmp2 = sb("cmp2", [P, TILES, EXPERTS * EXPERTS])
        rank = sb("rank", [P, TILES, EXPERTS])
        pick = sb("pick", [P, 3, TILES, EXPERTS])
        tmp = sb("tmp", [P, TILES, EXPERTS])
        total = sb("total", [P, EXPERTS, TILES])
        inc = sb("inc", [P, EXPERTS, TILES])
        pos = sb("pos", [P, EXPERTS, TILES])
        full = sb("full", [P, EXPERTS, TOKENS // SLOT])
        tiles = sb("tiles", [P, EXPERTS])
        ends = sb("ends", [P, EXPERTS])
        base = sb("base", [P, EXPERTS])
        gate = sb("gate", [P, 2, TILES])
        place = sb("place", [P, 2, TILES])
        place32 = sb("place32", [P, 2, TILES], mybir.dt.int32)
        owner = sb("owner", [1, SLOTS, EXPERTS])
        owned = sb("owned", [1, SLOTS])
        owned32 = sb("owned32", [1, SLOTS], mybir.dt.int32)
        before = sb("before", [P, P])
        w1 = sb("w1", [DC, NB, 2, FF])
        w2 = sb("w2", [P, NB, FC * D + FC])
        b2 = sb("b2", [P, NB, D])
        xin = sb("xin", [P, NB, ST, D])
        sT = sb("sT", [DC, NB, 2, SLOT])
        hT = sb("hT", [P, FC, SLOT])
        y = sb("y", [P, NB, ST, D])
        H, T, O = ps("H", [P, FC, 512]), ps("T", [P, 512]), ps("O", [P, 512])
        s_dve, s_var, s_log, s_guess = [sem(x) for x in ("dve", "var", "log", "guess")]
        s_zero, s_zeroed, s_before, s_n, s_T, s_xTa, s_xTd = [sem(x) for x in ("zero", "zeroed", "before", "n", "T", "xTa", "xTd")]
        s_lg, s_z, s_ex, s_pick, s_count, s_place, s_owned = [sem(x) for x in ("lg", "z", "ex", "pick", "count", "place", "owned")]
        s_sent = sem("sent")
        s_x, s_w, s_out = [[sem(f"{x}{b}") for b in range(NB)] for x in ("x", "w", "out")]
        s_turn, s_sT, s_up, s_gelu, s_down, s_y = [sem(x) for x in ("turn", "sT", "up", "gelu", "down", "y")]
        s_back = [sem(f"back{q}") for q in range(QUARTERS)]
        s_h = sem("h")
        block = ctx.enter_context(nc.Block())
        slot_rows = xs.rearrange("(s t p) d -> s p t d", t=ST, p=P)
        result_rows = ys.rearrange("(s t p) d -> s p t d", t=ST, p=P)

        @block.sync
        def _(sp):
            zero_rows = xs.rearrange("(k p r) d -> k p (r d)", p=P, r=ZR)
            sp.wait_ge(s_zero, 1)
            for k in range(SLOTS * ST // ZR):
                sp.dma_start(zero_rows[k], zero).then_inc(s_zeroed, 16)
            sp.wait_ge(s_zeroed, SLOTS * ST // ZR * 16)

            def load(i, b):
                sp.dma_start(xin[:, b], slot_rows[bass.ds(i, 1)].rearrange("a p t d -> p (a t) d")).then_inc(s_x[b], 16)
                e = sp.value_load(owned32[0:1, bass.ds(i, 1)], min_val=0, max_val=EXPERTS - 1)
                sp.dma_start(w1[:, b], e1[bass.ds(e, 1)].rearrange("a p c f -> p (a c) f")).then_inc(s_w[b], 16)
                sp.dma_start(w2[:, b], e2[bass.ds(e, 1)].rearrange("a p f -> p (a f)")).then_inc(s_w[b], 16)
                sp.dma_start(b2[:, b], eb2[bass.ds(e, 1)].broadcast_to([P, D])).then_inc(s_w[b], 16)

            def store(i, b):
                sp.dma_start(result_rows[bass.ds(i, 1)].rearrange("a p t d -> p (a t) d"), y[:, b]).then_inc(s_out[b], 16)

            sp.wait_ge(s_owned, 1)
            sp.wait_ge(s_sent, TILES * 2 * 16)
            for b in range(NB):
                load(b, b)
            with sp.Fori(0, SLOTS // NB - 1) as r:
                for b in range(NB):
                    sp.wait_ge(s_y, r * NB + b + 1)
                    load(r * NB + (b + NB), b)
                    store(r * NB + b, b)
            for b in range(NB):
                sp.wait_ge(s_y, SLOTS - NB + b + 1)
                sp.dma_start(result_rows[SLOTS - NB + b], y[:, b]).then_inc(s_out[b], 16)
            for b in range(NB):
                sp.wait_ge(s_out[b], SLOTS // NB * 16 + 16)

        @block.gpsimd
        def _(gp):
            nc.gpsimd.affine_select(out=before[:, :], in_=c.ones[:, :], compare_op=ALU.is_gt, fill=0.0,
                                    base=0, pattern=[[1, P]], channel_multiplier=-1).then_inc(s_before, 1)
            gp.wait_ge(s_zeroed, SLOTS * ST // ZR * 16)
            gp.wait_ge(s_place, 1)
            for t in range(TILES):
                for k in range(2):
                    nc.gpsimd.indirect_dma_start(xs, bass.IndirectOffsetOnAxis(place32[:, k, t:t + 1], 0),
                                                 c.x1[:, t, :], None).then_inc(s_sent, 16)
            gp.wait_ge(s_sent, TILES * 2 * 16)
            for b in range(NB):
                gp.wait_ge(s_out[b], SLOTS // NB * 16 + 16)
            for t in range(TILES):
                for k in range(2):
                    nc.gpsimd.indirect_dma_start((second if k else c.x1)[:, t, :], None, ys,
                                                 bass.IndirectOffsetOnAxis(place32[:, k, t:t + 1], 0)
                                                 ).then_inc(s_back[t // (TILES // QUARTERS)], 16)

        @block.vector
        def _(dve):
            own = Count(s_dve)
            nc.vector.memset(zero, 0.0).then_inc(s_zero, 1)
            token_stats(nc, dve, c, own.link, c.x1)
            norm_factors_dve(nc, dve, c, own.link, s_var, s_guess, twice=False)
            own.link(dve, nc.vector.memset(xT[DC:DC + 1, :, 0, :], 1.0))
            with dve.Fori(0, GROUPS // 2) as i:
                for b in range(2):
                    g = i * 2 + b
                    for j in range(TPG):
                        nc.vector.tensor_scalar(n[:, b, j, :], tile_view(c.x1, g, j), factor(c, 0, g, j), factor(c, 1, g, j),
                                                ALU.mult, ALU.add).then_inc(s_n, 1)
                for b in range(2):
                    g = i * 2 + b
                    dve.wait_ge(s_n, (g + 1) * TPG)
                    for j in range(TPG):
                        nc.vector.tensor_scalar(tile_view(c.x1, g, j), n[:, b, j, :], 1.0, None, ALU.mult)
                    dve.wait_ge(s_T, g * 2 + 2)
                    nc.vector.tensor_scalar(xT[0:DC, b, 1, :], H[0:DC, 2 * b + 1, :], col(c, "ln2g")[0:DC, 1:2],
                                            col(c, "ln2b")[0:DC, 1:2], ALU.mult, ALU.add).then_inc(s_xTd, 1)
                dve.wait_ge(s_xTd, i * 2 + 2)
            dve.wait_ge(s_lg, GROUPS)
            own.link(dve, nc.vector.tensor_scalar(logit[:, :, :].rearrange("p t e -> p (t e)"), O[:, 0:TILES * EXPERTS], 1.0,
                                                  None, ALU.mult))

            own.link(dve, nc.vector.tensor_reduce(top[:, :], logit[:, :, :], AX.X, ALU.max))
            nc.vector.tensor_tensor(ex[:, :, :], logit[:, :, :],
                                    top[:, :].rearrange("p (t o) -> p t o", o=1).broadcast_to([P, TILES, EXPERTS]),
                                    ALU.subtract).then_inc(s_z, 1)
            shape = [P, TILES, EXPERTS, EXPERTS]
            other = logit[:, :, :].rearrange("p t (o f) -> p t o f", o=1).broadcast_to(shape)
            this = logit[:, :, :].rearrange("p t (e o) -> p t e o", o=1).broadcast_to(shape)
            c1, c2 = (x[:, :, :].rearrange("p t (e f) -> p t e f", e=EXPERTS) for x in (cmp1, cmp2))
            own.link(dve, nc.vector.tensor_tensor(c1, other, this, ALU.is_gt))
            own.link(dve, nc.vector.tensor_tensor(c2, other, this, ALU.is_equal))
            tri = col(c, "tri").rearrange("p (o k) -> p o k", o=1).broadcast_to([P, TILES, EXPERTS * EXPERTS])
            own.link(dve, nc.vector.tensor_tensor(cmp2[:, :, :], cmp2[:, :, :], tri, ALU.mult))
            own.link(dve, nc.vector.tensor_tensor(cmp1[:, :, :], cmp1[:, :, :], cmp2[:, :, :], ALU.add))
            own.link(dve, nc.vector.tensor_reduce(rank[:, :, :], c1, AX.X, ALU.add))
            first, later, both = (pick[:, k] for k in range(3))
            own.link(dve, nc.vector.tensor_scalar(first, rank[:, :, :], 0.5, None, ALU.is_lt))
            own.link(dve, nc.vector.tensor_scalar(both, rank[:, :, :], 1.5, None, ALU.is_lt))
            dve.sem_inc(s_pick, 1)
            own.link(dve, nc.vector.tensor_tensor(later, both, first, ALU.subtract))
            own.link(dve, nc.vector.memset(pos[:, :, :], 1.0))
            own.link(dve, nc.vector.memset(pos[:, :, 0:1], 0.0))

            def te(x):
                return x[:, :, :].rearrange("p e t -> p t e")

            def over(x, n):
                return x[:, :].rearrange("p (e o) -> p e o", o=1).broadcast_to([P, EXPERTS, n])

            def per_tile(x):
                return x.rearrange("p (t e) -> p t e", e=EXPERTS)

            dve.wait_ge(s_count, 1)
            own.link(dve, nc.vector.tensor_scalar(te(total), per_tile(H[:, 1, 0:TILES * EXPERTS]), 1.0, None, ALU.mult))
            own.link(dve, nc.vector.tensor_tensor_scan(inc[:, :, :].rearrange("p e t -> p (e t)"),
                                                       pos[:, :, :].rearrange("p e t -> p (e t)"),
                                                       total[:, :, :].rearrange("p e t -> p (e t)"), 0.0, ALU.mult, ALU.add))
            starts = col(c, "starts").rearrange("p (o k) -> p o k", o=1).broadcast_to([P, EXPERTS, TOKENS // SLOT])
            own.link(dve, nc.vector.tensor_tensor(full[:, :, :], inc[:, :, TILES - 1:TILES].broadcast_to(
                [P, EXPERTS, TOKENS // SLOT]), starts, ALU.is_gt))
            own.link(dve, nc.vector.tensor_reduce(tiles[:, :], full[:, :, :], AX.X, ALU.add))
            own.link(dve, nc.vector.tensor_tensor_scan(ends[:, :], c.ones[:, 0:EXPERTS], tiles[:, :], 0.0, ALU.mult, ALU.add))
            slots = col(c, "slots")[0:1, :].rearrange("p (s o) -> p s o", o=1).broadcast_to([1, SLOTS, EXPERTS])
            own.link(dve, nc.vector.tensor_tensor(owner[:, :, :], slots, ends[0:1, :].rearrange("p (o e) -> p o e", o=1)
                                                  .broadcast_to([1, SLOTS, EXPERTS]), ALU.is_ge))
            own.link(dve, nc.vector.tensor_reduce(owned[:, :], owner[:, :, :], AX.X, ALU.add))
            own.link(dve, nc.vector.tensor_scalar(owned32[:, :], owned[:, :], EXPERTS - 1.0, None, ALU.min))
            dve.sem_inc(s_owned, 1)
            own.link(dve, nc.vector.tensor_tensor(base[:, :], ends[:, :], tiles[:, :], ALU.subtract))
            own.link(dve, nc.vector.tensor_scalar(base[:, :], base[:, :], float(SLOT), None, ALU.mult))
            own.link(dve, nc.vector.tensor_tensor(pos[:, :, :], inc[:, :, :], total[:, :, :], ALU.subtract))
            own.link(dve, nc.vector.tensor_tensor(pos[:, :, :], pos[:, :, :], over(base, TILES), ALU.add))
            own.link(dve, nc.vector.tensor_tensor(te(pos), te(pos), per_tile(H[:, 0, 0:TILES * EXPERTS]), ALU.add))
            for k in range(2):
                own.link(dve, nc.vector.tensor_tensor(tmp[:, :, :], te(pos), pick[:, k], ALU.mult))
                own.link(dve, nc.vector.tensor_reduce(place[:, k], tmp[:, :, :], AX.X, ALU.add))
            own.link(dve, nc.vector.tensor_scalar(place32[:, :, :], place[:, :, :], 1.0, None, ALU.mult))
            dve.sem_inc(s_place, 1)
            dve.wait_ge(s_ex, 1)
            for k in range(2):
                own.link(dve, nc.vector.tensor_tensor(tmp[:, :, :], ex[:, :, :], pick[:, k], ALU.mult))
                own.link(dve, nc.vector.tensor_reduce(gate[:, k], tmp[:, :, :], AX.X, ALU.add))
            own.link(dve, nc.vector.tensor_tensor(top[:, :], gate[:, 0], gate[:, 1], ALU.add))
            own.link(dve, nc.vector.reciprocal(top[:, :], top[:, :]))
            for k in range(2):
                own.link(dve, nc.vector.tensor_tensor(gate[:, k], gate[:, k], top[:, :], ALU.mult))

            def turned(i, b):
                dve.wait_ge(s_turn, i + 1)
                for cc in range(2):
                    nc.vector.tensor_scalar(sT[:, b, cc, :], T[0:DC, cc * SLOT:(cc + 1) * SLOT], col(c, "ln2g")[0:DC, cc:cc + 1],
                                            col(c, "ln2b")[0:DC, cc:cc + 1], ALU.mult, ALU.add).then_inc(s_sT, 1)

            turned(0, 0)
            for b in range(NB):
                dve.sem_inc(s_out[b], 16)

            def finish(i, b, round_):
                dve.wait_ge(s_w[b], (round_ + 1) * 48)
                dve.wait_ge(s_down, (i + 2) * FC)
                dve.wait_ge(s_out[b], round_ * 16 + 16)
                nc.vector.tensor_tensor(y[:, b], O[:, 0:ST * D].rearrange("p (t d) -> p t d", t=ST),
                                        b2[:, b:b + 1, :].broadcast_to([P, ST, D]), ALU.add).then_inc(s_y, 1)

            with dve.Fori(0, SLOTS // NB - 1) as r:
                for b in range(NB):
                    turned(r * NB + (b + 1), (b + 1) % NB)
                    finish(r * NB + b, b, r)
            for b in range(NB):
                if b + 1 < NB:
                    turned(SLOTS - NB + b + 1, b + 1)
                finish(SLOTS - NB + b, b, SLOTS // NB - 1)
            for q in range(QUARTERS):
                dve.wait_ge(s_back[q], TILES // QUARTERS * 2 * 16)
                for k in range(2):
                    src = second if k else c.x1
                    for t in range(q * (TILES // QUARTERS), (q + 1) * (TILES // QUARTERS)):
                        nc.vector.scalar_tensor_tensor(out=c.h[:, t, :], in0=src[:, t, :], scalar=gate[:, k, t:t + 1],
                                                       in1=c.h[:, t, :], op0=ALU.mult, op1=ALU.add).then_inc(s_h, 1)
                    dve.wait_ge(s_h, (q * 2 + k + 1) * (TILES // QUARTERS))

        @block.scalar
        def _(act):
            nc.scalar.preload_act_table_set(LOG_EXP)
            norm_factors_act(nc, act, c, s_var, s_log, s_guess, twice=False)
            with act.Fori(0, GROUPS // 2) as i:
                for b in range(2):
                    act.wait_ge(s_T, i * 4 + 2 * b + 1)
                    nc.scalar.activation(xT[0:DC, b, 0, :], H[0:DC, 2 * b, :], ACT.Identity, scale=col(c, "ln2g")[0:DC, 0:1],
                                         bias=col(c, "ln2b")[0:DC, 0:1]).then_inc(s_xTa, 1)
            act.wait_ge(s_z, 1)
            nc.scalar.activation(ex[:, :, :], ex[:, :, :], ACT.Exp).then_inc(s_ex, 1)
            nc.scalar.preload_act_table(ACT.Gelu)
            act.sem_inc(s_down, FC)
            with act.Fori(0, SLOTS // NB) as r:
                for b in range(NB):
                    i = r * NB + b
                    act.wait_ge(s_w[b], (r + 1) * 48)
                    for f in range(FC):
                        act.wait_ge(s_up, i * FC + f + 1)
                        act.wait_ge(s_down, i * FC + f + 1)
                        nc.scalar.activation(hT[:, f, :], H[:, f, 0:SLOT], ACT.Gelu,
                                             bias=w2[:, b, FC * D + f:FC * D + f + 1]).then_inc(s_gelu, 1)

        @block.tensor
        def _(pe):
            router = weight(c, "router")
            with pe.Fori(0, GROUPS // 2) as i:
                for b in range(2):
                    pe.wait_ge(s_n, (i * 2 + b) * TPG + TPG)
                    for cc in range(2):
                        for j in range(TPG):
                            mm = nc.tensor.transpose(H[0:DC, 2 * b + cc, j * P:(j + 1) * P],
                                                     n[:, b, j, cc * DC:(cc + 1) * DC], c.ident[:, :])
                        mm.then_inc(s_T, 1)
                for b in range(2):
                    g = i * 2 + b
                    pe.wait_ge(s_xTa, g + 1)
                    pe.wait_ge(s_xTd, g + 1)
                    for j in range(TPG):
                        o = O[:, bass.ds((g * TPG + j) * EXPERTS, EXPERTS)]
                        nc.tensor.matmul(o, xT[:, b, 0, j * P:(j + 1) * P], router[:, 0, :], start=True, stop=False)
                        mm = nc.tensor.matmul(o, xT[0:DC, b, 1, j * P:(j + 1) * P], router[0:DC, 1, :], start=False, stop=True)
                    mm.then_inc(s_lg, 1)
            pe.wait_ge(s_before, 1)
            pe.wait_ge(s_pick, 1)
            both = pick[:, 2].rearrange("p t e -> p (t e)")
            nc.tensor.matmul(H[:, 0, 0:TILES * EXPERTS], before[:, :], both, start=True, stop=True)
            nc.tensor.matmul(H[:, 1, 0:TILES * EXPERTS], c.ones[:, :], both, start=True, stop=True).then_inc(s_count, 1)
            pe.wait_ge(s_place, 1)

            def turn(i, b, round_):
                pe.wait_ge(s_x[b], (round_ + 1) * 16)
                if b or not (isinstance(round_, int) and round_ == 0):
                    pe.wait_ge(s_sT, i * 2)
                for cc in range(2):
                    for t in range(ST):
                        mm = nc.tensor.transpose(T[0:DC, cc * SLOT + t * P:cc * SLOT + (t + 1) * P],
                                                 xin[:, b, t, cc * DC:(cc + 1) * DC], c.ident[:, :])
                mm.then_inc(s_turn, 1)

            def slot_tile(i, b, round_, last=False):
                pe.wait_ge(s_w[b], (round_ + 1) * 48)
                pe.wait_ge(s_sT, i * 2 + 2)

                def down(f):
                    pe.wait_ge(s_gelu, i * FC + f + 1)
                    if f == 0 and (b or not isinstance(round_, int) or round_ > 0):
                        pe.wait_ge(s_y, i)
                    for t in range(ST):
                        mm = nc.tensor.matmul(O[:, t * D:(t + 1) * D], hT[:, f, t * P:(t + 1) * P],
                                              w2[:, b, f * D:(f + 1) * D], start=(f == 0 and t == 0), stop=(f == FC - 1),
                                              skip_group_check=True)
                    mm.then_inc(s_down, 1)

                for f in range(FC):
                    for cc in range(2):
                        mm = nc.tensor.matmul(H[:, f, 0:SLOT], w1[:, b, cc, f * P:(f + 1) * P], sT[:, b, cc, :],
                                              start=(cc == 0), stop=(cc == 1))
                    mm.then_inc(s_up, 1)
                    if f == FC - 2 and not last:
                        turn(i + 1, (b + 1) % NB, round_ + (b + 1) // NB)
                    if f >= 1:
                        down(f - 1)
                down(FC - 1)

            turn(0, 0, 0)
            for b in range(NB):
                slot_tile(b, b, 0)
            with pe.Fori(1, SLOTS // NB - 1) as r:
                for b in range(NB):
                    slot_tile(r * NB + b, b, r)
            for b in range(NB):
                slot_tile(SLOTS - NB + b, b, SLOTS // NB - 1, last=(b == NB - 1))



def scan_block(nc, c):
    with Semaphores(nc) as pool, ExitStack() as ctx:
        def sb(name, shape, dt=F32):
            return ctx.enter_context(nc.sbuf_tensor("s_" + name, shape, dt))

        def sem(name):
            return pool.new("scan_" + name)

        W = IC * GT
        IMG = GT // SEQ
        FIRST = 1e30
        n = sb("n", [P, TPG, D])
        n1 = sb("n1", [P, TPG, D])
        xT = sb("xT", [DC, 2, GT])
        xpad = sb("xpad", [P, IC, IMG, SEQ + TAPS - 1])
        even = c.x1[:, :, :].rearrange("p t d -> p (t d)")
        odd = sb("odd", [P, 4 * W])
        xc, sz, delta, u = ([x[:, i * W:(i + 1) * W] for x in (even, odd[:, :])] for i in range(4))
        pre = sb("pre", [P, W])
        soft = sb("soft", [P, W])
        yg = sb("yg", [P, W])
        SC = 2 * STATES
        parts = sb("parts", [3 * SC, 2, GT], BF16)
        rest = sb("rest", [2 * SC, GT])
        dt = sb("dt", [1, GT])
        cs = sb("cs", [P, 1, GT])
        wx = sb("wx", [P, IC, XP])
        pick = sb("pick", [3 * SC, SC], BF16)
        dA = sb("dA", [P, 2, W])
        hs = sb("hs", [P, 2, W])
        hc = sb("hc", [P, 2, W])
        A = sb("A", [P, IC * STATES])
        wo = sb("wo", [P, IC * D])
        part = sb("part", [P, 2])
        scale = sb("scale", [P, 4])
        ss, rs, rt = sb("ss", [P, TPG]), sb("rs", [P, TPG]), sb("rt", [P, TPG])
        banks = ctx.enter_context(nc.psum_tensor("s_banks", [P, 8, 512], F32))
        B, C, Y, X = banks[:, 0:1], banks[:, 1:2], banks[:, 2:5], [banks[:, i] for i in range(5, 8)]
        s_dve, s_dhl, s_dl, s_var, s_log, s_guess = [sem(x) for x in ("dve", "dve_head", "dve_tail", "var", "log", "guess")]
        s_part, s_tot, s_alog, s_A = [sem(x) for x in ("part", "tot", "alog", "A")]
        s_n, s_T, s_xT, s_inx, s_pad, s_conv, s_inz, s_sz, s_xc = [
            sem(x) for x in ("n", "T", "xT", "inx", "pad", "conv", "inz", "sz", "xc")]
        s_dbc, s_dbcs, s_parts, s_dt, s_pre, s_abs, s_soft, s_u, s_n1 = [
            sem(x) for x in ("dbc", "dbcs", "parts", "dt", "pre", "abs", "soft", "u", "n1")]
        s_B, s_C, s_cs, s_dBu, s_dA, s_scan, s_hcu = [sem(x) for x in ("B", "C", "cs", "dBu", "dA", "scan", "hcu")]
        s_hc = [sem("hc_even"), sem("hc_odd")]
        s_yg, s_sq, s_ss, s_v, s_r0, s_rg, s_out, s_h = [sem(x) for x in ("yg", "sq", "ss", "v", "r0", "rg", "out", "h")]
        block = ctx.enter_context(nc.Block())
        win = weight(c, "inproj")

        def chunk(x, i):
            return x[:, i * GT:(i + 1) * GT]

        def inner(g):
            return not isinstance(g, int)

        def all_groups(eng, state, head, tail, start=None, end=None):
            def group(g, b):
                more, before = inner(g) or g + 1 < GROUPS, inner(g) or g > 0
                if more:
                    head(-1, g + 1, 1 - b)
                if start:
                    start(g, b)
                for s in range(STATES):
                    def pieces():
                        if before:
                            tail(s, g - 1, 1 - b)
                        if more:
                            head(s, g + 1, 1 - b)
                    state(s, g, b, pieces)
                if end:
                    end(g, b)

            for k in range(-1, STATES):
                head(k, 0, 0)
            group(0, 0)
            with eng.Fori(0, GROUPS // 2 - 1) as i:
                group(i * 2 + 1, 1)
                group(i * 2 + 2, 0)
            group(GROUPS - 1, 1)
            for k in range(STATES):
                tail(k, GROUPS - 1, 1)

        HALF = STATES // 2

        def wait_used(eng, g, s, done):
            n = s // 2 + (1 if done else 0)
            if inner(g) or g * HALF + n > 0:
                eng.wait_ge(s_hc[s % 2], g * HALF + n)

        def times_c(eng, unit, q, p, c_rows):
            eng.wait_ge(s_scan, q + 3)
            eng.wait_ge(s_hcu, q + 1)
            unit.tensor_tensor(hc[:, p].rearrange("p (i t) -> p i t", i=IC), hs[:, p].rearrange("p (i t) -> p i t", i=IC),
                               c_rows.broadcast_to([P, IC, GT]), ALU.mult).then_inc(s_hc[p], 1)

        @block.gpsimd
        def _(gp):
            with gp.Fori(0, GROUPS) as g:
                for s in range(0, STATES, 2):
                    gp.wait_ge(s_cs, g * (STATES // 2) + s // 2 + 1)
                    times_c(gp, nc.gpsimd, g * STATES + s, 0, cs[:, :, :])

        @block.vector
        def _(dve):
            own = Count(s_dve)
            token_stats(nc, dve, c, own.link, c.h)
            norm_factors_dve(nc, dve, c, own.link, s_var, s_guess, twice=True)
            woraw = col(c, "outproj")
            own.link(dve, nc.vector.memset(part[:, :], 0.0))
            own.link(dve, nc.vector.tensor_reduce(part[0:DC, 0:1], win[0:DC], AX.XY, ALU.add, apply_absolute_value=True))
            own.link(dve, nc.vector.tensor_reduce(part[:, 1:2], woraw, AX.X, ALU.add, apply_absolute_value=True))
            dve.sem_inc(s_part, 1)
            dve.wait_ge(s_tot, 1)
            own.link(dve, nc.vector.tensor_scalar(scale[:, 0:1], X[0][:, 0:1], 1.0 / (2 * INNER * D), 1e-5, ALU.mult, ALU.max))
            own.link(dve, nc.vector.tensor_scalar(scale[:, 1:2], X[0][:, 1:2], 1.0 / (INNER * D), 1e-5, ALU.mult, ALU.max))
            own.link(dve, nc.vector.reciprocal(scale[:, 2:4], scale[:, 0:2]))
            for w, k, m in ((win[0:DC], 2, DC), (woraw, 3, P)):
                own.link(dve, nc.vector.tensor_scalar(w, w, scale[0:m, k:k + 1], 1.0, ALU.mult, ALU.min))
                own.link(dve, nc.vector.tensor_scalar(w, w, -1.0, ROUND, ALU.max, ALU.add))
                own.link(dve, nc.vector.tensor_scalar(w, w, ROUND, None, ALU.subtract))
            for i in range(IC):
                own.link(dve, nc.vector.tensor_scalar(wo[:, i * D:(i + 1) * D], woraw[:, i * D:(i + 1) * D],
                                                      col(c, "onorm")[:, i:i + 1], None, ALU.mult))
            nc.vector.tensor_scalar(A[:, :], col(c, "alog"), -20.0, 2.0, ALU.max, ALU.min).then_inc(s_alog, 1)
            dve.wait_ge(s_A, 1)
            own.link(dve, nc.vector.tensor_scalar(A[:, :], A[:, :], -1.0, None, ALU.mult))
            own.link(dve, nc.vector.memset(xpad[:, :, :, 0:TAPS - 1], 0.0))
            xproj = col(c, "xproj").rearrange("p (i o k) -> p i o k", i=IC, o=1)
            for i in range(IC):
                own.link(dve, nc.vector.tensor_scalar(wx[:, i, 0:3 * SC].rearrange("p (r k) -> p r k", r=3),
                                                      xproj[:, i, :, 1:].broadcast_to([P, 3, SC]), 1.0, None, ALU.mult))
            own.link(dve, nc.vector.tensor_scalar(wx[:, :, 3 * SC], xproj[:, :, 0, 0], 1.0, None, ALU.mult))
            for k in range(3):
                own.link(dve, nc.vector.tensor_scalar(pick[k * SC:(k + 1) * SC, :], c.ident[k * SC:(k + 1) * SC, k * SC:(k + 1) * SC],
                                                      1.0, None, ALU.mult))
            dve.sem_inc(s_part, 1)
            dve.sem_inc(s_scan, 2)
            HEAD_LINKS, TAIL_LINKS = IC * (TAPS - 1) + 3 + 4, 6

            def head(k, g, b):
                links = Count(s_dhl, g * HEAD_LINKS)
                if k == -1:
                    for j in range(TPG):
                        nc.vector.tensor_scalar(n[:, j, :], tile_view(c.h, g, j), factor(c, 2, g, j), factor(c, 3, g, j),
                                                ALU.mult, ALU.add).then_inc(s_n, 1)
                elif 3 <= k < 3 + IC:
                    i = k - 3
                    links.n = i * (TAPS - 1)
                    dve.wait_ge(s_pad, g * IC + i + 1)
                    out = chunk(pre, i).rearrange("p (m t) -> p m t", t=SEQ)
                    for tap in range(TAPS):
                        w = col(c, "conv")[:, i * TAPS + tap:i * TAPS + tap + 1]
                        src = xpad[:, i, :, tap:tap + SEQ]
                        if tap == 0:
                            links.link(dve, nc.vector.tensor_scalar(out, src, w, col(c, "convb")[:, i:i + 1], ALU.mult, ALU.add))
                        else:
                            ins = nc.vector.scalar_tensor_tensor(out=out, in0=src, scalar=w, in1=out, op0=ALU.mult, op1=ALU.add)
                            if tap < TAPS - 1:
                                links.link(dve, ins)
                            else:
                                ins.then_inc(s_conv, 1)
                elif k == 12:
                    links.n = IC * (TAPS - 1)
                    dve.wait_ge(s_dbc, g + 1)
                    nc.vector.tensor_scalar(dt[:, :], X[0][3 * SC:XP, :], 1.0, None, ALU.mult)
                    links.link(dve, nc.vector.tensor_scalar(parts[:, b, :], X[0][0:3 * SC, :], 1.0, None, ALU.mult))
                    links.link(dve, nc.vector.tensor_tensor(rest[:, :], X[0][0:2 * SC, :], parts[0:2 * SC, b, :], ALU.subtract))
                    dve.sem_inc(s_dbcs, 1)
                    links.link(dve, nc.vector.tensor_scalar(parts[0:2 * SC, b, :], rest[:, :], 1.0, None, ALU.mult))
                    links.link(dve, nc.vector.tensor_tensor(rest[0:SC, :], rest[0:SC, :], parts[0:SC, b, :], ALU.subtract))
                    nc.vector.tensor_scalar(parts[0:SC, b, :], rest[0:SC, :], 1.0, None, ALU.mult).then_inc(s_parts, 1)
                elif k == 14:
                    links.n = IC * (TAPS - 1) + 4
                    for j in range(TPG):
                        ins = nc.vector.tensor_scalar(n1[:, j, :], tile_view(c.h, g, j), factor(c, 0, g, j), factor(c, 1, g, j),
                                                      ALU.mult, ALU.add)
                    links.link(dve, ins)
                    here = c.h[:, bass.ds(g * TPG, TPG), :]
                    nc.vector.tensor_tensor(here, here, n1[:, :, :], ALU.add).then_inc(s_n1, 1)
                elif k == 13:
                    for i in range(IC):
                        dve.wait_ge(s_dt, g * IC + i + 1)
                        nc.vector.tensor_scalar(chunk(pre, i), X[i], col(c, "dtb")[:, i:i + 1], None, ALU.add).then_inc(s_pre, 1)
                elif k == 15:
                    links.n = IC * (TAPS - 1) + 5
                    dve.wait_ge(s_soft, g + 1)
                    links.link(dve, nc.vector.scalar_tensor_tensor(out=delta[b], in0=pre[:, :], scalar=0.0, in1=soft[:, :],
                                                                   op0=ALU.max, op1=ALU.add))
                    links.link(dve, nc.vector.tensor_tensor(u[b], delta[b], xc[b], ALU.mult))
                    nc.vector.memset(delta[b].rearrange("p (m t) -> p m t", t=SEQ)[:, :, 0:1], FIRST).then_inc(s_u, 1)

            def state(s, g, b, pieces):
                q, p = g * STATES + s, s % 2
                if s == 0:
                    dve.wait_ge(s_u, g + 1)
                dve.wait_ge(s_B, q + 1)
                wait_used(dve, g, s, False)
                nc.vector.tensor_tensor(hs[:, p].rearrange("p (i t) -> p i t", i=IC), u[b].rearrange("p (i t) -> p i t", i=IC),
                                        B.broadcast_to([P, IC, GT]), ALU.mult).then_inc(s_dBu, 1)
                dve.wait_ge(s_dBu, q + 1)
                dve.wait_ge(s_dA, q * IC + IC)
                nc.vector.tensor_tensor_scan(hs[:, p], dA[:, p], hs[:, p], 0.0, ALU.mult, ALU.add).then_inc(s_scan, 1)
                if s % 2:
                    dve.wait_ge(s_C, q + 1)
                    times_c(dve, nc.vector, q, p, C)
                pieces()

            def end(g, b):
                links = Count(s_dl, g * TAIL_LINKS)
                dve.wait_ge(s_hc[1], (g + 1) * HALF)
                dve.wait_ge(s_hcu, (g + 1) * STATES + 2)
                for i in range(IC):
                    ins = nc.vector.scalar_tensor_tensor(out=chunk(yg, i), in0=chunk(xc[b], i),
                                                         scalar=col(c, "dskip")[:, i:i + 1], in1=Y[:, i, :],
                                                         op0=ALU.mult, op1=ALU.add)
                links.link(dve, ins)
                nc.vector.tensor_tensor(yg[:, :], yg[:, :], sz[b], ALU.mult).then_inc(s_yg, 1)

            def tail(k, g, b):
                links = Count(s_dl, g * TAIL_LINKS)
                if k == 3:
                    links.n = 1
                    dve.wait_ge(s_ss, g + 1)
                    links.link(dve, nc.vector.tensor_scalar(ss[:, :], X[2][:, 0:TPG], 1.0 / INNER, LN_EPS, ALU.mult, ALU.add))
                    dve.sem_inc(s_v, 1)
                elif k == 5:
                    links.n = 2
                    dve.wait_ge(s_rg, g + 1)
                    links.link(dve, nc.vector.tensor_tensor(rt[:, :], rs[:, :], rs[:, :], ALU.mult))
                    links.link(dve, nc.vector.tensor_tensor(rt[:, :], rt[:, :], ss[:, :], ALU.mult))
                    links.link(dve, nc.vector.tensor_scalar(rt[:, :], rt[:, :], -0.5, 1.5, ALU.mult, ALU.add))
                    links.link(dve, nc.vector.scalar_tensor_tensor(out=rt[:, :], in0=rs[:, :], scalar=scale[:, 1:2],
                                                                   in1=rt[:, :], op0=ALU.mult, op1=ALU.mult))
                elif k in (6, 7):
                    a = k - 6
                    dve.wait_ge(s_n1, g + 1)
                    dve.wait_ge(s_out, g * 2 + a + 1)
                    for jj in range(2):
                        j = 2 * a + jj
                        ins = nc.vector.scalar_tensor_tensor(out=tile_view(c.h, g, j), in0=X[2 - a][:, jj * D:(jj + 1) * D],
                                                             scalar=rt[:, j:j + 1], in1=tile_view(c.h, g, j), op0=ALU.mult,
                                                             op1=ALU.add)
                    ins.then_inc(s_h, 1)

            all_groups(dve, state, head, tail, end=end)

        @block.scalar
        def _(act):
            nc.scalar.preload_act_table_set(LOG_EXP)
            norm_factors_act(nc, act, c, s_var, s_log, s_guess, twice=True)
            act.wait_ge(s_alog, 1)
            nc.scalar.activation(A[:, :], A[:, :], ACT.Exp).then_inc(s_A, 1)
            act.wait_ge(s_part, 2)

            def head(k, g, b):
                if k == 1:
                    for cc in range(2):
                        act.wait_ge(s_T, g * 2 + cc + 1)
                        nc.scalar.activation(xT[:, cc, :], X[cc][0:DC, :], ACT.Copy,
                                             scale=col(c, "rmsw")[0:DC, cc:cc + 1]).then_inc(s_xT, 1)
                elif 2 <= k < 2 + IC:
                    i = k - 2
                    act.wait_ge(s_inx, g * IC + i + 1)
                    nc.scalar.activation(xpad[:, i, :, TAPS - 1:], X[i % 2].rearrange("p (m t) -> p m t", t=SEQ), ACT.Copy,
                                         scale=scale[:, 0:1]).then_inc(s_pad, 1)
                elif k == 10:
                    act.wait_ge(s_inz, g * IC + IC)
                    for i in range(IC):
                        nc.scalar.activation(chunk(sz[b], i), X[i], ACT.Silu, scale=scale[:, 0:1]).then_inc(s_sz, 1)
                    act.wait_ge(s_conv, g * IC + IC)
                    nc.scalar.activation(xc[b], pre[:, :], ACT.Silu).then_inc(s_xc, 1)
                elif k == 15:
                    act.wait_ge(s_pre, g * IC + IC)
                    nc.scalar.activation(soft[:, :], pre[:, :], ACT.Abs).then_inc(s_abs, 1)
                    act.wait_ge(s_abs, g * 2 + 1)
                    nc.scalar.activation(soft[:, :], soft[:, :], ACT.Exp, scale=-1.0).then_inc(s_abs, 1)
                    act.wait_ge(s_abs, g * 2 + 2)
                    nc.scalar.activation(soft[:, :], soft[:, :], ACT.Ln, bias=1.0).then_inc(s_soft, 1)

            def state(s, g, b, pieces):
                q = g * STATES + s
                if s == 0:
                    act.wait_ge(s_u, g + 1)
                act.wait_ge(s_scan, q + 1)
                for i in range(IC):
                    nc.scalar.activation(dA[:, s % 2, i * GT:(i + 1) * GT], chunk(delta[b], i), ACT.Exp,
                                         scale=A[:, i * STATES + s:i * STATES + s + 1]).then_inc(s_dA, 1)
                if s % 2 == 0:
                    act.wait_ge(s_C, q + 1)
                    wait_used(act, g, s, False)
                    nc.scalar.activation(cs[:, 0, :], C[:, 0, :], ACT.Copy).then_inc(s_cs, 1)
                pieces()

            def tail(k, g, b):
                if k == 0:
                    act.wait_ge(s_yg, g + 1)
                    nc.scalar.activation(soft[:, :], yg[:, :], ACT.Square).then_inc(s_sq, 1)
                elif k == 5:
                    act.wait_ge(s_v, g + 1)
                    nc.scalar.activation(rs[:, :], ss[:, :], ACT.Ln).then_inc(s_r0, 1)
                    act.wait_ge(s_r0, g + 1)
                    nc.scalar.activation(rs[:, :], rs[:, :], ACT.Exp, scale=-0.5).then_inc(s_rg, 1)

            all_groups(act, state, head, tail)

        @block.tensor
        def _(pe):
            pe.wait_ge(s_part, 1)
            mm = nc.tensor.matmul(X[0][:, 0:2], c.ones[:, :], part[:, :], start=True, stop=True).then_inc(s_tot, 1)
            pe.wait_ge(s_part, 2)
            pe.sem_inc(s_hcu, 2)

            def project(i, bank):
                for cc in range(2):
                    mm = nc.tensor.matmul(bank, win[0:DC, cc, i * P:(i + 1) * P], xT[:, cc, :], start=(cc == 0), stop=(cc == 1))
                return mm

            def head(k, g, b):
                if k == 0:
                    pe.wait_ge(s_n, g * TPG + TPG)
                    if inner(g) or g > 0:
                        pe.wait_ge(s_pre, g * IC)
                    for cc in range(2):
                        for j in range(TPG):
                            mm = nc.tensor.transpose(X[cc][0:DC, j * P:(j + 1) * P], n[:, j, cc * DC:(cc + 1) * DC], c.ident[:, :])
                        mm.then_inc(s_T, 1)
                elif 1 <= k < 1 + IC:
                    i = k - 1
                    pe.wait_ge(s_xT, g * 2 + 2)
                    if i == 2:
                        pe.wait_ge(s_pad, g * IC + 1)
                    project(i, X[i % 2]).then_inc(s_inx, 1)
                elif k in (6, 7, 8):
                    i = {6: 0, 7: 2, 8: 1}[k]
                    pe.wait_ge(s_pad, g * IC + IC)
                    if i > 0 and (inner(g) or g > 1):
                        pe.wait_ge(s_h, g * 2 - 3 if i == 2 else g * 2 - 2)
                    project(IC + i, X[i]).then_inc(s_inz, 1)
                elif k == 11:
                    pe.wait_ge(s_xc, g + 1)
                    pe.wait_ge(s_sz, g * IC + 1)
                    for i in range(IC):
                        mm = nc.tensor.matmul(X[0][0:XP, :], wx[:, i, :], chunk(xc[b], i),
                                              start=(i == 0), stop=(i == IC - 1))
                    mm.then_inc(s_dbc, 1)
                elif k == 12:
                    pe.wait_ge(s_dbcs, g + 1)
                    for i in range(IC):
                        nc.tensor.matmul(X[i], c.rowp[0:1, ROWP_DT + i * P:ROWP_DT + (i + 1) * P], dt[:, :],
                                         start=True, stop=True).then_inc(s_dt, 1)

            def spread(bank, row, b):
                return nc.tensor.matmul(bank[:, 0, :], pick[:, row:row + 1].broadcast_to([3 * SC, P]), parts[:, b, :],
                                        start=True, stop=True)

            def start(g, b):
                pe.wait_ge(s_parts, g + 1)
                if inner(g) or g > 0:
                    pe.wait_ge(s_dBu, g * STATES)
                spread(B, 0, b).then_inc(s_B, 1)
                if inner(g) or g > 0:
                    pe.wait_ge(s_hc[1], g * HALF)
                spread(C, STATES, b).then_inc(s_C, 1)

            def state(s, g, b, pieces):
                q = g * STATES + s
                if s + 1 < STATES:
                    pe.wait_ge(s_dBu, q + 1)
                    spread(B, s + 1, b).then_inc(s_B, 1)
                if s > 0:
                    add(s - 1, g)
                if s % 2 == 0:
                    pe.wait_ge(s_cs, g * HALF + s // 2 + 1)
                else:
                    wait_used(pe, g, s, True)
                if s + 1 < STATES:
                    spread(C, STATES + s + 1, b).then_inc(s_C, 1)
                else:
                    add(s, g)
                pieces()

            def add(s, g):
                wait_used(pe, g, s, True)
                if s == 0 and (inner(g) or g > 0):
                    pe.wait_ge(s_yg, g)
                for i in range(IC):
                    mm = nc.tensor.matmul(Y[:, i, :], c.ident[:, :], hc[:, s % 2, i * GT:(i + 1) * GT], start=(s == 0),
                                          stop=(s == STATES - 1))
                mm.then_inc(s_hcu, 1)

            def tail(k, g, b):
                if k == 1:
                    pe.wait_ge(s_sq, g + 1)
                    pe.wait_ge(s_pre, (g + 2) * IC if inner(g) or g + 2 <= GROUPS else GROUPS * IC)
                    for j in range(TPG):
                        for i in range(IC):
                            at = i * GT + j * P
                            mm = nc.tensor.matmul(X[2][:, j:j + 1], soft[:, at:at + P], c.ones[:, 0:1], start=(i == 0),
                                                  stop=(i == IC - 1))
                    mm.then_inc(s_ss, 1)
                elif k in (4, 5):
                    a = k - 4
                    if a == 0:
                        pe.wait_ge(s_v, g + 1)
                    elif inner(g) or g + 2 < GROUPS:
                        pe.wait_ge(s_pad, (g + 2) * IC + 2)
                    for jj in range(2):
                        for i in range(IC):
                            at = i * GT + (2 * a + jj) * P
                            mm = nc.tensor.matmul(X[2 - a][:, jj * D:(jj + 1) * D], yg[:, at:at + P],
                                                  wo[:, i * D:(i + 1) * D], start=(i == 0), stop=(i == IC - 1))
                    mm.then_inc(s_out, 1)

            all_groups(pe, state, head, tail, start=start)



def feed_forward(nc, c, out):
    with Semaphores(nc) as pool, ExitStack() as ctx:
        def sb(name, shape, dt=F32):
            return ctx.enter_context(nc.sbuf_tensor("f_" + name, shape, dt))

        def sem(name):
            return pool.new("f_" + name)

        def ps(name, shape):
            return ctx.enter_context(nc.psum_tensor("f_" + name, shape, F32))

        n = sb("n", [P, TPG, D])
        xT = sb("xT", [DC, 2, 2, GT])
        hT = sb("hT", [P, FC, GT])
        y = sb("y", [P, 2, TPG, D])
        H, O = ps("H", [P, FC, 512]), ps("O", [P, 2, 512])
        w1, w2, b1 = weight(c, "f1"), col(c, "f2"), col(c, "f1b")
        s_dve, s_var, s_log, s_guess = [sem(x) for x in ("dve", "var", "log", "guess")]
        s_n, s_T, s_xT, s_up, s_gelu, s_o, s_y = [sem(x) for x in ("n", "T", "xT", "up", "gelu", "o", "y")]
        s_out = [sem("out0"), sem("out1")]
        block = ctx.enter_context(nc.Block())
        rows = out.rearrange("(t p) d -> p t d", p=P)

        def groups(eng, group):
            group(0, 0, False)
            group(1, 1, False)
            with eng.Fori(1, GROUPS // 2 - 1) as i:
                for b in range(2):
                    group(i * 2 + b, b, False)
            group(GROUPS - 2, 0, False)
            group(GROUPS - 1, 1, True)

        @block.sync
        def _(sp):
            for b in range(2):
                sp.sem_inc(s_out[b], 16)
            with sp.Fori(0, GROUPS // 2) as i:
                for b in range(2):
                    g = i * 2 + b
                    sp.wait_ge(s_y, g * TPG + TPG)
                    sp.dma_start(rows[:, bass.ds(g * TPG, TPG), :], y[:, b]).then_inc(s_out[b], 16)
            for b in range(2):
                sp.wait_ge(s_out[b], GROUPS // 2 * 16 + 16)

        @block.vector
        def _(dve):
            own = Count(s_dve)
            token_stats(nc, dve, c, own.link, c.x1)
            norm_factors_dve(nc, dve, c, own.link, s_var, s_guess, twice=False)

            def normalise(g):
                for j in range(TPG):
                    nc.vector.tensor_scalar(n[:, j, :], tile_view(c.x1, g, j), factor(c, 0, g, j), factor(c, 1, g, j),
                                            ALU.mult, ALU.add).then_inc(s_n, 1)

            def turned(g, b):
                for cc in range(2):
                    dve.wait_ge(s_T, g * 2 + cc + 1)
                    nc.vector.tensor_scalar(xT[:, b, cc, :], H[0:DC, cc, :], col(c, "g2")[0:DC, cc:cc + 1],
                                            col(c, "b2")[0:DC, cc:cc + 1], ALU.mult, ALU.add).then_inc(s_xT, 1)

            def group(g, b, last):
                if not last:
                    normalise(g + 1)
                    turned(g + 1, 1 - b)
                dve.wait_ge(s_out[b], (g - b) * 8 + 16)
                for j in range(TPG):
                    if j % 2 == 0:
                        dve.wait_ge(s_o, g * 2 + j // 2 + 1)
                    nc.vector.tensor_tensor(y[:, b, j, :], O[:, j // 2, (j % 2) * D:(j % 2 + 1) * D], tile_view(c.h, g, j),
                                            ALU.add).then_inc(s_y, 1)

            normalise(0)
            turned(0, 0)
            groups(dve, group)

        @block.scalar
        def _(act):
            nc.scalar.preload_act_table_set(LOG_EXP)
            norm_factors_act(nc, act, c, s_var, s_log, s_guess, twice=False)
            nc.scalar.preload_act_table(ACT.Gelu)
            with act.Fori(0, GROUPS) as g:
                for f in range(FC):
                    act.wait_ge(s_up, g * FC + f + 1)
                    nc.scalar.activation(hT[:, f, :], H[:, f, :], ACT.Gelu, bias=b1[:, f:f + 1]).then_inc(s_gelu, 1)

        @block.tensor
        def _(pe):
            def turn(g):
                pe.wait_ge(s_n, g * TPG + TPG)
                for cc in range(2):
                    for j in range(TPG):
                        mm = nc.tensor.transpose(H[0:DC, cc, j * P:(j + 1) * P], n[:, j, cc * DC:(cc + 1) * DC], c.ident[:, :])
                    mm.then_inc(s_T, 1)

            def group(g, b, last):
                pe.wait_ge(s_xT, g * 2 + 2)

                def down(f):
                    pe.wait_ge(s_gelu, g * FC + f + 1)
                    if f == 0 and not (isinstance(g, int) and g == 0):
                        pe.wait_ge(s_y, g * TPG)
                    for j in range(TPG):
                        o = O[:, j // 2, (j % 2) * D:(j % 2 + 1) * D]
                        if f == 0:
                            nc.tensor.matmul(o, c.ones[0:1, :], c.rowp[0:1, ROWP_BF2:ROWP_BF2 + D], start=(j % 2 == 0),
                                             stop=False, skip_group_check=True)
                        mm = nc.tensor.matmul(o, hT[:, f, j * P:(j + 1) * P], w2[:, f * D:(f + 1) * D], start=False,
                                              stop=(f == FC - 1), skip_group_check=True)
                        if f == FC - 1 and j % 2:
                            mm.then_inc(s_o, 1)

                for f in range(FC):
                    for cc in range(2):
                        mm = nc.tensor.matmul(H[:, f, :], w1[0:DC, cc, f * P:(f + 1) * P], xT[:, b, cc, :], start=(cc == 0),
                                              stop=(cc == 1))
                    mm.then_inc(s_up, 1)
                    if f == FC - 1 and not last:
                        turn(g + 1)
                    if f >= 1:
                        down(f - 1)
                down(FC - 1)

            turn(0)
            groups(pe, group)



STOP = 99


def program(nc, patches, w_tok, w97, rows, cols, proj, e1, e2, eb2, extra, out):
    with ExitStack() as ctx:
        c = make_core(nc, ctx)
        scratch = nc.dram_tensor("attention", (IMAGES, HEADS, SEQ, DH), F32, kind="Internal").ap()
        xs, ys = (nc.dram_tensor(x, (SLOTS * SLOT, D), F32, kind="Internal").ap() for x in ("expert_rows", "expert_results"))
        qk_rows = nc.dram_tensor("query_key_rows", (DC, 4, TOKENS), F32, kind="Internal").ap()
        v_rows = nc.dram_tensor("value_rows", (P, TILES, HEADS * (DH + 1)), F32, kind="Internal").ap()
        tokenize(nc, c, patches, w_tok, w97, rows, cols, extra)
        if STOP > 0:
            performer(nc, c, proj, scratch)
            performer_out(nc, c, scratch)
        if STOP > 1:
            attention(nc, c, ("aq", "ak", "av", "ao"), "ln1g", "ln1b", mixing=False, qk_rows=qk_rows, v_rows=v_rows)
            experts(nc, c, e1, e2, eb2, xs, ys)
        if STOP > 2:
            scan_block(nc, c)
        if STOP > 3:
            attention(nc, c, ("mq", "mk", "mv", "mo"), "g1", "b1", mixing=True, qk_rows=qk_rows, v_rows=v_rows)
            feed_forward(nc, c, out)
            return
        with ExitStack() as c2:
            s_o = c2.enter_context(nc.semaphore("s_o"))
            block = c2.enter_context(nc.Block())

            @block.sync
            def _(sp):
                sp.dma_start(out.rearrange("(t p) d -> p t d", p=P), c.h[:, :, :]).then_inc(s_o, 16)
                sp.wait_ge(s_o, 16)


def two_chunks(w, bias, np):
    out = np.zeros((DC + 1, 2, w.shape[1]), w.dtype)
    out[0:DC, 0], out[0:DC, 1] = w[0:DC], w[DC:D]
    if bias is not None:
        out[DC, 0] = bias
    return out


def by_block(w):
    return w.reshape(w.shape[:-1] + (3, 2, 2 * DH)).swapaxes(-3, -2).reshape(w.shape)


def kernel(**inputs):
    import numpy as np
    import concourse.bacc as _bacc
    from concourse.bass_utils import run_bass_kernel_spmd as _run

    a = {k: np.asarray(v) for k, v in inputs.items()}
    patches = a["x"].reshape(GROUPS, IMAGES // GROUPS, 3, 8, 16, 8, 16).transpose(0, 2, 4, 6, 1, 3, 5)
    patches = patches.reshape(GROUPS, PKC, P, GT).transpose(0, 2, 1, 3).reshape(GROUPS, P, PKC * GT)
    w_tok = a["L0_tok_W"].reshape(D, PKC, P).transpose(2, 1, 0).reshape(P, PKC * D)
    qkv, qkvb = a["L0_ffn_in_proj_w"].T, a["L0_ffn_in_proj_b"]
    w97 = {
        "pq": (by_block(a["L0_attn_Wq"]), by_block(a["L0_attn_bq"])),
        "pk": (by_block(a["L0_attn_Wk"]), by_block(a["L0_attn_bk"])),
        "pv": (a["L0_attn_Wv"], a["L0_attn_bv"]), "po": (a["L0_attn_Wo"], a["L0_attn_bo"]),
        "aq": (by_block(qkv[:, 0:D]), by_block(qkvb[0:D])), "ak": (by_block(qkv[:, D:2 * D]), by_block(qkvb[D:2 * D])),
        "av": (qkv[:, 2 * D:], qkvb[2 * D:]), "ao": (a["L0_ffn_out_proj_w"].T, a["L0_ffn_out_proj_b"]),
        "router": (a["L0_ffn_router_w"].T, a["L0_ffn_router_b"]),
        "mq": (by_block(a["L1_ffn_Wq"]), by_block(a["L1_ffn_bq"])),
        "mk": (by_block(a["L1_ffn_Wk"]), by_block(a["L1_ffn_bk"])),
        "mv": (np.concatenate([a["L1_ffn_Wv"], a["L1_ffn_Wr"][:, None]], 1),
               np.concatenate([a["L1_ffn_bv"], a["L1_ffn_br"].reshape(1)])),
        "mo": (a["L1_ffn_Wo"], a["L1_ffn_bo"]), "mm": (a["L1_ffn_Wm"], a["L1_ffn_bm"]),
        "f1": (a["L1_ffn_W1"], None), "inproj": (a["L1_attn_in_proj_weight"].T, None),
    }
    w97 = np.concatenate([two_chunks(*w97[n], np) for n, _ in W97], axis=2)
    rows = np.concatenate([a["L0_tok_b"], a["L0_tok_alpha_w"].reshape(1), a["L0_tok_alpha_a"].reshape(1)])[None, :]

    def chan(x):
        return x.reshape(IC, P, -1).transpose(1, 0, 2).reshape(P, -1)

    def half(x):
        out = np.zeros((P, 2), x.dtype)
        out[0:DC] = x.reshape(2, DC).T
        return out

    cols = {
        "f2": a["L1_ffn_W2"].reshape(FC, P, D).transpose(1, 0, 2).reshape(P, FC * D),
        "outproj": chan(a["L1_attn_out_proj_weight"].T), "xproj": chan(a["L1_attn_x_proj_weight"].T),
        "f1b": a["L1_ffn_bf1"].reshape(FC, P).T, "conv": chan(a["L1_attn_conv_weight"].reshape(INNER, TAPS)),
        "convb": chan(a["L1_attn_conv_bias"]), "dtb": chan(a["L1_attn_dt_proj_bias"]),
        "alog": chan(a["L1_attn_A_log"]), "dskip": chan(a["L1_attn_D"]), "onorm": chan(a["L1_attn_out_norm_weight"]),
        "ln1g": half(a["L0_ffn_ln1_g"]), "ln1b": half(a["L0_ffn_ln1_b"]), "ln2g": half(a["L0_ffn_ln2_g"]),
        "ln2b": half(a["L0_ffn_ln2_b"]), "rmsw": half(a["L1_attn_norm_weight"]), "g1": half(a["L1_ffn_g1"]),
        "b1": half(a["L1_ffn_b1"]), "g2": half(a["L1_ffn_g2"]), "b2": half(a["L1_ffn_b2"]),
    }
    headsum = np.zeros((P, 3, 2), np.float32)
    for b in range(3):
        for r in range(2):
            headsum[32 * b + DH * r:32 * b + DH * (r + 1), b, r] = 0.5 / np.sqrt(DH)
    cols["headsum"] = headsum.reshape(P, 6)
    cols["half"] = np.tile(np.repeat(np.eye(2, dtype=np.float32), DH, axis=0), (4, 1))
    cols["tri"] = np.tile(np.tril(np.ones((EXPERTS, EXPERTS), np.float32), -1).reshape(1, -1), (P, 1))
    cols["starts"] = np.tile(np.arange(TOKENS // SLOT, dtype=np.float32) * SLOT, (P, 1))
    cols["slots"] = np.tile(np.arange(SLOTS, dtype=np.float32), (P, 1))
    cols = np.concatenate([cols[n] for n, _ in COLS], axis=1)
    proj = np.zeros((3, 2, DH, 3, 2, FEATURES), np.float32)
    for b in range(3):
        for r in range(2):
            proj[b, r, :, b, r, :] = a["L0_attn_proj"].T
    proj = proj.reshape(DC, 3, 2 * FEATURES)
    e1 = a["L0_ffn_w1"].reshape(EXPERTS, 2, DC, FF).transpose(0, 2, 1, 3)
    e2 = a["L0_ffn_w2"].reshape(EXPERTS, FC, P, D).transpose(0, 2, 1, 3).reshape(EXPERTS, P, FC * D)
    e2 = np.concatenate([e2, a["L0_ffn_b1"].reshape(EXPERTS, FC, P).transpose(0, 2, 1)], axis=2)
    extra = np.concatenate([a["L1_attn_dt_proj_weight"].reshape(-1), a["L1_ffn_bf2"], a["L1_ffn_bm"]])[None, :]
    arrays = dict(patches=patches, w_tok=w_tok, w97=w97, rows=rows, cols=cols, proj=proj, e1=e1, e2=e2,
                  eb2=a["L0_ffn_b2"], extra=extra)
    arrays = {k: np.ascontiguousarray(v) for k, v in arrays.items()}
    nc = _bacc.Bacc("TRN2", target_bir_lowering=False, num_devices=1)
    args = [nc.dram_tensor(f"in_{k}", v.shape, F32, kind="ExternalInput").ap() for k, v in arrays.items()]
    out = nc.dram_tensor("out", (TOKENS, D), F32, kind="ExternalOutput").ap()
    program(nc, *args, out)
    r = _run(nc, [{f"in_{k}": v for k, v in arrays.items()}], core_ids=[0])
    return r.results[0]["out"].reshape(IMAGES, SEQ, D)
```
